# Optimizing a Trainium2 kernel written in Bass

```python
import numpy as np
import jax
import jax.numpy as jnp

def _softmax(x, axis=-1):
    return jax.nn.softmax(x, axis=axis)

def _gelu(x):
    return jax.nn.gelu(x, approximate=True)

def _silu(x):
    return jax.nn.silu(x)

def _sigmoid(x):
    return jax.nn.sigmoid(x)

def _layernorm(x, axis=-1, eps=1e-05):
    m = jnp.mean(x, axis=axis, keepdims=True)
    v = jnp.var(x, axis=axis, keepdims=True)
    return (x - m) / jnp.sqrt(v + eps)

def _scatter_add(tgt, idx, src, axis=0):
    return tgt.at[idx].add(src)

def _segment_sum(src, seg, n):
    return jax.ops.segment_sum(src, seg, n)
kernel_name = 'mk_decoder_preln_d2_seqx_r4_838b66'

def setup_inputs(seed: int=0):
    np.random.seed(seed)
    _w = jnp.asarray

    def _rec_inputs():
        import jax
        import jax.numpy as jnp
        _rk = jax.random.key(seed)
        x = -0.0002928 + 1 * jax.random.normal(jax.random.fold_in(_rk, 1), (16, 256, 256), jnp.float32)
        _lenS = 256 - jax.random.randint(jax.random.fold_in(_rk, 7), (16,), 0, max(1, 256 // 4) + 1, jnp.int32)
        _lenS2 = 120 - jax.random.randint(jax.random.fold_in(_rk, 8), (16,), 0, max(1, 120 // 4) + 1, jnp.int32)
        _ctx_768P = jax.random.normal(jax.random.fold_in(_rk, 11), (16, 16, 192), jnp.float32)
        _ctx_768c = jax.random.dirichlet(jax.random.fold_in(_rk, 511), 0.3 * jnp.ones((16,), jnp.float32), (16, 120))
        _ctx_768t = jnp.einsum('bsk,bkd->bsd', _ctx_768c, _ctx_768P)
        _ctx_768t = _ctx_768t * jax.lax.rsqrt(jnp.mean(jnp.square(_ctx_768t)) + 1e-12) * 0.953939
        ctx_768 = 2.09791e-05 + 1.00001 * (_ctx_768t + 0.3 * jax.random.normal(jax.random.fold_in(_rk, 611), (16, 120, 192), jnp.float32))
        return (x, ctx_768)
    x, ctx_768 = _rec_inputs()

    def _L0_attn_setup():
        import jax, jax.numpy as jnp
        import numpy as np
        DIM = 256
        HEADS = 16
        HEAD_DIM = DIM // HEADS

        def _layernorm(x, gamma, beta, eps=1e-05):
            mu = jnp.mean(x, axis=-1, keepdims=True)
            var = jnp.mean(jnp.square(x - mu), axis=-1, keepdims=True)
            return (x - mu) * jax.lax.rsqrt(var + eps) * gamma + beta
        key = jax.random.key(seed)
        k_x, k_in, k_out, k_g, k_b = jax.random.split(key, 5)
        x = jax.random.normal(k_x, (4, 512, DIM), dtype=jnp.float32)
        in_proj_w = jax.random.normal(k_in, (3 * DIM, DIM), dtype=jnp.float32) * (1.0 / np.sqrt(DIM))
        out_proj_w = jax.random.normal(k_out, (DIM, DIM), dtype=jnp.float32) * (1.0 / np.sqrt(DIM))
        ln_gamma = jnp.ones((DIM,), dtype=jnp.float32)
        ln_beta = jnp.zeros((DIM,), dtype=jnp.float32)
        return {'x': x, 'in_proj_w': in_proj_w, 'out_proj_w': out_proj_w, 'ln_gamma': ln_gamma, 'ln_beta': ln_beta}
    _L0_attn_all = _L0_attn_setup()
    _L0_attn_in = {k: v for k, v in _L0_attn_all.items() if k in ('in_proj_w', 'out_proj_w', 'ln_gamma', 'ln_beta')}
    del _L0_attn_all

    def _L0_xattn_setup():
        import jax, jax.numpy as jnp
        import numpy as np
        N_HEADS = 16
        EMBED_DIM = 256
        CROSS_DIM = 192
        HEAD_DIM = EMBED_DIM // N_HEADS
        key = jax.random.key(seed)
        ks = jax.random.split(key, 12)
        B, SQ, SKV = (2, 512, 512)
        s_in = 1.0 / np.sqrt(EMBED_DIM)
        s_cross = 1.0 / np.sqrt(CROSS_DIM)
        return {'x': jax.random.normal(ks[0], (B, SQ, EMBED_DIM), jnp.float32), 'y': jax.random.normal(ks[1], (B, SKV, CROSS_DIM), jnp.float32), 'wq': jax.random.normal(ks[2], (EMBED_DIM, EMBED_DIM), jnp.float32) * s_in, 'bq': jax.random.normal(ks[3], (EMBED_DIM,), jnp.float32) * s_in, 'wk': jax.random.normal(ks[4], (EMBED_DIM, CROSS_DIM), jnp.float32) * s_cross, 'bk': jax.random.normal(ks[5], (EMBED_DIM,), jnp.float32) * s_cross, 'wv': jax.random.normal(ks[6], (EMBED_DIM, CROSS_DIM), jnp.float32) * s_cross, 'bv': jax.random.normal(ks[7], (EMBED_DIM,), jnp.float32) * s_cross, 'wo': jax.random.normal(ks[8], (EMBED_DIM, EMBED_DIM), jnp.float32) * s_in, 'bo': jax.random.normal(ks[9], (EMBED_DIM,), jnp.float32) * s_in}
    _L0_xattn_all = _L0_xattn_setup()
    _L0_xattn_in = {k: v for k, v in _L0_xattn_all.items() if k in ('wq', 'bq', 'wk', 'bk', 'wv', 'bv', 'wo', 'bo')}
    del _L0_xattn_all

    def _L0_ffn_setup():
        import jax, jax.numpy as jnp
        import numpy as np
        INT4_QMAX = 7.0

        def simulate_quantize_int4(w):
            scale = jnp.max(jnp.abs(w)) / INT4_QMAX
            q = jnp.clip(jnp.round(w / scale), -8.0, 7.0)
            return q * scale
        key = jax.random.key(seed)
        k_x, k_w, k_bias, k_a, k_b = jax.random.split(key, 5)
        d_in, features, rank = (256, 256, 16)
        x = jax.random.normal(k_x, (4, 2048, d_in), dtype=jnp.float32)
        kernel = jax.random.normal(k_w, (d_in, features), dtype=jnp.float32)
        bias = jax.random.normal(k_bias, (features,), dtype=jnp.float32)
        a = jax.random.normal(k_a, (d_in, rank), dtype=jnp.float32) * (1.0 / np.sqrt(d_in))
        b = jax.random.normal(k_b, (rank, features), dtype=jnp.float32) * 0.01
        return {'x': x, 'kernel': kernel, 'bias': bias, 'a': a, 'b': b}
    _L0_ffn_all = _L0_ffn_setup()
    _L0_ffn_in = {k: v for k, v in _L0_ffn_all.items() if k in ('kernel', 'bias', 'a', 'b')}
    del _L0_ffn_all

    def _L1_attn_setup():
        import jax, jax.numpy as jnp
        import numpy as np
        D = 256
        H = 16
        HD = D // H
        ROPE_BASE = 10000.0
        EPS_RMS = 1e-08
        EPS_RENORM = 1e-08

        def rms_norm(x, scale):
            norm = jnp.mean(x * x, axis=-1, keepdims=True)
            return scale * (x * jax.lax.rsqrt(norm + EPS_RMS))

        def rope_tables(seq_len):
            inv_freq = 1.0 / ROPE_BASE ** (jnp.arange(0, HD, 2, dtype=jnp.float32) / HD)
            t = jnp.arange(seq_len, dtype=jnp.float32)
            freqs = t[:, None] * inv_freq[None, :]
            emb = jnp.concatenate([freqs, freqs], axis=-1)
            return (jnp.cos(emb), jnp.sin(emb))

        def apply_rotary(x, cos, sin):
            x1 = x[..., ::2]
            x2 = x[..., 1::2]
            x_rot = jnp.stack([-x2, x1], axis=-1).reshape(x.shape)
            return x * cos + x_rot * sin
        key = jax.random.key(seed)
        ks = jax.random.split(key, 11)
        B, L = (2, 512)
        s = 1.0 / np.sqrt(D)
        inp = {'x': jax.random.normal(ks[0], (B, L, D), dtype=jnp.float32), 'q_w': jax.random.uniform(ks[1], (D, D), jnp.float32, -s, s), 'q_b': jax.random.uniform(ks[2], (D,), jnp.float32, -s, s), 'k_w': jax.random.uniform(ks[3], (D, D), jnp.float32, -s, s), 'k_b': jax.random.uniform(ks[4], (D,), jnp.float32, -s, s), 'v_w': jax.random.uniform(ks[5], (D, D), jnp.float32, -s, s), 'v_b': jax.random.uniform(ks[6], (D,), jnp.float32, -s, s), 'o_w': jax.random.uniform(ks[7], (D, D), jnp.float32, -s, s), 'o_b': jax.random.uniform(ks[8], (D,), jnp.float32, -s, s), 'qn_scale': jnp.ones((D,), dtype=jnp.float32), 'kn_scale': jnp.ones((D,), dtype=jnp.float32)}
        return inp
    _L1_attn_all = _L1_attn_setup()
    _L1_attn_in = {k: v for k, v in _L1_attn_all.items() if k in ('q_w', 'q_b', 'k_w', 'k_b', 'v_w', 'v_b', 'o_w', 'o_b', 'qn_scale', 'kn_scale')}
    del _L1_attn_all

    def _L1_xattn_setup():
        import jax, jax.numpy as jnp
        import numpy as np
        IMG_DIM, TXT_DIM, HID = (256, 192, 256)
        B, LQ, LK = (8, 512, 512)
        key = jax.random.key(seed)
        ks = jax.random.split(key, 8)
        s_img = 1.0 / np.sqrt(IMG_DIM)
        s_txt = 1.0 / np.sqrt(TXT_DIM)
        return {'image_features': jax.random.normal(ks[0], (B, LQ, IMG_DIM), jnp.float32), 'text_features': jax.random.normal(ks[1], (B, LK, TXT_DIM), jnp.float32), 'Wq': jax.random.uniform(ks[2], (IMG_DIM, HID), jnp.float32, -s_img, s_img), 'bq': jax.random.uniform(ks[3], (HID,), jnp.float32, -s_img, s_img), 'Wk': jax.random.uniform(ks[4], (TXT_DIM, HID), jnp.float32, -s_txt, s_txt), 'bk': jax.random.uniform(ks[5], (HID,), jnp.float32, -s_txt, s_txt), 'Wv': jax.random.uniform(ks[6], (TXT_DIM, HID), jnp.float32, -s_txt, s_txt), 'bv': jax.random.uniform(ks[7], (HID,), jnp.float32, -s_txt, s_txt)}
    _L1_xattn_all = _L1_xattn_setup()
    _L1_xattn_in = {k: v for k, v in _L1_xattn_all.items() if k in ('Wq', 'bq', 'Wk', 'bk', 'Wv', 'bv')}
    del _L1_xattn_all

    def _L1_ffn_setup():
        import jax, jax.numpy as jnp
        import numpy as np
        CHUNK = 128
        NUM_BITS = 6
        key = jax.random.key(seed)
        k1, k2, k3 = jax.random.split(key, 3)
        B, L, D, E = (4, 1024, 256, 64)
        x = jax.random.normal(k1, (B, L, D), dtype=jnp.float32)
        expert_weights = jax.random.normal(k2, (E, D, D), dtype=jnp.float32) * 0.02
        hyperplanes = jax.random.normal(k3, (D, NUM_BITS), dtype=jnp.float32)
        return {'x': x, 'expert_weights': expert_weights, 'hyperplanes': hyperplanes}
    _L1_ffn_all = _L1_ffn_setup()
    _L1_ffn_in = {k: v for k, v in _L1_ffn_all.items() if k in ('expert_weights', 'hyperplanes')}
    del _L1_ffn_all
    return {'x': x, 'ctx_768': ctx_768, 'L0_attn_in_proj_w': _L0_attn_in['in_proj_w'], 'L0_attn_out_proj_w': _L0_attn_in['out_proj_w'], 'L0_attn_ln_gamma': _L0_attn_in['ln_gamma'], 'L0_attn_ln_beta': _L0_attn_in['ln_beta'], 'L0_xattn_wq': _L0_xattn_in['wq'], 'L0_xattn_bq': _L0_xattn_in['bq'], 'L0_xattn_wk': _L0_xattn_in['wk'], 'L0_xattn_bk': _L0_xattn_in['bk'], 'L0_xattn_wv': _L0_xattn_in['wv'], 'L0_xattn_bv': _L0_xattn_in['bv'], 'L0_xattn_wo': _L0_xattn_in['wo'], 'L0_xattn_bo': _L0_xattn_in['bo'], 'L0_ffn_kernel': _L0_ffn_in['kernel'], 'L0_ffn_bias': _L0_ffn_in['bias'], 'L0_ffn_a': _L0_ffn_in['a'], 'L0_ffn_b': _L0_ffn_in['b'], 'L1_attn_q_w': _L1_attn_in['q_w'], 'L1_attn_q_b': _L1_attn_in['q_b'], 'L1_attn_k_w': _L1_attn_in['k_w'], 'L1_attn_k_b': _L1_attn_in['k_b'], 'L1_attn_v_w': _L1_attn_in['v_w'], 'L1_attn_v_b': _L1_attn_in['v_b'], 'L1_attn_o_w': _L1_attn_in['o_w'], 'L1_attn_o_b': _L1_attn_in['o_b'], 'L1_attn_qn_scale': _L1_attn_in['qn_scale'], 'L1_attn_kn_scale': _L1_attn_in['kn_scale'], 'L1_xattn_Wq': _L1_xattn_in['Wq'], 'L1_xattn_bq': _L1_xattn_in['bq'], 'L1_xattn_Wk': _L1_xattn_in['Wk'], 'L1_xattn_bk': _L1_xattn_in['bk'], 'L1_xattn_Wv': _L1_xattn_in['Wv'], 'L1_xattn_bv': _L1_xattn_in['bv'], 'L1_ffn_expert_weights': _L1_ffn_in['expert_weights'], 'L1_ffn_hyperplanes': _L1_ffn_in['hyperplanes']}

def reference(x, ctx_768, L0_attn_in_proj_w, L0_attn_out_proj_w, L0_attn_ln_gamma, L0_attn_ln_beta, L0_xattn_wq, L0_xattn_bq, L0_xattn_wk, L0_xattn_bk, L0_xattn_wv, L0_xattn_bv, L0_xattn_wo, L0_xattn_bo, L0_ffn_kernel, L0_ffn_bias, L0_ffn_a, L0_ffn_b, L1_attn_q_w, L1_attn_q_b, L1_attn_k_w, L1_attn_k_b, L1_attn_v_w, L1_attn_v_b, L1_attn_o_w, L1_attn_o_b, L1_attn_qn_scale, L1_attn_kn_scale, L1_xattn_Wq, L1_xattn_bq, L1_xattn_Wk, L1_xattn_bk, L1_xattn_Wv, L1_xattn_bv, L1_ffn_expert_weights, L1_ffn_hyperplanes):
    import jax
    import jax.numpy as jnp

    def _L0_attn_ref(x, in_proj_w, out_proj_w, ln_gamma, ln_beta):
        import jax, jax.numpy as jnp
        import numpy as np
        DIM = 256
        HEADS = 16
        HEAD_DIM = DIM // HEADS

        def _layernorm(x, gamma, beta, eps=1e-05):
            mu = jnp.mean(x, axis=-1, keepdims=True)
            var = jnp.mean(jnp.square(x - mu), axis=-1, keepdims=True)
            return (x - mu) * jax.lax.rsqrt(var + eps) * gamma + beta
        B, S, D = x.shape
        h = _layernorm(x, ln_gamma, ln_beta)
        qkv = jnp.einsum('bsd,ed->bse', h, in_proj_w)
        q, k, v = jnp.split(qkv, 3, axis=-1)

        def heads(t):
            return t.reshape(B, S, HEADS, HEAD_DIM).transpose(0, 2, 1, 3)
        q, k, v = (heads(q), heads(k), heads(v))
        scale = 1.0 / np.sqrt(HEAD_DIM)
        scores = jnp.einsum('bhqd,bhkd->bhqk', q, k) * scale
        attn = jax.nn.softmax(scores, axis=-1)
        o = jnp.einsum('bhqk,bhkd->bhqd', attn, v)
        o = o.transpose(0, 2, 1, 3).reshape(B, S, D)
        return jnp.einsum('bsd,ed->bse', o, out_proj_w)

    def _L0_xattn_ref(x, y, wq, bq, wk, bk, wv, bv, wo, bo):
        import jax, jax.numpy as jnp
        import numpy as np
        N_HEADS = 16
        EMBED_DIM = 256
        CROSS_DIM = 192
        HEAD_DIM = EMBED_DIM // N_HEADS
        B, SQ, E = x.shape
        q = x @ wq.T + bq
        k = y @ wk.T + bk
        v = y @ wv.T + bv
        q = q.reshape(B, SQ, N_HEADS, HEAD_DIM).transpose(0, 2, 1, 3)
        k = k.reshape(B, -1, N_HEADS, HEAD_DIM).transpose(0, 2, 1, 3)
        v = v.reshape(B, -1, N_HEADS, HEAD_DIM).transpose(0, 2, 1, 3)
        scale = 1.0 / jnp.sqrt(jnp.asarray(HEAD_DIM, x.dtype))
        score = jnp.einsum('bhqd,bhkd->bhqk', q, k) * scale
        attn = jax.nn.softmax(score, axis=-1)
        out = jnp.einsum('bhqk,bhkd->bhqd', attn, v)
        out = out.transpose(0, 2, 1, 3).reshape(B, SQ, E)
        return out @ wo.T + bo

    def _L0_ffn_ref(x, kernel, bias, a, b):
        import jax, jax.numpy as jnp
        import numpy as np
        INT4_QMAX = 7.0

        def simulate_quantize_int4(w):
            scale = jnp.max(jnp.abs(w)) / INT4_QMAX
            q = jnp.clip(jnp.round(w / scale), -8.0, 7.0)
            return q * scale
        w = simulate_quantize_int4(kernel)
        y = jnp.einsum('bsd,df->bsf', x, w) + bias
        lora = jnp.einsum('bsr,rf->bsf', jnp.einsum('bsd,dr->bsr', x, a), b)
        return y + lora

    def _L1_attn_ref(x, q_w, q_b, k_w, k_b, v_w, v_b, o_w, o_b, qn_scale, kn_scale):
        import jax, jax.numpy as jnp
        import numpy as np
        D = 256
        H = 16
        HD = D // H
        ROPE_BASE = 10000.0
        EPS_RMS = 1e-08
        EPS_RENORM = 1e-08

        def rms_norm(x, scale):
            norm = jnp.mean(x * x, axis=-1, keepdims=True)
            return scale * (x * jax.lax.rsqrt(norm + EPS_RMS))

        def rope_tables(seq_len):
            inv_freq = 1.0 / ROPE_BASE ** (jnp.arange(0, HD, 2, dtype=jnp.float32) / HD)
            t = jnp.arange(seq_len, dtype=jnp.float32)
            freqs = t[:, None] * inv_freq[None, :]
            emb = jnp.concatenate([freqs, freqs], axis=-1)
            return (jnp.cos(emb), jnp.sin(emb))

        def apply_rotary(x, cos, sin):
            x1 = x[..., ::2]
            x2 = x[..., 1::2]
            x_rot = jnp.stack([-x2, x1], axis=-1).reshape(x.shape)
            return x * cos + x_rot * sin
        B, L, _ = x.shape
        q = rms_norm(x, qn_scale) @ q_w.T + q_b
        k = rms_norm(x, kn_scale) @ k_w.T + k_b
        v = x @ v_w.T + v_b
        q = q.reshape(B, L, H, HD).transpose(0, 2, 1, 3)
        k = k.reshape(B, L, H, HD).transpose(0, 2, 1, 3)
        v = v.reshape(B, L, H, HD).transpose(0, 2, 1, 3)
        cos, sin = rope_tables(L)
        q = apply_rotary(q, cos, sin)
        k = apply_rotary(k, cos, sin)
        scale = 1.0 / np.sqrt(HD)
        scores = jnp.einsum('bhqd,bhkd->bhqk', q, k) * scale
        weights = jax.nn.sigmoid(scores)
        weights = weights / (jnp.sum(weights, axis=-1, keepdims=True) + EPS_RENORM)
        attn = jnp.einsum('bhqk,bhkd->bhqd', weights, v)
        attn = attn.transpose(0, 2, 1, 3).reshape(B, L, D)
        return attn @ o_w.T + o_b

    def _L1_xattn_ref(image_features, text_features, Wq, bq, Wk, bk, Wv, bv):
        import jax, jax.numpy as jnp
        import numpy as np
        IMG_DIM, TXT_DIM, HID = (256, 192, 256)
        B, LQ, LK = (8, 512, 512)
        query = jnp.einsum('bqi,ih->bqh', image_features, Wq) + bq
        key = jnp.einsum('bkt,th->bkh', text_features, Wk) + bk
        value = jnp.einsum('bkt,th->bkh', text_features, Wv) + bv
        scale = 1.0 / jnp.sqrt(jnp.asarray(HID, query.dtype))
        scores = jnp.einsum('bqh,bkh->bqk', query, key) * scale
        weights = jax.nn.softmax(scores, axis=-1)
        attended = jnp.einsum('bqk,bkh->bqh', weights, value)
        return attended

    def _L1_ffn_ref(x, expert_weights, hyperplanes):
        import jax, jax.numpy as jnp
        import numpy as np
        CHUNK = 128
        NUM_BITS = 6
        B, L, D = x.shape
        C = L // CHUNK
        xr = x.reshape(B, C, CHUNK, D)
        chunk_emb = xr.mean(axis=2)
        proj = chunk_emb @ hyperplanes
        bits = (proj > 0).astype(jnp.int32)
        powers = (2 ** jnp.arange(NUM_BITS)).astype(jnp.int32)
        e1 = jnp.sum(bits * powers, axis=-1)
        weakest = jnp.argmin(jnp.abs(proj), axis=-1)
        flip = (2 ** weakest).astype(jnp.int32)
        e2 = jnp.bitwise_xor(e1, flip)
        out = jnp.zeros_like(xr)
        for idx in (e1, e2):
            w = expert_weights[idx]
            out = out + jnp.einsum('bcld,bcde->bcle', xr, w)
        out = out * 0.5
        return out.reshape(B, L, D)
    x = x + _L0_attn_ref(_layernorm(x, axis=-1), L0_attn_in_proj_w, L0_attn_out_proj_w, L0_attn_ln_gamma, L0_attn_ln_beta)
    x = x + _L0_xattn_ref(_layernorm(x, axis=-1), ctx_768, L0_xattn_wq, L0_xattn_bq, L0_xattn_wk, L0_xattn_bk, L0_xattn_wv, L0_xattn_bv, L0_xattn_wo, L0_xattn_bo)
    x = x + _L0_ffn_ref(_layernorm(x, axis=-1), L0_ffn_kernel, L0_ffn_bias, L0_ffn_a, L0_ffn_b)
    x = x + _L1_attn_ref(_layernorm(x, axis=-1), L1_attn_q_w, L1_attn_q_b, L1_attn_k_w, L1_attn_k_b, L1_attn_v_w, L1_attn_v_b, L1_attn_o_w, L1_attn_o_b, L1_attn_qn_scale, L1_attn_kn_scale)
    x = x + _L1_xattn_ref(_layernorm(x, axis=-1), ctx_768, L1_xattn_Wq, L1_xattn_bq, L1_xattn_Wk, L1_xattn_bk, L1_xattn_Wv, L1_xattn_bv)
    x = x + _L1_ffn_ref(_layernorm(x, axis=-1), L1_ffn_expert_weights, L1_ffn_hyperplanes)
    return x

_drawn_inputs = setup_inputs


def setup_inputs(seed=0):
    import zlib

    import numpy as np

    out = dict(_drawn_inputs(seed))
    spreads = {'L0_attn_ln_gamma': (1.0, 0.2),
     'L0_attn_ln_beta': (0.0, 0.1),
     'L1_attn_qn_scale': (1.0, 0.6),
     'L1_attn_kn_scale': (1.0, 0.6)}
    factors = {'L0_xattn_bq': 4.714,
     'L0_xattn_bk': 64.0,
     'L0_ffn_a': 8.0,
     'L0_ffn_b': 8.0,
     'L1_attn_q_w': 8.0,
     'L1_attn_q_b': 52.14,
     'L1_attn_k_w': 8.0,
     'L1_attn_k_b': 64.0,
     'L1_attn_v_w': 5.703,
     'L1_attn_v_b': 8.0,
     'L1_attn_o_w': 5.797,
     'L1_attn_o_b': 8.0,
     'L1_xattn_Wq': 8.0,
     'L1_xattn_bq': 22.887,
     'L1_xattn_Wk': 8.0,
     'L1_xattn_bk': 64.0,
     'L1_xattn_Wv': 3.001,
     'L1_xattn_bv': 8.0,
     'L1_ffn_expert_weights': 4.076,
     'L1_ffn_hyperplanes': 4.108}
    for name, (base, spread) in spreads.items():
        noise = np.random.default_rng([zlib.crc32(name.encode()), seed]).standard_normal(out[name].shape)
        drawn = base * np.exp(spread * noise) if base else spread * noise
        out[name] = jnp.asarray(drawn.astype(out[name].dtype))
    for name, factor in factors.items():
        out[name] = (out[name] * factor).astype(out[name].dtype)
    return out
```

```python
from contextlib import ExitStack

import numpy as np

import concourse.bass as bass
from concourse import mybir

ALU = mybir.AluOpType
ACT = mybir.ActivationFunctionType
F32 = mybir.dt.float32
BF16 = mybir.dt.bfloat16
I32 = mybir.dt.int32
AX_X = mybir.AxisListType.X

P = 128
B = 16
S = 256
D = 256
H = 16
HD = D // H
TT = S // P
KT = D // P
SC = 120
C = 192
HH = P // HD
BF_PARTS = 3
PAIRS = [(0, 0), (0, 1), (1, 0), (0, 2), (2, 0), (1, 1)]
STACK = len(PAIRS) * HD
STACK_M = STACK + BF_PARTS
EPS_LN = 1e-5
EPS_RMS = 1e-8
EPS_RENORM = 1e-8
NB = 6
E_COUNT = 64
CHUNKS = B * TT
W_NAMES = ["in_q", "in_k", "in_v", "in_o", "x_q", "x_k", "x_v", "x_o", "l_q", "l_k", "l_v", "l_o"]


def rope_tables():
    inv = (1.0 / np.float32(10000.0) ** (np.arange(0, HD, 2, dtype=np.float32) / np.float32(HD))).astype(np.float32)
    freqs = np.arange(S, dtype=np.float32)[:, None] * inv[None, :]
    emb = np.concatenate([freqs, freqs], axis=-1)
    cos, sin = np.cos(emb).astype(np.float32), np.sin(emb).astype(np.float32)
    sin = sin * np.where(np.arange(HD) % 2 == 0, -1.0, 1.0).astype(np.float32)
    out = []
    for t in (cos, sin):
        t = t.reshape(TT, P, 1, HD, 1).transpose(1, 0, 2, 3, 4)
        out.append(np.ascontiguousarray(np.broadcast_to(t, (P, TT, KT, HD, HH)).reshape(P, TT * D)).astype(np.float32))
    return out


def over_batches(eng, step):
    step(-1, 1, False, True)
    step(0, 0, True, True)
    with eng.Fori(0, B // 2 - 1) as i:
        step(2 * i + 1, 1, True, True)
        step(2 * i + 2, 0, True, True)
    step(B - 1, 1, True, False)


def alone(eng, passed):
    eng.sem_inc(passed, 1)


class StageSemaphores:

    def __init__(self, nc):
        self.nc, self.held = nc, []

    def __enter__(self):
        return self

    def new(self, name):
        self.held.append(self.nc.alloc_semaphore(name))
        return self.held[-1]

    def __exit__(self, *_):
        self.nc.clear_and_free_semaphores(self.held)
        self.nc.all_engine_barrier()


def known(n, *values):
    return isinstance(n, int) and n in values


def at(n):
    return bass.ds(n * (TT * D), TT * D)


def tile_at(n, tt):
    return bass.ds(n * (TT * D) + tt * D, D)


def norm_stats(dve, passed, link, x, n, st, mv, stats_ok, factors_ok):
    for t in range(TT):
        i = dve.bn_stats(st[:, t, :], x[:, tile_at(n, t)])
    link(i)
    alone(dve, passed)
    for t in range(TT):
        i = dve.bn_aggr(mv[:, t, :], st[:, t, :])
    i.then_inc(stats_ok, 1)
    dve.wait_ge(factors_ok, n + 1)


FACTOR_LINKS = {False: 1, True: 6}


def norm_factors(pool, passed, link, n, mv, small, minus_half, second_eps, stats_ok, factors_ok):
    pool.wait_ge(stats_ok, n + 1)
    alone(pool, passed)
    link(pool.tensor_scalar(small[:, 3, :], mv[:, :, 1], EPS_LN, None, ALU.add))
    i = pool.tensor_tensor(small[:, 0, :], small[:, 3, :], minus_half[:, 0:TT], ALU.pow)
    if second_eps is not None:
        link(i)
        link(pool.tensor_tensor(small[:, 1, :], mv[:, :, 1], small[:, 0, :], ALU.mult))
        link(pool.tensor_tensor(small[:, 3, :], small[:, 1, :], small[:, 0, :], ALU.mult))
        alone(pool, passed)
        link(pool.tensor_scalar(small[:, 3, :], small[:, 3, :], second_eps, None, ALU.add))
        link(pool.tensor_tensor(small[:, 1, :], small[:, 3, :], minus_half[:, 0:TT], ALU.pow))
        i = pool.tensor_tensor(small[:, 2, :], small[:, 1, :], small[:, 0, :], ALU.mult)
    i.then_inc(factors_ok, 1)


def setup_stage(nc, t, d):
    with ExitStack() as ctx:
        stage_sems = ctx.enter_context(StageSemaphores(nc))
        sem = lambda name: stage_sems.new(name)
        sb = lambda name, shape, dt: ctx.enter_context(nc.sbuf_tensor(name, shape, dt))
        raw = sb("raw", [P, len(W_NAMES), 2, D], F32)
        rows = sb("rows", [1, 5, D], F32)
        cols = sb("cols", [P, 4, KT], F32)
        beta_bc = sb("beta_bc", [P, KT, P], F32)
        zeros = sb("zeros", [P, P], F32)
        ffn_w = sb("ffn_w", [P, KT, D], F32)
        lora_a = sb("lora_a", [P, 2, HD], F32)
        lora_b = sb("lora_b", [HD, D], F32)
        lora_aT = sb("lora_aT", [HD, KT, P], F32)
        amax = sb("amax", [P, 1], F32)
        amax_all = sb("amax_all", [P, 1], F32)
        step7 = sb("step7", [P, 1], F32)
        inv_step = sb("inv_step", [P, 1], F32)
        quant = sb("quant", [P, KT, D], F32)
        ps = [ctx.enter_context(nc.psum_tensor(f"setup_ps{i}", [P, 2, D], F32)) for i in range(4)]

        w_in = sem("w_in")
        x_in = sem("x_in")
        small_in = sem("small_in")
        ident0 = sem("ident0")
        ident_ok = sem("ident_ok")
        ones_ok = sem("ones_ok")
        w_ps = sem("w_ps")
        w_out = sem("w_out")
        bcast_ps = sem("bcast_ps")
        bcast_out = sem("bcast_out")
        bias_ps = sem("bias_ps")
        bias_out = sem("bias_out")
        beta_ok = sem("beta_ok")
        scaled = sem("scaled")
        amax_ok = sem("amax_ok")
        amax_red = sem("amax_red")
        dve_own = sem("dve_own")
        aT_ps = sem("aT_ps")
        aT_ok = sem("aT_ok")
        ab_ps = sem("ab_ps")

        w_src = {"in_q": d["in_proj"][0:D], "in_k": d["in_proj"][D:2 * D], "in_v": d["in_proj"][2 * D:3 * D],
                 "in_o": d["out_proj"], "x_q": d["x_wq"], "x_k": d["x_wk"], "x_v": d["x_wv"], "x_o": d["x_wo"],
                 "l_q": d["l_qw"], "l_k": d["l_kw"], "l_v": d["l_vw"], "l_o": d["l_ow"]}
        block = ctx.enter_context(nc.Block())

        @block.sync
        def _(sp):
            for j, name in enumerate(W_NAMES):
                src = w_src[name]
                sp.dma_start(raw[:, j, :, 0:src.shape[1]], src.rearrange("(t p) f -> p t f", p=P)).then_inc(w_in, 16)
            sp.dma_start(ffn_w[:, :, :], d["ffn_w"].rearrange("(t p) f -> p t f", p=P)).then_inc(small_in, 16)
            sp.dma_start(lora_a[:, :, :], d["ffn_a"].rearrange("(t p) f -> p t f", p=P)).then_inc(small_in, 16)
            sp.dma_start(lora_b[:, :], d["ffn_b"]).then_inc(small_in, 16)
            sp.dma_start(t["hyper"][:, :, :], d["hyper"].rearrange("(t p) f -> p t f", p=P)).then_inc(small_in, 16)
            sp.dma_start(t["c_wq"][:, :, :], d["c_wq"].rearrange("(t p) f -> p t f", p=P)).then_inc(small_in, 16)
            for name in ("c_wk", "c_wv"):
                sp.dma_start(t[name][:, 0, :], d[name][0:P, :]).then_inc(small_in, 16)
                sp.dma_start(t[name][0:C - P, 1, :], d[name][P:C, :]).then_inc(small_in, 16)
            sp.dma_start(t["cos"][:, :], d["cos"]).then_inc(small_in, 16)
            sp.dma_start(t["sin"][:, :], d["sin"]).then_inc(small_in, 16)
            x_v = d["x"].rearrange("b (t p) f -> p (b t) f", p=P)
            for q in range(4):
                n = CHUNKS // 4
                sp.dma_start(t["x"][:, q * n * D:(q + 1) * n * D].rearrange("p (c f) -> p c f", f=D),
                             x_v[:, q * n:(q + 1) * n, :]).then_inc(x_in, 16)
            sp.wait_ge(x_in, 64)
            sp.wait_ge(small_in, 16 * 29)

        @block.scalar
        def _(act):
            for j, name in enumerate(("x_bv", "l_bq", "l_bk", "l_bv", "c_bv")):
                act.dma_start(rows[0:1, j, :], d[name].rearrange("(a n) -> a n", a=1)).then_inc(small_in, 16)
            for name in ("x_bo", "l_bo", "ffn_bias"):
                act.dma_start(t["row_" + name][0:1, :], d[name].rearrange("(a n) -> a n", a=1)).then_inc(small_in, 16)
            with nc.allow_non_contiguous_dma(reason="a vector of 256 spread over partitions"):
                for j, name in enumerate(("ln_gamma", "ln_beta", "qn", "kn")):
                    act.dma_start(cols[:, j, :], d[name].rearrange("(t p) -> p t", p=P)).then_inc(small_in, 16)
                for name in ("x_bq", "x_bk"):
                    for m in range(KT):
                        act.dma_start(t["col_" + name][:, m:m + 1],
                                      d[name].rearrange("(m h c) -> m c h", h=HH, c=HD)[m]).then_inc(small_in, 16)
                for name in ("c_bq", "c_bk"):
                    act.dma_start(t["col_" + name][:, :], d[name].rearrange("(t p) -> p t", p=P)).then_inc(small_in, 16)

        @block.gpsimd
        def _(pool):
            ident, ident_bf = t["ident"], t["ident_bf"]
            pool.memset(ident[:, :], 0.0).then_inc(ident0, 1)
            pool.memset(ident_bf[:, :], 0.0).then_inc(ident0, 1)
            pool.wait_ge(ident0, 2)
            for m in (ident, ident_bf):
                pool.affine_select(out=m[:, :], in_=m[:, :], compare_op=ALU.not_equal, fill=1.0, base=0,
                                   pattern=[[-1, P]], channel_multiplier=1).then_inc(ident_ok, 1)
            pool.wait_ge(amax_ok, 1)
            pool.partition_all_reduce(amax_all[:, :], amax[:, :], P, bass.bass_isa.ReduceOp.max).then_inc(amax_red, 1)

        @block.vector
        def _(dve):
            own = [0]

            def link(i):
                own[0] += 1
                i.then_inc(dve_own, 1)
                dve.wait_ge(dve_own, own[0])

            dve.memset(t["ones"][:, :], 1.0).then_inc(ones_ok, 1)
            dve.memset(zeros[:, :], 0.0)
            dve.memset(t["minus_half"][:, :], -0.5)
            link(dve.memset(t["head_ones"][:, :, :], 0.0))
            for par in range(2):
                link(dve.memset(t["head_ones"][:, par, par * HD:(par + 1) * HD], 1.0))
            for par in range(2):
                dve.memset(t["v"][par][:, :, :, :], 0.0)
                dve.memset(t["kstack"][par][STACK:STACK_M, :], 1.0)
            for j, name in enumerate(W_NAMES):
                dve.wait_ge(w_ps, j + 1)
                kk = [(0, P), (1, C - P)] if name in ("x_k", "x_v") else [(0, P), (1, P)]
                for k, rows_k in kk:
                    out, in_ = t["wT"][0:rows_k, j, k, :], ps[j % 2][0:rows_k, k, :]
                    if name[-1] in "qk":
                        out = out.rearrange("p (m c h) -> p m h c", m=KT, c=HD)
                        in_ = in_.rearrange("p (m h c) -> p m h c", m=KT, c=HD)
                        for m in range(KT):
                            i = dve.tensor_copy(out[:, m], in_[:, m])
                    else:
                        i = dve.tensor_copy(out, in_)
                i.then_inc(w_out, 1)
            dve.wait_ge(small_in, 16 * 29)
            for k in range(KT):
                i = dve.tensor_scalar(beta_bc[:, k, :], zeros[:, :], cols[:, 1, k:k + 1], None, ALU.add)
            i.then_inc(beta_ok, 1)
            dve.wait_ge(bias_ps, 1)
            dve.tensor_copy(t["col_in_q"][:, :], ps[2][:, 0, 0:KT])
            dve.tensor_copy(t["col_in_k"][:, :], ps[2][:, 0, KT:2 * KT])
            dve.tensor_copy(t["bc_in_v"][:, :], ps[3][:, 0, :]).then_inc(bias_out, 1)
            dve.wait_ge(w_out, len(W_NAMES))
            for j, col in ((0, 0), (1, 0), (2, 0), (8, 2), (9, 3)):
                for k in range(KT):
                    dve.tensor_scalar(t["wT"][:, j, k, :], t["wT"][:, j, k, :], cols[:, col, k:k + 1], None,
                                      ALU.mult).then_inc(scaled, 1)
            for j, name in enumerate(("bc_x_v", "bc_l_q", "bc_l_k", "bc_l_v", "bc_c_v", "bc_x_o", "bc_l_o", "bc_ffn")):
                dve.wait_ge(bcast_ps, j + 1)
                out, in_ = t[name][:, :], ps[j % 2][:, 0, :]
                if name in ("bc_l_q", "bc_l_k"):
                    out = out.rearrange("p (m c h) -> p m h c", m=KT, c=HD)
                    in_ = in_.rearrange("p (m h c) -> p m h c", m=KT, c=HD)
                    for m in range(KT):
                        i = dve.tensor_copy(out[:, m], in_[:, m])
                else:
                    i = dve.tensor_copy(out, in_)
                i.then_inc(bcast_out, 1)
            dve.tensor_reduce(amax[:, :], ffn_w[:, :, :].rearrange("p t f -> p (t f)"), AX_X, ALU.max,
                              apply_absolute_value=True).then_inc(amax_ok, 1)
            dve.wait_ge(amax_red, 1)
            link(dve.tensor_scalar(step7[:, :], amax_all[:, :], 1.0 / 7.0, None, ALU.mult))
            link(dve.reciprocal(inv_step[:, :], step7[:, :]))
            link(dve.tensor_scalar(quant[:, :, :], ffn_w[:, :, :], inv_step[:, 0:1], None, ALU.mult))
            link(dve.tensor_scalar(quant[:, :, :], quant[:, :, :], 12582912.0, None, ALU.add))
            link(dve.tensor_scalar(quant[:, :, :], quant[:, :, :], 12582912.0, None, ALU.subtract))
            link(dve.tensor_scalar(quant[:, :, :], quant[:, :, :], -8.0, 7.0, ALU.max, ALU.min))
            link(dve.tensor_scalar(quant[:, :, :], quant[:, :, :], step7[:, 0:1], None, ALU.mult))
            dve.wait_ge(aT_ps, 1)
            dve.tensor_copy(lora_aT[:, :, :], ps[2][0:HD, 0, :].rearrange("p (k c) -> p k c", k=KT)).then_inc(aT_ok, 1)
            dve.wait_ge(ab_ps, 1)
            dve.tensor_tensor(t["ffn"][:, :, :], quant[:, :, :], ps[3][:, :, :], ALU.add)

        @block.tensor
        def _(pe):
            ident = t["ident"]
            pe.wait_ge(ident_ok, 2)
            for j, name in enumerate(W_NAMES):
                pe.wait_ge(w_in, 16 * len(W_NAMES))
                if j >= 2:
                    pe.wait_ge(w_out, j - 1)
                kk = [(0, P), (1, C - P)] if name in ("x_k", "x_v") else [(0, P), (1, P)]
                for k, rows_k in kk:
                    for e in range(2):
                        i = pe.transpose(ps[j % 2][0:rows_k, k, e * P:(e + 1) * P],
                                         raw[:, j, e, k * P:k * P + rows_k], ident[:, :])
                i.then_inc(w_ps, 1)
            pe.wait_ge(w_out, len(W_NAMES))
            pe.wait_ge(beta_ok, 1)
            for j in range(2):
                for m in range(KT):
                    for k in range(KT):
                        pe.matmul(ps[2][:, 0, j * KT + m:j * KT + m + 1], t["wT"][:, j, k, m * P:(m + 1) * P],
                                  cols[:, 1, k:k + 1], start=(k == 0), stop=(k == KT - 1))
            for k in range(KT):
                i = pe.matmul(ps[3][:, 0, :], beta_bc[:, k, :], t["wT"][:, 2, k, :], start=(k == 0), stop=(k == KT - 1))
            i.then_inc(bias_ps, 1)
            pe.wait_ge(small_in, 16 * 29)
            pe.wait_ge(ones_ok, 1)
            srcs = [rows[0:1, j, :] for j in range(5)] + [t["row_" + n][0:1, :] for n in ("x_bo", "l_bo", "ffn_bias")]
            for j, src in enumerate(srcs):
                if j >= 2:
                    pe.wait_ge(bcast_out, j - 1)
                pe.matmul(ps[j % 2][:, 0, :], t["ones"][0:1, :], src, start=True, stop=True).then_inc(bcast_ps, 1)
            pe.wait_ge(bias_out, 1)
            for k in range(KT):
                i = pe.transpose(ps[2][0:HD, 0, k * P:(k + 1) * P], lora_a[:, k, :], ident[:, :])
            i.then_inc(aT_ps, 1)
            pe.wait_ge(aT_ok, 1)
            for k in range(KT):
                i = pe.matmul(ps[3][:, k, :], lora_aT[:, k, :], lora_b[:, :], start=True, stop=True)
            i.then_inc(ab_ps, 1)


def attention_stage(nc, t, d, kind):
    cross, sigmoid = kind == "cross", kind == "sigmoid"
    SK = SC if cross else S
    KC = 1 if cross else TT
    KP = SC if cross else P
    NC = 4 * KC
    HB = 512 // SK
    NS = TT * H // HB
    RQ = STACK if sigmoid else STACK_M
    WQ, WK, WV, WO = [{"self": 0, "cross": 4, "sigmoid": 8}[kind] + i for i in range(4)]
    with ExitStack() as ctx:
        pre = kind + "_"
        stage_sems = ctx.enter_context(StageSemaphores(nc))
        sem = lambda name: stage_sems.new(pre + name)
        sb = lambda name, shape, dt: ctx.enter_context(nc.sbuf_tensor(pre + name, shape, dt))
        st = sb("st", [P, TT, 6], F32)
        mv = sb("mv", [P, TT, 2], F32)
        small = sb("small", [P, 4, TT], F32)
        z = sb("z", [P, TT * D], F32)
        zT = sb("zT", [P, KT, S], F32)
        qf = sb("qf", [P, KT * S], F32)
        kf = sb("kf", [P, KT * SK], F32)
        rest = [sb(f"rest{i}", [P, KT * S], F32) for i in range(2)]
        qpart = [sb(f"qpart{i}", [P, KT * S], BF16) for i in range(BF_PARTS)]
        kpart = [sb(f"kpart{i}", [P, KT * SK], BF16) for i in range(BF_PARTS)]
        probs = [sb(f"probs{i}", [P, 4 * S], F32) for i in range(2)]
        rden = sb("rden", [P, 2, S], F32)
        attnT = sb("attnT", [P, KT, S], F32)
        qstack, kstack, v = t["qstack"], t["kstack"], t["v"]
        if cross:
            cx = sb("cx", [SC, C], F32)
            cxT = sb("cxT", [P, 2, SC], F32)
        if sigmoid:
            tok = [sb(f"tok{i}", [P, TT * D], F32) for i in range(2)]
            tok_cos = [sb(f"tok_cos{i}", [P, TT * D], F32) for i in range(2)]
            tok_sin = [sb(f"tok_sin{i}", [P, TT * D], F32) for i in range(2)]
            tok_rot = [sb(f"tok_rot{i}", [P, TT * D], F32) for i in range(2)]
            dsum = sb("dsum", [P, 2, S], F32)
        else:
            nmax = sb("nmax", [P, TT, H], F32)
            nrest = [sb(f"nrest{i}", [P, TT, H], F32) for i in range(2)]
            nparts = sb("nparts", [P, TT, BF_PARTS, H], BF16)
            nT = sb("nT", [BF_PARTS * H, S], BF16)
        pre_bank = [ctx.enter_context(nc.psum_tensor(f"{pre}bank{i}", [P, 512], F32)) for i in range(2)]
        sT = [ctx.enter_context(nc.psum_tensor(f"{pre}sT{i}", [P, 4 * S], F32)) for i in range(2)]
        od = [ctx.enter_context(nc.psum_tensor(f"{pre}od{i}", [P, 2, S], F32)) for i in range(2)]

        stats_ok = sem("stats_ok")
        factors_ok = sem("factors_ok")
        z_ok = sem("z_ok")
        dve_own = sem("dve_own")
        main_own = sem("main_own")
        pool_own = sem("pool_own")
        zT_ps, zT_ok = sem("zT_ps"), sem("zT_ok")
        q_ps, qf_ok = sem("q_ps"), sem("qf_ok")
        k_ps, kf_ok = sem("k_ps"), sem("kf_ok")
        v_ps, v_ok = sem("v_ps"), sem("v_ok")
        q_parts, k_parts = sem("q_parts"), sem("k_parts")
        q_dma, k_dma = sem("q_dma"), sem("k_dma")
        sT_ps, p_ok = sem("sT_ps"), sem("p_ok")
        pv_ps, attn_ok = sem("pv_ps"), sem("attn_ok")
        out_ps, res_ok, bo_ok = sem("out_ps"), sem("res_ok"), sem("bo_ok")
        cx_dma, cx_ps, cx_ok = (sem("cx_dma"), sem("cx_ps"), sem("cx_ok")) if cross else (None,) * 3
        s_ps, max_ok, n_ok = (sem("s_ps"), sem("max_ok"), sem("n_ok")) if not sigmoid else (None,) * 3
        nT_ps, nT_ok, n_dma = (sem("nT_ps"), sem("nT_ok"), sem("n_dma")) if not sigmoid else (None,) * 3
        tok_ok, rot_ok, tokq_ps, tokk_ps = (
            (sem("tok_ok"), sem("rot_ok"), sem("tokq_ps"), sem("tokk_ps")) if sigmoid else (None,) * 4)

        jobs = {"z": (zT_ok, 1, 1)}
        if sigmoid:
            jobs.update(tokq=(tok_ok, 2, 1), tokk=(tok_ok, 2, 2), v=(v_ok, 1, 1), q=(qf_ok, 1, 1), k=(kf_ok, 1, 1))
        else:
            if cross:
                jobs.update(cx=(cx_ok, 1, 1))
            jobs.update(q=(qf_ok, 1, 1), k=(kf_ok, 1, 1), v=(v_ok, 1, 1))
            jobs.update({("s", i): (max_ok, NS, i + 1) for i in range(NS)})
            jobs.update(nT=(nT_ok, 1, 1))
        order = list(jobs)

        def bank(job):
            return pre_bank[order.index(job) % 2]

        def bank_free(pe, job, n, first):
            j = order.index(job)
            if j >= 2:
                s, per, val = jobs[order[j - 2]]
                pe.wait_ge(s, n * per + val)
            elif not first:
                last = [o for i, o in enumerate(order) if i % 2 == j % 2][-1]
                s, per, val = jobs[last]
                pe.wait_ge(s, (n - 1) * per + val)

        def heads(c):
            half, par = c // KC // 2, c // KC % 2
            return half, par, [(g, 8 * half + 2 * g + par, ((2 * g + par) * KT + half)) for g in range(4)]

        block = ctx.enter_context(nc.Block())

        @block.sync
        def _(sp):
            passed = sem("sp_passed")
            def step(n, parity, main, pre):
                if not pre:
                    return
                n, parity, first = n + 1, 1 - parity, not main
                if cross:
                    if not first:
                        sp.wait_ge(cx_ps, n)
                        alone(sp, passed)
                    sp.dma_start(cx[:, :], d["ctx"][bass.ds(n, 1), :, :].rearrange("b s c -> (b s) c")
                                 ).then_inc(cx_dma, 16)
                sp.wait_ge(q_parts, n + 1)
                alone(sp, passed)
                if not first and not known(n, 1):
                    sp.wait_ge(sT_ps, (n - 1) * NC)
                for r, (a, _) in enumerate(PAIRS):
                    dst = qstack[parity][r * HD:(r + 1) * HD, :].rearrange("c (h x) -> c h x", h=HH)
                    sp.dma_start(dst, qpart[a][:, :]).then_inc(q_dma, 16)
                sp.wait_ge(k_parts, n + 1)
                for r, (_, b) in enumerate(PAIRS):
                    dst = kstack[parity][r * HD:(r + 1) * HD, 0:H * SK].rearrange("c (h x) -> c h x", h=HH)
                    sp.dma_start(dst, kpart[b][:, :]).then_inc(k_dma, 16)
                if not sigmoid:
                    sp.wait_ge(nT_ok, n + 1)
                    dst = qstack[parity][STACK:STACK_M, :].rearrange("c (h x) -> c h x", h=H)
                    sp.dma_start(dst, nT[:, :]).then_inc(n_dma, 16)

            over_batches(sp, step)

        @block.gpsimd
        def _(pool):
            passed = sem("pool_passed")
            second_eps = None if cross else EPS_RMS if sigmoid else EPS_LN
            per = FACTOR_LINKS[not cross] + (10 if sigmoid else 6)

            def step(n, parity, main, pre):
                m, first = n + 1, not main
                own = [0]

                def link(i):
                    own[0] += 1
                    i.then_inc(pool_own, 1)
                    pool.wait_ge(pool_own, m * per + own[0])

                if pre:
                    norm_factors(pool, passed, link, m, mv, small, t["minus_half"], second_eps, stats_ok, factors_ok)
                if main and kind != "self":
                    pool.wait_ge(z_ok, n + 1)
                    bias = t["bc_x_o" if cross else "bc_l_o"]
                    for tt in range(TT):
                        x_t = t["x"][:, tile_at(n, tt)]
                        i = pool.tensor_tensor(x_t, x_t, bias[:, :], ALU.add)
                    i.then_inc(bo_ok, 1)
                if not pre:
                    return

                if sigmoid:
                    for j in range(2):
                        pool.wait_ge(tok_ok, 2 * m + j + 1)
                        if not first:
                            pool.wait_ge(q_ps if j == 0 else k_ps, m)
                        pair = lambda a: a[:, :].rearrange("p (x two h) -> p x two h", two=2, h=HH)
                        link(pool.tensor_tensor(tok_cos[j][:, :], tok[j][:, :], t["cos"][:, :], ALU.mult))
                        pool.tensor_tensor(pair(tok_sin[j])[:, :, 0], pair(tok[j])[:, :, 1], pair(t["sin"])[:, :, 0], ALU.mult)
                        link(pool.tensor_tensor(pair(tok_sin[j])[:, :, 1], pair(tok[j])[:, :, 0], pair(t["sin"])[:, :, 1], ALU.mult))
                        i = pool.tensor_tensor(tok_rot[j][:, :], tok_cos[j][:, :], tok_sin[j][:, :], ALU.add)
                        i.then_inc(rot_ok, 1)
                for j, (src, parts, src_ok, dma, done, w) in enumerate((
                        (qf, qpart, qf_ok, q_dma, q_parts, KT * S), (kf, kpart, kf_ok, k_dma, k_parts, KT * SK))):
                    pool.wait_ge(src_ok, m + 1)
                    if not first:
                        pool.wait_ge(dma, m * 16 * len(PAIRS))
                    alone(pool, passed)
                    link(pool.tensor_copy(parts[0][:, :], src[:, :]))
                    link(pool.tensor_tensor(rest[j][:, 0:w], src[:, :], parts[0][:, :], ALU.subtract))
                    alone(pool, passed)
                    link(pool.tensor_copy(parts[1][:, :], rest[j][:, 0:w]))
                    i = pool.tensor_tensor(parts[2][:, :], rest[j][:, 0:w], parts[1][:, :], ALU.subtract)
                    i.then_inc(done, 1)
                assert own[0] == per, own

            over_batches(pool, step)

        @block.scalar
        def _(act):
            def exp(n, c, sem_n):
                g = n * NC + c
                act.wait_ge(sT_ps, g + 1)
                if not (sem_n and c < 2):
                    act.wait_ge(pv_ps, g - 1)
                func = ACT.Sigmoid if sigmoid else ACT.Exp
                act.activation(probs[c % 2][0:KP, :], sT[c % 2][0:KP, :], func, scale=HD ** -0.5).then_inc(p_ok, 1)

            def evac(job, m, first):
                if job == "z":
                    act.wait_ge(zT_ps, m + 1)
                    if not first:
                        act.wait_ge(v_ps, m)
                    act.activation(zT[:, :, :].rearrange("p k s -> p (k s)"), bank("z")[:, :], ACT.Identity).then_inc(zT_ok, 1)
                elif job == "cx":
                    act.wait_ge(cx_ps, m + 1)
                    if not first:
                        act.wait_ge(v_ps, m)
                    act.activation(cxT[:, 0, :], bank("cx")[:, 0:SC], ACT.Identity)
                    act.activation(cxT[0:C - P, 1, :], bank("cx")[0:C - P, SC:2 * SC], ACT.Identity).then_inc(cx_ok, 1)
                else:
                    ps_sem, dst, parts, ok, bias, w = {
                        "q": (q_ps, qf, q_parts, qf_ok, "q", S), "k": (k_ps, kf, k_parts, kf_ok, "k", SK)}[job]
                    act.wait_ge(ps_sem, m + 1)
                    if not first:
                        act.wait_ge(parts, m)
                    if sigmoid:
                        i = act.activation(dst[:, :], bank(job)[:, 0:KT * w], ACT.Identity)
                    else:
                        col = t[("col_x_b" if cross else "col_in_") + bias]
                        for j in range(KT):
                            i = act.activation(dst[:, j * w:(j + 1) * w], bank(job)[:, j * w:(j + 1) * w], ACT.Identity,
                                               bias=col[:, j:j + 1])
                    i.then_inc(ok, 1)

            def step(n, parity, main, pre):
                m, first = n + 1, not main
                todo = {0: ["z", "cx"] if cross else ["z"], 1: ["q", "k"]}
                if sigmoid:
                    todo = {0: ["z"], 4: ["q"], 5: ["k"]}
                sem_n = known(n, 0)
                for c in range(NC):
                    if main:
                        exp(n, c, sem_n)
                    if pre:
                        for job in todo.get(c, []):
                            evac(job, m, first)
                if pre and not sigmoid:
                    act.wait_ge(nT_ps, m + 1)
                    if not first:
                        act.wait_ge(n_dma, 16 * m)
                    act.activation(nT[:, :], bank("nT")[0:BF_PARTS * H, 0:S // 2].bitcast(BF16), ACT.Identity).then_inc(nT_ok, 1)

            over_batches(act, step)

        @block.vector
        def _(dve):
            passed = sem("dve_passed")
            def prepare_norm(m, first, link):
                norm_stats(dve, passed, link, t["x"], m, st, mv, stats_ok, factors_ok)
                if not first:
                    dve.wait_ge(zT_ps, m)
                r = 2 if kind == "self" else 0
                for tt in range(TT):
                    i = dve.tensor_scalar(z[:, tt * D:(tt + 1) * D], t["x"][:, tile_at(m, tt)],
                                          mv[:, tt, 0:1], small[:, r, tt:tt + 1], ALU.subtract, ALU.mult)
                i.then_inc(z_ok, 1)

            def token_major(m, j, first):
                dve.wait_ge(tokq_ps if j == 0 else tokk_ps, m + 1)
                if not first:
                    dve.wait_ge(q_ps if j == 0 else k_ps, m)
                for tt in range(TT):
                    i = dve.scalar_tensor_tensor(tok[j][:, tt * D:(tt + 1) * D], bank("tokq" if j == 0 else "tokk")[:, tt * D:(tt + 1) * D],
                                                 small[:, 1, tt:tt + 1], t["bc_l_q" if j == 0 else "bc_l_k"][:, :], ALU.mult, ALU.add)
                i.then_inc(tok_ok, 1)

            def values(m, parity, second):
                dve.wait_ge(v_ps, m + 1)
                if second is not None:
                    dve.wait_ge(pv_ps, second)
                bias = t["bc_x_v" if cross else "bc_l_v" if sigmoid else "bc_in_v"]
                for k in range(KC):
                    src = bank("v")[0:KP, k * D:(k + 1) * D].rearrange("p (x two c) -> p x two c", two=2, c=HD)
                    b = bias[0:KP, :].rearrange("p (x two c) -> p x two c", two=2, c=HD)
                    for par in range(2):
                        dst = v[parity][0:KP, k, :, par * 48:par * 48 + HD]
                        i = dve.tensor_tensor(dst, src[:, :, par, :], b[:, :, par, :], ALU.add)
                i.then_inc(v_ok, 1)

            def maxima(m, i, first):
                dve.wait_ge(s_ps, m * NS + i + 1)
                tt, h0 = i // (NS // TT), i % (NS // TT) * HB
                dve.tensor_reduce(nmax[:, tt, h0:h0 + HB], bank(("s", i))[:, 0:HB * SK].rearrange("p (h k) -> p h k", h=HB),
                                  AX_X, ALU.max, negate=True).then_inc(max_ok, 1)

            def max_parts(m, first, link):
                dve.wait_ge(max_ok, (m + 1) * NS)
                if not first:
                    dve.wait_ge(nT_ps, m)
                link(dve.tensor_copy(nparts[:, :, 0, :], nmax[:, :, :]))
                link(dve.tensor_tensor(nrest[0][:, :, :], nmax[:, :, :], nparts[:, :, 0, :], ALU.subtract))
                link(dve.tensor_copy(nparts[:, :, 1, :], nrest[0][:, :, :]))
                dve.tensor_tensor(nparts[:, :, 2, :], nrest[0][:, :, :], nparts[:, :, 1, :], ALU.subtract).then_inc(n_ok, 1)

            def normalise(n, half, link2):
                dve.wait_ge(pv_ps, n * NC + (half + 1) * NC // 2)
                src = od[half][:, 1, :]
                if sigmoid:
                    link2(dve.tensor_scalar(dsum[:, half], src, EPS_RENORM, None, ALU.add))
                    src = dsum[:, half]
                link2(dve.reciprocal(rden[:, half], src))
                dve.tensor_tensor(attnT[:, half, :], od[half][:, 0, :], rden[:, half], ALU.mult).then_inc(attn_ok, 1)

            def residual(n):
                dve.wait_ge(out_ps, n + 1)
                if kind != "self":
                    dve.wait_ge(bo_ok, n + 1)
                x_n = t["x"][:, at(n)]
                dve.tensor_tensor(x_n, od[0][:, :, :].rearrange("p a s -> p (a s)"), x_n, ALU.add).then_inc(res_ok, 1)

            per_pre = 1 if sigmoid else 4
            per_main = 4 if sigmoid else 2

            def step(n, parity, main, pre):
                m, first = n + 1, not main
                own, own2 = [0], [0]

                def link(i):
                    own[0] += 1
                    i.then_inc(dve_own, 1)
                    dve.wait_ge(dve_own, m * per_pre + own[0])

                def link2(i):
                    own2[0] += 1
                    i.then_inc(main_own, 1)
                    dve.wait_ge(main_own, n * per_main + own2[0])

                if pre:
                    prepare_norm(m, first, link)
                    if sigmoid:
                        token_major(m, 0, first)
                        token_major(m, 1, first)
                    values(m, 1 - parity, None if known(m, 0, 1) else (m - 1) * NC)
                    if not sigmoid:
                        for i in range(NS // 2):
                            maxima(m, i, first)
                if main:
                    if not known(n, 0):
                        dve.wait_ge(out_ps, n)
                    normalise(n, 0, link2)
                if pre and not sigmoid:
                    for i in range(NS // 2, NS):
                        maxima(m, i, first)
                    max_parts(m, first, link)
                if main:
                    normalise(n, 1, link2)
                    residual(n)
                if pre:
                    assert own[0] == per_pre, own
                if main:
                    assert own2[0] == per_main, own2

            over_batches(dve, step)

        @block.tensor
        def _(pe):
            passed = sem("pe_passed")
            ident = t["ident"]

            def prepare(job, m, parity, first):
                if job == "z":
                    pe.wait_ge(z_ok, m + 1)
                    bank_free(pe, job, m, first)
                    for k in range(KT):
                        for tt in range(TT):
                            i = pe.transpose(bank("z")[:, k * S + tt * P:k * S + (tt + 1) * P],
                                             z[:, tt * D + k * P:tt * D + (k + 1) * P], ident[:, :])
                    i.then_inc(zT_ps, 1)
                elif job == "cx":
                    pe.wait_ge(cx_dma, 16 * (m + 1))
                    bank_free(pe, job, m, first)
                    pe.transpose(bank("cx")[:, 0:SC], cx[:, 0:P], ident[0:SC, 0:SC])
                    pe.transpose(bank("cx")[0:C - P, SC:2 * SC], cx[:, P:C], ident[0:SC, 0:SC]).then_inc(cx_ps, 1)
                elif job in ("q", "k") and sigmoid:
                    j = 0 if job == "q" else 1
                    pe.wait_ge(rot_ok, 2 * m + j + 1)
                    bank_free(pe, job, m, first)
                    for k in range(KT):
                        for tt in range(TT):
                            i = pe.transpose(bank(job)[:, k * S + tt * P:k * S + (tt + 1) * P],
                                             tok_rot[j][:, tt * D + k * P:tt * D + (k + 1) * P], ident[:, :])
                    i.then_inc(q_ps if job == "q" else k_ps, 1)
                elif job in ("q", "k"):
                    w, wd = (WQ, S) if job == "q" else (WK, SK)
                    pe.wait_ge(zT_ok, m + 1)
                    if cross and job == "k":
                        pe.wait_ge(cx_ok, m + 1)
                    bank_free(pe, job, m, first)
                    for mt in range(KT):
                        for k in range(KT):
                            src, kp = (cxT, (P, C - P)[k]) if cross and job == "k" else (zT, P)
                            i = pe.matmul(bank(job)[:, mt * wd:(mt + 1) * wd], t["wT"][0:kp, w, k, mt * P:(mt + 1) * P],
                                          src[0:kp, k, :], start=(k == 0), stop=(k == KT - 1))
                    i.then_inc(q_ps if job == "q" else k_ps, 1)
                elif job in ("tokq", "tokk", "v"):
                    w = {"tokq": WQ, "tokk": WK, "v": WV}[job]
                    pe.wait_ge(zT_ok, m + 1)
                    bank_free(pe, job, m, first)
                    for tt in range(KC):
                        for k in range(KT):
                            src, kp = (cxT, (P, C - P)[k]) if cross else (zT, P)
                            i = pe.matmul(bank(job)[0:KP, tt * D:(tt + 1) * D], src[0:kp, k, tt * P:tt * P + KP],
                                          t["wT"][0:kp, w, k, :], start=(k == 0), stop=(k == KT - 1))
                    i.then_inc({"tokq": tokq_ps, "tokk": tokk_ps, "v": v_ps}[job], 1)
                elif job == "nT":
                    pe.wait_ge(n_ok, m + 1)
                    bank_free(pe, job, m, first)
                    alone(pe, passed)
                    for tt in range(TT):
                        i = pe.transpose(bank("nT")[0:BF_PARTS * H, tt * P // 2:(tt + 1) * P // 2].bitcast(BF16),
                                         nparts[:, tt, :, :].rearrange("p a h -> p (a h)"), t["ident_bf"][:, :])
                    i.then_inc(nT_ps, 1)
                else:
                    i0 = job[1]
                    if i0 == 0:
                        pe.wait_ge(q_dma, (m + 1) * 16 * len(PAIRS))
                        pe.wait_ge(k_dma, (m + 1) * 16 * len(PAIRS))
                    bank_free(pe, job, m, first)
                    tt, h0 = i0 // (NS // TT), i0 % (NS // TT) * HB
                    for j in range(HB):
                        i = pe.matmul(bank(job)[:, j * SK:(j + 1) * SK],
                                      qstack[parity][0:STACK, (h0 + j) * S + tt * P:(h0 + j) * S + (tt + 1) * P],
                                      kstack[parity][0:STACK, (h0 + j) * SK:(h0 + j + 1) * SK], start=True, stop=True)
                    i.then_inc(s_ps, 1)

            def scores(n, c, parity, n0):
                g = n * NC + c
                if not (n0 and c < 2):
                    pe.wait_ge(p_ok, g - 1)
                kt = c % KC
                for j, (_, _, col) in enumerate(heads(c)[2]):
                    i = pe.matmul(sT[c % 2][0:KP, j * S:(j + 1) * S],
                                  kstack[parity][0:RQ, col * SK + kt * KP:col * SK + (kt + 1) * KP],
                                  qstack[parity][0:RQ, col * S:(col + 1) * S], start=True, stop=True)
                i.then_inc(sT_ps, 1)

            def times_values(n, c, parity, n0):
                half, par, hs = heads(c)
                if c == 0 and not n0:
                    pe.wait_ge(res_ok, n)
                pe.wait_ge(p_ok, n * NC + c + 1)
                kt = c % KC
                first = c % (NC // 2) == 0
                last = c % (NC // 2) == NC // 2 - 1
                for which in range(2):
                    for j, (g, h, _) in enumerate(hs):
                        lhs = v[parity][0:KP, kt, h // 2, par * 32:(par + 1) * 32] if which == 0 else t["head_ones"][0:KP, par, :]
                        i = pe.matmul(od[half][32 * g:32 * (g + 1), which, :], lhs, probs[c % 2][0:KP, j * S:(j + 1) * S],
                                      start=(first and which == 0), stop=last, skip_group_check=True)
                i.then_inc(pv_ps, 1)

            def project(n):
                pe.wait_ge(attn_ok, TT * (n + 1))
                for tt in range(TT):
                    for k in range(KT):
                        i = pe.matmul(od[0][:, tt, :], attnT[:, k, tt * P:(tt + 1) * P], t["wT"][:, WO, k, :],
                                      start=(k == 0), stop=(k == KT - 1))
                i.then_inc(out_ps, 1)

            def step(n, parity, main, pre):
                m, first = n + 1, not main
                n0 = known(n, 0)
                if sigmoid:
                    todo = {0: ["z"], 1: ["tokq", "tokk"], 2: ["v"], 4: ["q"], 5: ["k"]}
                elif cross:
                    todo = {0: ["z", "cx"], 1: ["q", "k", "v"], 3: [("s", i) for i in range(NS)]}
                else:
                    todo = {0: ["z"], 1: ["q", "k"], 2: ["v"]}
                    for c in range(4, NC):
                        todo[c] = [("s", i) for i in range((c - 4) * NS // 4, (c - 3) * NS // 4)]
                if main:
                    pe.wait_ge(q_dma, (n + 1) * 16 * len(PAIRS))
                    pe.wait_ge(k_dma, (n + 1) * 16 * len(PAIRS))
                    pe.wait_ge(v_ok, n + 1)
                    if not sigmoid:
                        pe.wait_ge(n_dma, 16 * (n + 1))
                for c in range(NC):
                    if main:
                        scores(n, c, parity, n0)
                    if pre:
                        for job in todo.get(c, []):
                            prepare(job, m, 1 - parity, first)
                    if main and c >= 1:
                        times_values(n, c - 1, parity, n0)
                if main:
                    times_values(n, NC - 1, parity, n0)
                if pre and not sigmoid:
                    prepare("nT", m, 1 - parity, first)
                if main:
                    project(n)

            over_batches(pe, step)


def linear_stage(nc, t, d):
    with ExitStack() as ctx:
        stage_sems = ctx.enter_context(StageSemaphores(nc))
        sem = lambda name: stage_sems.new("ffn_" + name)
        sb = lambda name, shape, dt: ctx.enter_context(nc.sbuf_tensor("ffn_" + name, shape, dt))
        st = sb("st", [P, TT, 6], F32)
        mv = sb("mv", [P, TT, 2], F32)
        small = sb("small", [P, 4, TT], F32)
        z = [sb(f"z{i}", [P, TT * D], F32) for i in range(2)]
        zT = [sb(f"zT{i}", [P, KT * S], F32) for i in range(2)]
        zT_bank = [ctx.enter_context(nc.psum_tensor(f"ffn_zT_bank{i}", [P, 512], F32)) for i in range(2)]
        out_bank = [ctx.enter_context(nc.psum_tensor(f"ffn_out_bank{i}", [P, 512], F32)) for i in range(2)]
        stats_ok, factors_ok, pool_own, z_ok, zT_ps, zT_ok, out_ps, res_ok, bo_ok, dve_own = map(
            sem, ("stats_ok", "factors_ok", "pool_own", "z_ok", "zT_ps", "zT_ok", "out_ps", "res_ok", "bo_ok", "dve_own"))
        block = ctx.enter_context(nc.Block())

        @block.vector
        def _(dve):
            passed = sem("dve_passed")
            def step(n, parity, main, pre):
                m = n + 1
                own = [0]

                def link(i):
                    own[0] += 1
                    i.then_inc(dve_own, 1)
                    dve.wait_ge(dve_own, m + own[0])

                if pre:
                    norm_stats(dve, passed, link, t["x"], m, st, mv, stats_ok, factors_ok)
                    if not known(m, 0, 1):
                        dve.wait_ge(zT_ps, m - 1)
                    for tt in range(TT):
                        i = dve.tensor_scalar(z[1 - parity][:, tt * D:(tt + 1) * D], t["x"][:, tile_at(m, tt)],
                                              mv[:, tt, 0:1], small[:, 0, tt:tt + 1], ALU.subtract, ALU.mult)
                    i.then_inc(z_ok, 1)
                if main:
                    dve.wait_ge(out_ps, n + 1)
                    dve.wait_ge(bo_ok, n + 1)
                    x_n = t["x"][:, at(n)]
                    dve.tensor_tensor(x_n, out_bank[parity][:, :], x_n, ALU.add).then_inc(res_ok, 1)

            over_batches(dve, step)

        @block.gpsimd
        def _(pool):
            passed = sem("pool_passed")
            def step(n, parity, main, pre):
                def link(i):
                    i.then_inc(pool_own, 1)
                    pool.wait_ge(pool_own, n + 2)

                if pre:
                    norm_factors(pool, passed, link, n + 1, mv, small, t["minus_half"], None, stats_ok, factors_ok)
                if main:
                    pool.wait_ge(z_ok, n + 1)
                    for tt in range(TT):
                        x_t = t["x"][:, tile_at(n, tt)]
                        i = pool.tensor_tensor(x_t, x_t, t["bc_ffn"][:, :], ALU.add)
                    i.then_inc(bo_ok, 1)

            over_batches(pool, step)

        @block.scalar
        def _(act):
            def step(n, parity, main, pre):
                m = n + 1
                if pre:
                    act.wait_ge(zT_ps, m + 1)
                    if not known(m, 0, 1):
                        act.wait_ge(out_ps, m - 1)
                    act.activation(zT[1 - parity][:, :], zT_bank[1 - parity][:, :], ACT.Identity).then_inc(zT_ok, 1)

            over_batches(act, step)

        @block.tensor
        def _(pe):
            passed = sem("pe_passed")
            def step(n, parity, main, pre):
                m = n + 1
                if pre:
                    pe.wait_ge(z_ok, m + 1)
                    if not known(m, 0, 1):
                        pe.wait_ge(zT_ok, m - 1)
                    for k in range(KT):
                        for tt in range(TT):
                            i = pe.transpose(zT_bank[1 - parity][:, k * S + tt * P:k * S + (tt + 1) * P],
                                             z[1 - parity][:, tt * D + k * P:tt * D + (k + 1) * P], t["ident"][:, :])
                    i.then_inc(zT_ps, 1)
                if main:
                    pe.wait_ge(zT_ok, n + 1)
                    if not known(n, 0, 1):
                        pe.wait_ge(res_ok, n - 1)
                    for tt in range(TT):
                        for k in range(KT):
                            i = pe.matmul(out_bank[parity][:, tt * D:(tt + 1) * D],
                                          zT[parity][:, k * S + tt * P:k * S + (tt + 1) * P], t["ffn"][:, k, :],
                                          start=(k == 0), stop=(k == KT - 1))
                    i.then_inc(out_ps, 1)

            over_batches(pe, step)


def single_head_stage(nc, t, d):
    SCALE = D ** -0.5
    with ExitStack() as ctx:
        stage_sems = ctx.enter_context(StageSemaphores(nc))
        sem = lambda name: stage_sems.new("one_" + name)
        sb = lambda name, shape, dt: ctx.enter_context(nc.sbuf_tensor("one_" + name, shape, dt))
        st = sb("st", [P, TT, 6], F32)
        mv = sb("mv", [P, TT, 2], F32)
        small = sb("small", [P, 4, TT], F32)
        z = sb("z", [P, TT * D], F32)
        zT = sb("zT", [P, KT, S], F32)
        cx = sb("cx", [SC, C], F32)
        cxT = sb("cxT", [P, 2, SC], F32)
        qT = [sb(f"qT{i}", [P, KT, S], F32) for i in range(2)]
        kT = [sb(f"kT{i}", [P, KT, SC], F32) for i in range(2)]
        v = [sb(f"v{i}", [SC, D], F32) for i in range(2)]
        nmax = sb("nmax", [P, TT], F32)
        nbias = sb("nbias", [P, TT], F32)
        probs = sb("probs", [P, TT, SC], F32)
        sums = sb("sums", [P, TT], F32)
        rden = sb("rden", [P, TT], F32)
        pT = sb("pT", [SC, S], F32)
        pre_bank = [ctx.enter_context(nc.psum_tensor(f"one_pre{i}", [P, 512], F32)) for i in range(2)]
        s_bank = ctx.enter_context(nc.psum_tensor("one_s_bank", [P, 512], F32))
        pT_bank = ctx.enter_context(nc.psum_tensor("one_pT_bank", [P, 512], F32))
        out_bank = ctx.enter_context(nc.psum_tensor("one_out_bank", [P, 512], F32))
        stats_ok, factors_ok, pool_own = map(sem, ("stats_ok", "factors_ok", "pool_own"))
        (z_ok, dve_own, main_own, zT_ps, zT_ok, cx_dma, cx_ps, cx_ok, q_ps, q_ok, k_ps, k_ok, v_ps, v_ok, s_ps,
         max_ok, exp_ok, pT_ps, pT_ok, out_ps, res_ok) = map(sem, (
             "z_ok", "dve_own", "main_own", "zT_ps", "zT_ok", "cx_dma", "cx_ps", "cx_ok", "q_ps", "q_ok", "k_ps",
             "k_ok", "v_ps", "v_ok", "s_ps", "max_ok", "exp_ok", "pT_ps", "pT_ok", "out_ps", "res_ok"))
        block = ctx.enter_context(nc.Block())

        @block.sync
        def _(sp):
            passed = sem("sp_passed")
            def step(n, parity, main, pre):
                m = n + 1
                if pre:
                    if main:
                        sp.wait_ge(cx_ps, m)
                        alone(sp, passed)
                    sp.dma_start(cx[:, :], d["ctx"][bass.ds(m, 1), :, :].rearrange("b s c -> (b s) c")
                                 ).then_inc(cx_dma, 16)

            over_batches(sp, step)

        @block.gpsimd
        def _(pool):
            passed = sem("pool_passed")
            def step(n, parity, main, pre):
                def link(i):
                    i.then_inc(pool_own, 1)
                    pool.wait_ge(pool_own, n + 2)

                if pre:
                    norm_factors(pool, passed, link, n + 1, mv, small, t["minus_half"], None, stats_ok, factors_ok)

            over_batches(pool, step)

        @block.vector
        def _(dve):
            passed = sem("dve_passed")
            def step(n, parity, main, pre):
                m = n + 1
                own, own2 = [0], [0]

                def link(i):
                    own[0] += 1
                    i.then_inc(dve_own, 1)
                    dve.wait_ge(dve_own, m + own[0])

                if main:
                    dve.wait_ge(s_ps, n + 1)
                    i = dve.tensor_reduce(nmax[:, :], s_bank[:, 0:TT * SC].rearrange("p (t k) -> p t k", t=TT),
                                          AX_X, ALU.max, negate=True)
                    i.then_inc(main_own, 1)
                    dve.wait_ge(main_own, 2 * n + 1)
                    dve.tensor_scalar(nbias[:, :], nmax[:, :], SCALE, None, ALU.mult).then_inc(max_ok, 1)
                if pre:
                    norm_stats(dve, passed, link, t["x"], m, st, mv, stats_ok, factors_ok)
                    if main:
                        dve.wait_ge(zT_ps, m)
                    for tt in range(TT):
                        i = dve.tensor_scalar(z[:, tt * D:(tt + 1) * D], t["x"][:, tile_at(m, tt)],
                                              mv[:, tt, 0:1], small[:, 0, tt:tt + 1], ALU.subtract, ALU.mult)
                    i.then_inc(z_ok, 1)
                    dve.wait_ge(v_ps, m + 1)
                    if not known(m, 0, 1):
                        dve.wait_ge(out_ps, m - 1)
                    dve.tensor_tensor(v[1 - parity][:, :], pre_bank[0][0:SC, 0:D], t["bc_c_v"][0:SC, :],
                                      ALU.add).then_inc(v_ok, 1)
                if main:
                    dve.wait_ge(exp_ok, n + 1)
                    dve.reciprocal(rden[:, :], sums[:, :]).then_inc(main_own, 1)
                    dve.wait_ge(main_own, 2 * n + 2)
                    dve.wait_ge(out_ps, n + 1)
                    for tt in range(TT):
                        x_t = t["x"][:, tile_at(n, tt)]
                        i = dve.scalar_tensor_tensor(x_t, out_bank[:, tt * D:(tt + 1) * D], rden[:, tt:tt + 1], x_t,
                                                     ALU.mult, ALU.add)
                    i.then_inc(res_ok, 1)

            over_batches(dve, step)

        @block.scalar
        def _(act):
            def step(n, parity, main, pre):
                m = n + 1
                if main:
                    act.wait_ge(max_ok, n + 1)
                    if not known(n, 0):
                        act.wait_ge(pT_ps, n)
                        act.wait_ge(res_ok, n)
                    for tt in range(TT):
                        i = act.activation(probs[:, tt, :], s_bank[:, tt * SC:(tt + 1) * SC], ACT.Exp,
                                           bias=nbias[:, tt:tt + 1], scale=SCALE, accum_out=sums[:, tt:tt + 1])
                    i.then_inc(exp_ok, 1)
                if pre:
                    act.wait_ge(zT_ps, m + 1)
                    if main:
                        act.wait_ge(q_ps, m)
                    act.activation(zT[:, :, :].rearrange("p k s -> p (k s)"), pre_bank[0][:, :], ACT.Identity).then_inc(zT_ok, 1)
                    act.wait_ge(cx_ps, m + 1)
                    if main:
                        act.wait_ge(v_ps, m)
                    act.activation(cxT[:, 0, :], pre_bank[1][:, 0:SC], ACT.Identity)
                    act.activation(cxT[0:C - P, 1, :], pre_bank[1][0:C - P, SC:2 * SC], ACT.Identity).then_inc(cx_ok, 1)
                    act.wait_ge(q_ps, m + 1)
                    if not known(m, 0, 1):
                        act.wait_ge(s_ps, m - 1)
                    for j in range(KT):
                        i = act.activation(qT[1 - parity][:, j, :], pre_bank[0][:, j * S:(j + 1) * S], ACT.Identity,
                                           bias=t["col_c_bq"][:, j:j + 1])
                    i.then_inc(q_ok, 1)
                    act.wait_ge(k_ps, m + 1)
                    for j in range(KT):
                        i = act.activation(kT[1 - parity][:, j, :], pre_bank[1][:, j * SC:(j + 1) * SC], ACT.Identity,
                                           bias=t["col_c_bk"][:, j:j + 1])
                    i.then_inc(k_ok, 1)
                if main:
                    act.wait_ge(pT_ps, n + 1)
                    if not known(n, 0):
                        act.wait_ge(out_ps, n)
                    act.activation(pT[:, :], pT_bank[0:SC, 0:S], ACT.Identity).then_inc(pT_ok, 1)

            over_batches(act, step)

        @block.tensor
        def _(pe):
            passed = sem("pe_passed")
            ident = t["ident"]

            def step(n, parity, main, pre):
                m, par = n + 1, 1 - parity
                if main:
                    pe.wait_ge(q_ok, n + 1)
                    pe.wait_ge(k_ok, n + 1)
                    if not known(n, 0):
                        pe.wait_ge(exp_ok, n)
                    for tt in range(TT):
                        for k in range(KT):
                            i = pe.matmul(s_bank[:, tt * SC:(tt + 1) * SC], qT[parity][:, k, tt * P:(tt + 1) * P],
                                          kT[parity][:, k, :], start=(k == 0), stop=(k == KT - 1))
                    i.then_inc(s_ps, 1)
                if pre:
                    pe.wait_ge(z_ok, m + 1)
                    if main:
                        pe.wait_ge(v_ok, m)
                    for k in range(KT):
                        for tt in range(TT):
                            i = pe.transpose(pre_bank[0][:, k * S + tt * P:k * S + (tt + 1) * P],
                                             z[:, tt * D + k * P:tt * D + (k + 1) * P], ident[:, :])
                    i.then_inc(zT_ps, 1)
                    pe.wait_ge(cx_dma, 16 * (m + 1))
                    if main:
                        pe.wait_ge(k_ok, m)
                    pe.transpose(pre_bank[1][:, 0:SC], cx[:, 0:P], ident[0:SC, 0:SC])
                    pe.transpose(pre_bank[1][0:C - P, SC:2 * SC], cx[:, P:C], ident[0:SC, 0:SC]).then_inc(cx_ps, 1)
                    pe.wait_ge(zT_ok, m + 1)
                    for j in range(KT):
                        for k in range(KT):
                            i = pe.matmul(pre_bank[0][:, j * S:(j + 1) * S], t["c_wq"][:, k, j * P:(j + 1) * P],
                                          zT[:, k, :], start=(k == 0), stop=(k == KT - 1))
                    i.then_inc(q_ps, 1)
                    pe.wait_ge(cx_ok, m + 1)
                    for j in range(KT):
                        for k, kp in ((0, P), (1, C - P)):
                            i = pe.matmul(pre_bank[1][:, j * SC:(j + 1) * SC], t["c_wk"][0:kp, k, j * P:(j + 1) * P],
                                          cxT[0:kp, k, :], start=(k == 0), stop=(k == 1))
                    i.then_inc(k_ps, 1)
                    pe.wait_ge(q_ok, m + 1)
                    for k, kp in ((0, P), (1, C - P)):
                        i = pe.matmul(pre_bank[0][0:SC, 0:D], cxT[0:kp, k, :], t["c_wv"][0:kp, k, :],
                                      start=(k == 0), stop=(k == 1))
                    i.then_inc(v_ps, 1)
                if main:
                    pe.wait_ge(exp_ok, n + 1)
                    if not known(n, 0):
                        pe.wait_ge(pT_ok, n)
                    for tt in range(TT):
                        i = pe.transpose(pT_bank[0:SC, tt * P:(tt + 1) * P], probs[:, tt, :], ident[:, :])
                    i.then_inc(pT_ps, 1)
                    pe.wait_ge(pT_ok, n + 1)
                    pe.wait_ge(v_ok, n + 1)
                    if not known(n, 0):
                        pe.wait_ge(res_ok, n)
                    for tt in range(TT):
                        i = pe.matmul(out_bank[:, tt * D:(tt + 1) * D], pT[:, tt * P:(tt + 1) * P], v[parity][:, :],
                                      start=True, stop=True)
                    i.then_inc(out_ps, 1)

            over_batches(pe, step)


def expert_stage(nc, t, d):
    RING = 4
    with ExitStack() as ctx:
        stage_sems = ctx.enter_context(StageSemaphores(nc))
        sem = lambda name: stage_sems.new("moe_" + name)
        sb = lambda name, shape, dt: ctx.enter_context(nc.sbuf_tensor("moe_" + name, shape, dt))
        st = sb("st", [P, TT, 6], F32)
        mv = sb("mv", [P, TT, 2], F32)
        small = sb("small", [P, 4, TT], F32)
        z = [sb(f"z{i}", [P, TT * D], F32) for i in range(2)]
        zT_all = sb("zT_all", [P, B * KT * S], F32)
        zT = [sb(f"zT{i}", [P, KT, P], F32) for i in range(RING)]
        col_sums = sb("col_sums", [P, B * KT * TT], F32)
        emb = sb("emb", [P, KT, B, TT], F32)
        work = sb("work", [CHUNKS, 8, NB], F32)
        one = sb("one", [CHUNKS, 8], F32)
        picked = sb("picked", [CHUNKS, 2], I32)
        picked_row = sb("picked_row", [1, 2 * CHUNKS], I32)
        experts = [sb(f"experts{i}", [P, 2, KT, D], F32) for i in range(RING)]
        zT_bank = [ctx.enter_context(nc.psum_tensor(f"moe_zT_bank{i}", [P, 512], F32)) for i in range(2)]
        out_bank = [ctx.enter_context(nc.psum_tensor(f"moe_out_bank{i}", [P, 512], F32)) for i in range(RING)]
        hash_bank = ctx.enter_context(nc.psum_tensor("moe_hash", [P, 512], F32))
        stats_ok, factors_ok, pool_own = map(sem, ("stats_ok", "factors_ok", "pool_own"))
        (z_ok, dve_own, zT_ps, zT_ok, sum_ok, emb_ok, hash_ps, hash_own, picked_ok, picked_dma, w_dma0, w_dma1, w_dma2,
         w_dma3, zcopy_ok, out_ps, res_ok, store) = map(sem, (
             "z_ok", "dve_own", "zT_ps", "zT_ok", "sum_ok", "emb_ok", "hash_ps", "hash_own", "picked_ok", "picked_dma",
             "w_dma0", "w_dma1", "w_dma2", "w_dma3", "zcopy_ok", "out_ps", "res_ok", "store"))
        w_dma = [w_dma0, w_dma1, w_dma2, w_dma3]
        block = ctx.enter_context(nc.Block())

        def over_chunks(eng, step):
            for slot in range(RING):
                step(0, slot, slot)
            with eng.Fori(1, CHUNKS // RING) as i:
                for slot in range(RING):
                    step(i, i * RING + slot, slot)

        @block.sync
        def _(sp):
            sp.wait_ge(picked_ok, 1)
            sp.dma_start(picked_row[:, :], picked[:, :]).then_inc(picked_dma, 16)
            sp.wait_ge(picked_dma, 16)

            def step(i, c, slot):
                for j in range(2):
                    e = sp.value_load(picked_row[0:1, bass.ds(c * 2 + j, 1)], min_val=0, max_val=E_COUNT - 1)
                    if not known(i, 0) and j == 0:
                        sp.wait_ge(out_ps, c - RING + 1)
                    sp.dma_start(experts[slot][:, j, :, :],
                                 d["experts"][bass.ds(e, 1), :, :].rearrange("e (t p) f -> p (e t) f", p=P)
                                 ).then_inc(w_dma[slot], 16)

            over_chunks(sp, step)

        @block.gpsimd
        def _(pool):
            passed = sem("pool_passed")
            def step(n, parity, main, pre):
                def link(i):
                    i.then_inc(pool_own, 1)
                    pool.wait_ge(pool_own, n + 2)

                if pre:
                    norm_factors(pool, passed, link, n + 1, mv, small, t["minus_half"], None, stats_ok, factors_ok)

            over_batches(pool, step)
            pool.wait_ge(zT_ok, B)

            def step(i, c, slot):
                if not known(i, 0):
                    pool.wait_ge(out_ps, c - RING + 1)
                base = i * (RING // TT * KT * S) + (slot // TT) * (KT * S) + (slot % TT) * P
                alone(pool, passed)
                for k in range(KT):
                    j = pool.tensor_copy(zT[slot][:, k, :], zT_all[:, bass.ds(base + k * S, P)])
                j.then_inc(zcopy_ok, 1)

            over_chunks(pool, step)

        @block.vector
        def _(dve):
            passed = sem("dve_passed")
            def step(n, parity, main, pre):
                m = n + 1
                own = [0]

                def link(i):
                    own[0] += 1
                    i.then_inc(dve_own, 1)
                    dve.wait_ge(dve_own, m + own[0])

                if pre:
                    norm_stats(dve, passed, link, t["x"], m, st, mv, stats_ok, factors_ok)
                    if not known(m, 0, 1):
                        dve.wait_ge(zT_ps, m - 1)
                    for tt in range(TT):
                        i = dve.tensor_scalar(z[1 - parity][:, tt * D:(tt + 1) * D], t["x"][:, tile_at(m, tt)],
                                              mv[:, tt, 0:1], small[:, 0, tt:tt + 1], ALU.subtract, ALU.mult)
                    i.then_inc(z_ok, 1)
                if main:
                    dve.wait_ge(zT_ok, n + 1)
                    dve.tensor_reduce(col_sums[:, bass.ds(n * (KT * TT), KT * TT)],
                                      zT_all[:, bass.ds(n * (KT * S), KT * S)].rearrange("p (x s) -> p x s", s=P),
                                      AX_X, ALU.add).then_inc(sum_ok, 1)

            over_batches(dve, step)
            own = [0]

            def link(i):
                own[0] += 1
                i.then_inc(hash_own, 1)
                dve.wait_ge(hash_own, own[0])

            dve.wait_ge(sum_ok, B)
            sums = col_sums[:, :].rearrange("p (b k t) -> p k b t", k=KT, t=TT)
            for k in range(KT):
                i = dve.tensor_scalar(emb[:, k], sums[:, k], 1.0 / P, None, ALU.mult)
            i.then_inc(emb_ok, 1)
            W = lambda j: work[:, j, :]
            powers, proj, bits, weights, small_abs, tie, cand, flipped = map(W, range(8))
            for b in range(NB):
                i = dve.memset(work[:, 0, b:b + 1], float(2 ** b))
            link(i)
            dve.wait_ge(hash_ps, 1)
            link(dve.tensor_copy(proj, hash_bank[0:CHUNKS, 0:NB]))
            link(dve.tensor_scalar(bits, proj, 0.0, None, ALU.is_gt))
            link(dve.tensor_tensor(weights, bits, powers, ALU.mult))
            link(dve.tensor_reduce(one[:, 0:1], weights, AX_X, ALU.add))
            link(dve.scalar_tensor_tensor(small_abs, proj, -1.0, proj, ALU.mult, ALU.max))
            link(dve.tensor_reduce(one[:, 1:2], small_abs, AX_X, ALU.min))
            link(dve.tensor_scalar(tie, small_abs, one[:, 1:2], None, ALU.is_equal))
            link(dve.tensor_scalar(tie, tie, -float(2 ** NB), float(2 ** NB), ALU.mult, ALU.add))
            link(dve.tensor_tensor(cand, tie, powers, ALU.add))
            link(dve.tensor_reduce(one[:, 2:3], cand, AX_X, ALU.min))
            link(dve.tensor_scalar(flipped, powers, one[:, 2:3], None, ALU.is_equal))
            link(dve.tensor_tensor(flipped, flipped, weights, ALU.mult))
            link(dve.tensor_reduce(one[:, 3:4], flipped, AX_X, ALU.add))
            link(dve.tensor_tensor(one[:, 4:5], one[:, 0:1], one[:, 2:3], ALU.add))
            link(dve.tensor_scalar(one[:, 5:6], one[:, 3:4], -2.0, None, ALU.mult))
            link(dve.tensor_tensor(one[:, 6:7], one[:, 4:5], one[:, 5:6], ALU.add))
            dve.tensor_copy(picked[:, 0:1], one[:, 0:1])
            dve.tensor_copy(picked[:, 1:2], one[:, 6:7]).then_inc(picked_ok, 1)

            def chunk(i, c, slot):
                dve.wait_ge(out_ps, c + 1)
                x_c = t["x"][:, bass.ds(c * D, D)]
                dve.scalar_tensor_tensor(x_c, out_bank[slot][:, 0:D], 0.5, x_c, ALU.mult, ALU.add).then_inc(res_ok, 1)

            over_chunks(dve, chunk)

        @block.scalar
        def _(act):
            def step(n, parity, main, pre):
                m = n + 1
                if pre:
                    act.wait_ge(zT_ps, m + 1)
                    act.activation(zT_all[:, bass.ds(m * (KT * S), KT * S)], zT_bank[1 - parity][:, :],
                                   ACT.Identity).then_inc(zT_ok, 1)

            over_batches(act, step)

            def chunk(i, c, slot):
                act.wait_ge(res_ok, c + 1)
                seq = i * (RING // TT) + slot // TT
                act.dma_start(d["out"][bass.ds(seq, 1), (slot % TT) * P:(slot % TT + 1) * P, :].rearrange("b p f -> (b p) f"),
                              t["x"][:, bass.ds(c * D, D)]).then_inc(store, 16)

            over_chunks(act, chunk)
            act.wait_ge(store, 16 * CHUNKS)

        @block.tensor
        def _(pe):
            passed = sem("pe_passed")
            def step(n, parity, main, pre):
                m = n + 1
                if pre:
                    pe.wait_ge(z_ok, m + 1)
                    if not known(m, 0, 1):
                        pe.wait_ge(zT_ok, m - 1)
                    for k in range(KT):
                        for tt in range(TT):
                            i = pe.transpose(zT_bank[1 - parity][:, k * S + tt * P:k * S + (tt + 1) * P],
                                             z[1 - parity][:, tt * D + k * P:tt * D + (k + 1) * P], t["ident"][:, :])
                    i.then_inc(zT_ps, 1)

            over_batches(pe, step)
            pe.wait_ge(emb_ok, 1)
            for k in range(KT):
                i = pe.matmul(hash_bank[0:CHUNKS, 0:NB], emb[:, k].rearrange("p b t -> p (b t)"), t["hyper"][:, k, :],
                              start=(k == 0), stop=(k == KT - 1))
            i.then_inc(hash_ps, 1)

            def chunk(i, c, slot):
                pe.wait_ge(zcopy_ok, c + 1)
                pe.wait_ge(w_dma[slot], i * 32 + 32)
                if not known(i, 0):
                    pe.wait_ge(res_ok, c - RING + 1)
                for j in range(2):
                    for k in range(KT):
                        m = pe.matmul(out_bank[slot][:, 0:D], zT[slot][:, k, :], experts[slot][:, j, k, :],
                                      start=(j == 0 and k == 0), stop=(j == 1 and k == KT - 1))
                m.then_inc(out_ps, 1)

            over_chunks(pe, chunk)


def decoder_kernel(nc, d):
    with ExitStack() as ctx:
        def sb(name, shape, dt):
            return ctx.enter_context(nc.sbuf_tensor(name, shape, dt))

        t = {"x": sb("x_res", [P, CHUNKS * D], F32),
             "wT": sb("wT", [P, len(W_NAMES), KT, D], F32),
             "ident": sb("ident", [P, P], F32), "ident_bf": sb("ident_bf", [P, P], BF16),
             "ones": sb("ones", [P, P], F32), "head_ones": sb("head_ones", [P, 2, 32], F32),
             "minus_half": sb("minus_half", [P, TT], F32),
             "hyper": sb("hyper_w", [P, KT, NB], F32), "cos": sb("cos_t", [P, TT * D], F32), "sin": sb("sin_t", [P, TT * D], F32),
             "ffn": sb("ffn_m", [P, KT, D], F32),
             "v": [sb(f"v_heads{i}", [P, TT, H // 2, 64], F32) for i in range(2)],
             "qstack": [sb(f"qstack{i}", [STACK_M, H * S], BF16) for i in range(2)],
             "kstack": [sb(f"kstack{i}", [STACK_M, H * S], BF16) for i in range(2)]}
        for name in ("c_wq", "c_wk", "c_wv"):
            t[name] = sb(name + "_m", [P, KT, D], F32)
        for name in ("bc_in_v", "bc_x_v", "bc_l_q", "bc_l_k", "bc_l_v", "bc_c_v", "bc_x_o", "bc_l_o", "bc_ffn"):
            t[name] = sb(name, [P, D], F32)
        for name in ("row_x_bo", "row_l_bo", "row_ffn_bias"):
            t[name] = sb(name, [1, D], F32)
        for name in ("col_in_q", "col_in_k", "col_x_bq", "col_x_bk", "col_c_bq", "col_c_bk"):
            t[name] = sb(name, [P, KT], F32)
        setup_stage(nc, t, d)
        attention_stage(nc, t, d, "self")
        attention_stage(nc, t, d, "cross")
        linear_stage(nc, t, d)
        attention_stage(nc, t, d, "sigmoid")
        single_head_stage(nc, t, d)
        expert_stage(nc, t, d)


_INS = {
    "x": "x", "ctx": "ctx_768", "in_proj": "L0_attn_in_proj_w", "out_proj": "L0_attn_out_proj_w",
    "ln_gamma": "L0_attn_ln_gamma", "ln_beta": "L0_attn_ln_beta",
    "x_wq": "L0_xattn_wq", "x_bq": "L0_xattn_bq", "x_wk": "L0_xattn_wk", "x_bk": "L0_xattn_bk",
    "x_wv": "L0_xattn_wv", "x_bv": "L0_xattn_bv", "x_wo": "L0_xattn_wo", "x_bo": "L0_xattn_bo",
    "ffn_w": "L0_ffn_kernel", "ffn_bias": "L0_ffn_bias", "ffn_a": "L0_ffn_a", "ffn_b": "L0_ffn_b",
    "l_qw": "L1_attn_q_w", "l_bq": "L1_attn_q_b", "l_kw": "L1_attn_k_w", "l_bk": "L1_attn_k_b",
    "l_vw": "L1_attn_v_w", "l_bv": "L1_attn_v_b", "l_ow": "L1_attn_o_w", "l_bo": "L1_attn_o_b",
    "qn": "L1_attn_qn_scale", "kn": "L1_attn_kn_scale",
    "c_wq": "L1_xattn_Wq", "c_bq": "L1_xattn_bq", "c_wk": "L1_xattn_Wk", "c_bk": "L1_xattn_bk",
    "c_wv": "L1_xattn_Wv", "c_bv": "L1_xattn_bv",
    "experts": "L1_ffn_expert_weights", "hyper": "L1_ffn_hyperplanes",
}


def kernel(**inputs):
    import numpy as _np
    import concourse.bacc as _bacc
    from concourse import mybir as _mybir
    from concourse.bass_utils import run_bass_kernel_spmd as _run

    nc = _bacc.Bacc("TRN2", target_bir_lowering=False, num_devices=1)
    arrays = {key: _np.ascontiguousarray(inputs[name]) for key, name in _INS.items()}
    arrays["cos"], arrays["sin"] = rope_tables()
    arrays = {f"in_{key}": a for key, a in arrays.items()}
    d = {key[3:]: nc.dram_tensor(key, a.shape, _mybir.dt.from_np(a.dtype), kind="ExternalInput").ap()
         for key, a in arrays.items()}
    d["out"] = nc.dram_tensor("out_y", (B, S, D), _mybir.dt.float32, kind="ExternalOutput").ap()
    decoder_kernel(nc, d)
    r = _run(nc, [arrays], core_ids=[0])
    return r.results[0]["out_y"]
```

```python
from contextlib import ExitStack

import numpy as np

import concourse.bass as bass
from concourse import mybir

ALU = mybir.AluOpType
ACT = mybir.ActivationFunctionType
F32 = mybir.dt.float32
BF16 = mybir.dt.bfloat16
I32 = mybir.dt.int32
AX_X = mybir.AxisListType.X

P = 128
B = 16
S = 256
D = 256
H = 16
HD = D // H
TT = S // P
KT = D // P
SC = 120
C = 192
HH = P // HD
BF_PARTS = 3
PAIRS = [(0, 0), (0, 1), (1, 0), (0, 2), (2, 0), (1, 1)]
STACK = len(PAIRS) * HD
STACK_M = STACK + BF_PARTS
EPS_LN = 1e-5
EPS_RMS = 1e-8
EPS_RENORM = 1e-8
NB = 6
E_COUNT = 64
CHUNKS = B * TT
W_NAMES = ["in_q", "in_k", "in_v", "in_o", "x_q", "x_k", "x_v", "x_o", "l_q", "l_k", "l_v", "l_o"]


def rope_tables():
    inv = (1.0 / np.float32(10000.0) ** (np.arange(0, HD, 2, dtype=np.float32) / np.float32(HD))).astype(np.float32)
    freqs = np.arange(S, dtype=np.float32)[:, None] * inv[None, :]
    emb = np.concatenate([freqs, freqs], axis=-1)
    cos, sin = np.cos(emb).astype(np.float32), np.sin(emb).astype(np.float32)
    sin = sin * np.where(np.arange(HD) % 2 == 0, -1.0, 1.0).astype(np.float32)
    out = []
    for t in (cos, sin):
        t = t.reshape(TT, P, 1, HD, 1).transpose(1, 0, 2, 3, 4)
        out.append(np.ascontiguousarray(np.broadcast_to(t, (P, TT, KT, HD, HH)).reshape(P, TT * D)).astype(np.float32))
    return out


def over_batches(eng, step):
    step(-1, 1, False, True)
    step(0, 0, True, True)
    with eng.Fori(0, B // 2 - 1) as i:
        step(2 * i + 1, 1, True, True)
        step(2 * i + 2, 0, True, True)
    step(B - 1, 1, True, False)


def over_batches_ahead(eng, step):
    for n in range(-2, 1):
        step(n, n % 2)
    with eng.Fori(0, B // 2 - 2) as i:
        step(2 * i + 1, 1)
        step(2 * i + 2, 0)
    for n in range(B - 3, B + 1):
        step(n, n % 2)


def doing(n):
    if not isinstance(n, int):
        return True, True, True, True
    return tuple(0 <= n + ahead < B for ahead in (-1, 0, 1, 2))


def alone(eng, passed):
    eng.sem_inc(passed, 1)


class StageSemaphores:

    def __init__(self, nc):
        self.nc, self.held = nc, []

    def __enter__(self):
        return self

    def new(self, name):
        self.held.append(self.nc.alloc_semaphore(name))
        return self.held[-1]

    def __exit__(self, *_):
        self.nc.clear_and_free_semaphores(self.held)
        self.nc.all_engine_barrier()


def known(n, *values):
    return isinstance(n, int) and n in values


def at(n):
    return bass.ds(n * (TT * D), TT * D)


def tile_at(n, tt):
    return bass.ds(n * (TT * D) + tt * D, D)


def tile_stats(dve, passed, link, x, n, st, mv):
    alone(dve, passed)
    for t in range(TT):
        i = dve.bn_stats(st[:, t, 0:6], x[:, tile_at(n, t)])
    link(i)
    alone(dve, passed)
    for t in range(TT):
        i = dve.bn_aggr(st[:, t, 6:8], st[:, t, 0:6])
    link(i)
    alone(dve, passed)
    return dve.tensor_copy(mv[:, bass.ds(n * (TT * 2), TT * 2)].rearrange("p (t two) -> p t two", two=2), st[:, :, 6:8])


def norm_factors(pool, own_sem, t, second_eps, factors_ok):
    own = [0]

    def link(i):
        own[0] += 1
        i.then_inc(own_sem, 1)
        pool.wait_ge(own_sem, own[0])

    f, var = t["factors"], t["mv"][:, :].rearrange("p (c two) -> p c two", two=2)[:, :, 1]
    link(pool.tensor_scalar(f[:, 3, :], var, EPS_LN, None, ALU.add))
    i = pool.tensor_tensor(f[:, 0, :], f[:, 3, :], t["minus_half"][:, :], ALU.pow)
    if second_eps is not None:
        link(i)
        link(pool.tensor_tensor(f[:, 1, :], var, f[:, 0, :], ALU.mult))
        link(pool.tensor_tensor(f[:, 3, :], f[:, 1, :], f[:, 0, :], ALU.mult))
        link(pool.tensor_scalar(f[:, 3, :], f[:, 3, :], second_eps, None, ALU.add))
        link(pool.tensor_tensor(f[:, 1, :], f[:, 3, :], t["minus_half"][:, :], ALU.pow))
        i = pool.tensor_tensor(f[:, 2, :], f[:, 1, :], f[:, 0, :], ALU.mult)
    i.then_inc(factors_ok, 1)


def normalise_rows(dve, t, z, n, which=0):
    for tt in range(TT):
        i = dve.tensor_scalar(z[:, tt * D:(tt + 1) * D], t["x"][:, tile_at(n, tt)],
                              t["mv"][:, bass.ds(n * (TT * 2) + tt * 2, 1)], t["factors"][:, which, bass.ds(n * TT + tt, 1)],
                              ALU.subtract, ALU.mult)
    return i


def setup_stage(nc, t, d):
    with ExitStack() as ctx:
        stage_sems = ctx.enter_context(StageSemaphores(nc))
        sem = lambda name: stage_sems.new(name)
        sb = lambda name, shape, dt: ctx.enter_context(nc.sbuf_tensor(name, shape, dt))
        raw = sb("raw", [P, len(W_NAMES), 2, D], F32)
        st = sb("st", [P, CHUNKS, 6], F32)
        rows = sb("rows", [1, 5, D], F32)
        cols = sb("cols", [P, 4, KT], F32)
        beta_bc = sb("beta_bc", [P, KT, P], F32)
        zeros = sb("zeros", [P, P], F32)
        ffn_w = sb("ffn_w", [P, KT, D], F32)
        lora_a = sb("lora_a", [P, 2, HD], F32)
        lora_b = sb("lora_b", [HD, D], F32)
        lora_aT = sb("lora_aT", [HD, KT, P], F32)
        amax = sb("amax", [P, 1], F32)
        amax_all = sb("amax_all", [P, 1], F32)
        step7 = sb("step7", [P, 1], F32)
        inv_step = sb("inv_step", [P, 1], F32)
        quant = sb("quant", [P, KT, D], F32)
        ps = [ctx.enter_context(nc.psum_tensor(f"setup_ps{i}", [P, 2, D], F32)) for i in range(4)]

        w_in = sem("w_in")
        x_in = sem("x_in")
        small_in = sem("small_in")
        ident0 = sem("ident0")
        ident_ok = sem("ident_ok")
        ones_ok = sem("ones_ok")
        w_ps = sem("w_ps")
        w_out = sem("w_out")
        bcast_ps = sem("bcast_ps")
        bcast_out = sem("bcast_out")
        bias_ps = sem("bias_ps")
        bias_out = sem("bias_out")
        beta_ok = sem("beta_ok")
        scaled = sem("scaled")
        amax_ok = sem("amax_ok")
        amax_red = sem("amax_red")
        dve_own = sem("dve_own")
        aT_ps = sem("aT_ps")
        aT_ok = sem("aT_ok")
        ab_ps = sem("ab_ps")

        w_src = {"in_q": d["in_proj"][0:D], "in_k": d["in_proj"][D:2 * D], "in_v": d["in_proj"][2 * D:3 * D],
                 "in_o": d["out_proj"], "x_q": d["x_wq"], "x_k": d["x_wk"], "x_v": d["x_wv"], "x_o": d["x_wo"],
                 "l_q": d["l_qw"], "l_k": d["l_kw"], "l_v": d["l_vw"], "l_o": d["l_ow"]}
        block = ctx.enter_context(nc.Block())

        @block.sync
        def _(sp):
            for j, name in enumerate(W_NAMES):
                src = w_src[name]
                sp.dma_start(raw[:, j, :, 0:src.shape[1]], src.rearrange("(t p) f -> p t f", p=P)).then_inc(w_in, 16)
            sp.dma_start(ffn_w[:, :, :], d["ffn_w"].rearrange("(t p) f -> p t f", p=P)).then_inc(small_in, 16)
            sp.dma_start(lora_a[:, :, :], d["ffn_a"].rearrange("(t p) f -> p t f", p=P)).then_inc(small_in, 16)
            sp.dma_start(lora_b[:, :], d["ffn_b"]).then_inc(small_in, 16)
            sp.dma_start(t["hyper"][:, :, :], d["hyper"].rearrange("(t p) f -> p t f", p=P)).then_inc(small_in, 16)
            sp.dma_start(t["c_wq"][:, :, :], d["c_wq"].rearrange("(t p) f -> p t f", p=P)).then_inc(small_in, 16)
            for name in ("c_wk", "c_wv"):
                sp.dma_start(t[name][:, 0, :], d[name][0:P, :]).then_inc(small_in, 16)
                sp.dma_start(t[name][0:C - P, 1, :], d[name][P:C, :]).then_inc(small_in, 16)
            sp.dma_start(t["cos"][:, :], d["cos"]).then_inc(small_in, 16)
            sp.dma_start(t["sin"][:, :], d["sin"]).then_inc(small_in, 16)
            x_v = d["x"].rearrange("b (t p) f -> p (b t) f", p=P)
            for q in range(4):
                n = CHUNKS // 4
                sp.dma_start(t["x"][:, q * n * D:(q + 1) * n * D].rearrange("p (c f) -> p c f", f=D),
                             x_v[:, q * n:(q + 1) * n, :]).then_inc(x_in, 16)
            sp.wait_ge(x_in, 64)
            sp.wait_ge(small_in, 16 * 29)

        @block.scalar
        def _(act):
            for j, name in enumerate(("x_bv", "l_bq", "l_bk", "l_bv", "c_bv")):
                act.dma_start(rows[0:1, j, :], d[name].rearrange("(a n) -> a n", a=1)).then_inc(small_in, 16)
            for name in ("x_bo", "l_bo", "ffn_bias"):
                act.dma_start(t["row_" + name][0:1, :], d[name].rearrange("(a n) -> a n", a=1)).then_inc(small_in, 16)
            with nc.allow_non_contiguous_dma(reason="a vector of 256 spread over partitions"):
                for j, name in enumerate(("ln_gamma", "ln_beta", "qn", "kn")):
                    act.dma_start(cols[:, j, :], d[name].rearrange("(t p) -> p t", p=P)).then_inc(small_in, 16)
                for name in ("x_bq", "x_bk"):
                    for m in range(KT):
                        act.dma_start(t["col_" + name][:, m:m + 1],
                                      d[name].rearrange("(m h c) -> m c h", h=HH, c=HD)[m]).then_inc(small_in, 16)
                for name in ("c_bq", "c_bk"):
                    act.dma_start(t["col_" + name][:, :], d[name].rearrange("(t p) -> p t", p=P)).then_inc(small_in, 16)

        @block.gpsimd
        def _(pool):
            ident, ident_bf = t["ident"], t["ident_bf"]
            pool.memset(ident[:, :], 0.0).then_inc(ident0, 1)
            pool.memset(ident_bf[:, :], 0.0).then_inc(ident0, 1)
            pool.wait_ge(ident0, 2)
            for m in (ident, ident_bf):
                pool.affine_select(out=m[:, :], in_=m[:, :], compare_op=ALU.not_equal, fill=1.0, base=0,
                                   pattern=[[-1, P]], channel_multiplier=1).then_inc(ident_ok, 1)
            pool.wait_ge(amax_ok, 1)
            pool.partition_all_reduce(amax_all[:, :], amax[:, :], P, bass.bass_isa.ReduceOp.max).then_inc(amax_red, 1)

        @block.vector
        def _(dve):
            own = [0]

            def link(i):
                own[0] += 1
                i.then_inc(dve_own, 1)
                dve.wait_ge(dve_own, own[0])

            dve.memset(t["ones"][:, :], 1.0).then_inc(ones_ok, 1)
            dve.memset(zeros[:, :], 0.0)
            dve.memset(t["minus_half"][:, :], -0.5)
            link(dve.memset(t["head_ones"][:, :, :], 0.0))
            for par in range(2):
                link(dve.memset(t["head_ones"][:, par, par * HD:(par + 1) * HD], 1.0))
            for par in range(2):
                dve.memset(t["v"][par][:, :, :, :], 0.0)
                dve.memset(t["kstack"][par][STACK:STACK_M, :], 1.0)
            for j, name in enumerate(W_NAMES):
                dve.wait_ge(w_ps, j + 1)
                kk = [(0, P), (1, C - P)] if name in ("x_k", "x_v") else [(0, P), (1, P)]
                for k, rows_k in kk:
                    out, in_ = t["wT"][0:rows_k, j, k, :], ps[j % 2][0:rows_k, k, :]
                    if name[-1] in "qk":
                        out = out.rearrange("p (m c h) -> p m h c", m=KT, c=HD)
                        in_ = in_.rearrange("p (m h c) -> p m h c", m=KT, c=HD)
                        for m in range(KT):
                            i = dve.tensor_copy(out[:, m], in_[:, m])
                    else:
                        i = dve.tensor_copy(out, in_)
                i.then_inc(w_out, 1)
            dve.wait_ge(small_in, 16 * 29)
            for k in range(KT):
                i = dve.tensor_scalar(beta_bc[:, k, :], zeros[:, :], cols[:, 1, k:k + 1], None, ALU.add)
            i.then_inc(beta_ok, 1)
            dve.wait_ge(bias_ps, 1)
            dve.tensor_copy(t["col_in_q"][:, :], ps[2][:, 0, 0:KT])
            dve.tensor_copy(t["col_in_k"][:, :], ps[2][:, 0, KT:2 * KT])
            dve.tensor_copy(t["bc_in_v"][:, :], ps[3][:, 0, :]).then_inc(bias_out, 1)
            dve.wait_ge(w_out, len(W_NAMES))
            for j, col in ((0, 0), (1, 0), (2, 0), (8, 2), (9, 3)):
                for k in range(KT):
                    dve.tensor_scalar(t["wT"][:, j, k, :], t["wT"][:, j, k, :], cols[:, col, k:k + 1], None,
                                      ALU.mult).then_inc(scaled, 1)
            for j, name in enumerate(("bc_x_v", "bc_l_q", "bc_l_k", "bc_l_v", "bc_c_v", "bc_x_o", "bc_l_o", "bc_ffn")):
                dve.wait_ge(bcast_ps, j + 1)
                out, in_ = t[name][:, :], ps[j % 2][:, 0, :]
                if name in ("bc_l_q", "bc_l_k"):
                    out = out.rearrange("p (m c h) -> p m h c", m=KT, c=HD)
                    in_ = in_.rearrange("p (m h c) -> p m h c", m=KT, c=HD)
                    for m in range(KT):
                        i = dve.tensor_copy(out[:, m], in_[:, m])
                else:
                    i = dve.tensor_copy(out, in_)
                i.then_inc(bcast_out, 1)
            dve.wait_ge(x_in, 16 * 4)
            for c in range(CHUNKS):
                i = dve.bn_stats(st[:, c, :], t["x"][:, c * D:(c + 1) * D])
            link(i)
            for c in range(CHUNKS):
                dve.bn_aggr(t["mv"][:, 2 * c:2 * c + 2], st[:, c, :])
            dve.tensor_reduce(amax[:, :], ffn_w[:, :, :].rearrange("p t f -> p (t f)"), AX_X, ALU.max,
                              apply_absolute_value=True).then_inc(amax_ok, 1)
            dve.wait_ge(amax_red, 1)
            link(dve.tensor_scalar(step7[:, :], amax_all[:, :], 1.0 / 7.0, None, ALU.mult))
            link(dve.reciprocal(inv_step[:, :], step7[:, :]))
            link(dve.tensor_scalar(quant[:, :, :], ffn_w[:, :, :], inv_step[:, 0:1], None, ALU.mult))
            link(dve.tensor_scalar(quant[:, :, :], quant[:, :, :], 12582912.0, None, ALU.add))
            link(dve.tensor_scalar(quant[:, :, :], quant[:, :, :], 12582912.0, None, ALU.subtract))
            link(dve.tensor_scalar(quant[:, :, :], quant[:, :, :], -8.0, 7.0, ALU.max, ALU.min))
            link(dve.tensor_scalar(quant[:, :, :], quant[:, :, :], step7[:, 0:1], None, ALU.mult))
            dve.wait_ge(aT_ps, 1)
            dve.tensor_copy(lora_aT[:, :, :], ps[2][0:HD, 0, :].rearrange("p (k c) -> p k c", k=KT)).then_inc(aT_ok, 1)
            dve.wait_ge(ab_ps, 1)
            dve.tensor_tensor(t["ffn"][:, :, :], quant[:, :, :], ps[3][:, :, :], ALU.add)

        @block.tensor
        def _(pe):
            ident = t["ident"]
            pe.wait_ge(ident_ok, 2)
            for j, name in enumerate(W_NAMES):
                pe.wait_ge(w_in, 16 * len(W_NAMES))
                if j >= 2:
                    pe.wait_ge(w_out, j - 1)
                kk = [(0, P), (1, C - P)] if name in ("x_k", "x_v") else [(0, P), (1, P)]
                for k, rows_k in kk:
                    for e in range(2):
                        i = pe.transpose(ps[j % 2][0:rows_k, k, e * P:(e + 1) * P],
                                         raw[:, j, e, k * P:k * P + rows_k], ident[:, :])
                i.then_inc(w_ps, 1)
            pe.wait_ge(w_out, len(W_NAMES))
            pe.wait_ge(beta_ok, 1)
            for j in range(2):
                for m in range(KT):
                    for k in range(KT):
                        pe.matmul(ps[2][:, 0, j * KT + m:j * KT + m + 1], t["wT"][:, j, k, m * P:(m + 1) * P],
                                  cols[:, 1, k:k + 1], start=(k == 0), stop=(k == KT - 1))
            for k in range(KT):
                i = pe.matmul(ps[3][:, 0, :], beta_bc[:, k, :], t["wT"][:, 2, k, :], start=(k == 0), stop=(k == KT - 1))
            i.then_inc(bias_ps, 1)
            pe.wait_ge(small_in, 16 * 29)
            pe.wait_ge(ones_ok, 1)
            srcs = [rows[0:1, j, :] for j in range(5)] + [t["row_" + n][0:1, :] for n in ("x_bo", "l_bo", "ffn_bias")]
            for j, src in enumerate(srcs):
                if j >= 2:
                    pe.wait_ge(bcast_out, j - 1)
                pe.matmul(ps[j % 2][:, 0, :], t["ones"][0:1, :], src, start=True, stop=True).then_inc(bcast_ps, 1)
            pe.wait_ge(bias_out, 1)
            for k in range(KT):
                i = pe.transpose(ps[2][0:HD, 0, k * P:(k + 1) * P], lora_a[:, k, :], ident[:, :])
            i.then_inc(aT_ps, 1)
            pe.wait_ge(aT_ok, 1)
            for k in range(KT):
                i = pe.matmul(ps[3][:, k, :], lora_aT[:, k, :], lora_b[:, :], start=True, stop=True)
            i.then_inc(ab_ps, 1)


def attention_stage(nc, t, d, kind):
    cross, sigmoid = kind == "cross", kind == "sigmoid"
    SK = SC if cross else S
    KC = 1 if cross else TT
    KP = SC if cross else P
    NC = 4 * KC
    HB = 512 // SK
    NS = TT * H // HB
    RQ = STACK if sigmoid else STACK_M
    STACKED = 16 * len(PAIRS)
    WQ, WK, WV, WO = [{"self": 0, "cross": 4, "sigmoid": 8}[kind] + i for i in range(4)]
    with ExitStack() as ctx:
        pre = kind + "_"
        stage_sems = ctx.enter_context(StageSemaphores(nc))
        sem = lambda name: stage_sems.new(pre + name)
        sb = lambda name, shape, dt: ctx.enter_context(nc.sbuf_tensor(pre + name, shape, dt))
        st = sb("st", [P, TT, 8], F32)
        z = sb("z", [P, TT * D], F32)
        zT = sb("zT", [P, KT, S], F32)
        rest = {"q": sb("qrest", [P, KT * S], F32), "k": sb("krest", [P, KT * SK], F32)}
        parts = {"q": [[sb(f"qpart{p}{i}", [P, KT * S], BF16) for i in range(BF_PARTS)] for p in range(2)],
                 "k": [[sb(f"kpart{p}{i}", [P, KT * SK], BF16) for i in range(BF_PARTS)] for p in range(2)]}
        width = {"q": S, "k": SK}
        probs = [sb(f"probs{i}", [P, 4 * S], F32) for i in range(2)]
        rden = sb("rden", [P, 2, S], F32)
        attnT = sb("attnT", [P, KT, S], F32)
        qstack, kstack, v = t["qstack"], t["kstack"], t["v"]
        if cross:
            cx = sb("cx", [SC, C], F32)
            cxT = sb("cxT", [P, 2, SC], F32)
        if sigmoid:
            tok = [sb(f"tok{i}", [P, TT * D], F32) for i in range(2)]
            tok_cos = [sb(f"tok_cos{i}", [P, TT * D], F32) for i in range(2)]
            tok_sin = [sb(f"tok_sin{i}", [P, TT * D], F32) for i in range(2)]
            tok_rot = [sb(f"tok_rot{i}", [P, TT * D], F32) for i in range(2)]
            dsum = sb("dsum", [P, 2, S], F32)
        else:
            nmax = sb("nmax", [P, TT, H], F32)
            nrest = sb("nrest", [P, TT, H], F32)
            nparts = sb("nparts", [P, TT, BF_PARTS, H], BF16)
            nT = sb("nT", [BF_PARTS * H, S], BF16)
        pre_bank = [ctx.enter_context(nc.psum_tensor(f"{pre}bank{i}", [P, 512], F32)) for i in range(2)]
        sT = [ctx.enter_context(nc.psum_tensor(f"{pre}sT{i}", [P, 4 * S], F32)) for i in range(2)]
        od = [ctx.enter_context(nc.psum_tensor(f"{pre}od{i}", [P, 2, S], F32)) for i in range(2)]

        factors_ok, pool_own = sem("factors_ok"), sem("pool_own")
        z_ok = sem("z_ok")
        parts_own = sem("parts_own")
        main_own = sem("main_own")
        stats_own = sem("stats_own")
        rope_own = sem("rope_own")
        zT_ps, zT_ok = sem("zT_ps"), sem("zT_ok")
        proj_ps = {"q": sem("q_ps"), "k": sem("k_ps")}
        first_ok = {"q": sem("q_first"), "k": sem("k_first")}
        rest_ok = {"q": sem("q_rest"), "k": sem("k_rest")}
        second_ok = {"q": sem("q_second"), "k": sem("k_second")}
        parts_ok = {"q": sem("q_parts"), "k": sem("k_parts")}
        stack_dma = {"q": sem("q_dma"), "k": sem("k_dma")}
        v_ps, v_ok = sem("v_ps"), sem("v_ok")
        sT_ps, p_ok = sem("sT_ps"), sem("p_ok")
        pv_ps, attn_ok = sem("pv_ps"), sem("attn_ok")
        out_ps, res_ok, bo_ok = sem("out_ps"), sem("res_ok"), sem("bo_ok")
        cx_dma, cx_ps, cx_ok = (sem("cx_dma"), sem("cx_ps"), sem("cx_ok")) if cross else (None,) * 3
        s_ps, max_ok, n_ok = (sem("s_ps"), sem("max_ok"), sem("n_ok")) if not sigmoid else (None,) * 3
        nT_ps, nT_ok, n_dma = (sem("nT_ps"), sem("nT_ok"), sem("n_dma")) if not sigmoid else (None,) * 3
        tok_ok, rot_ok, tokq_ps, tokk_ps = (
            (sem("tok_ok"), sem("rot_ok"), sem("tokq_ps"), sem("tokk_ps")) if sigmoid else (None,) * 4)

        jobs = {"v": (1, v_ok, 1, 1), "z": (2, zT_ok, 1, 1)}
        if sigmoid:
            jobs.update(tokq=(2, tok_ok, 2, 1), tokk=(2, tok_ok, 2, 2))
        if cross:
            jobs.update(cx=(2, cx_ok, 1, 1))
        jobs.update(q=(2, rest_ok["q"], 1, 1), k=(2, rest_ok["k"], 1, 1))
        if not sigmoid:
            jobs.update({("s", i): (1, max_ok, NS, i + 1) for i in range(NS)})
            jobs.update(nT=(1, nT_ok, 1, 1))
        order = list(jobs)

        def bank(job):
            return pre_bank[order.index(job) % 2]

        def bank_free(pe, job, n):
            mine = order.index(job)
            for back, others in ((0, order[:mine]), (1, order), (2, order)):
                for other in reversed(others):
                    ahead, s, per, val = jobs[other]
                    if order.index(other) % 2 == mine % 2 and doing(n - back)[ahead + 1]:
                        pe.wait_ge(s, (n - back + ahead) * per + val)
                        return

        def heads(c):
            half, par = c // KC // 2, c // KC % 2
            return half, par, [(g, 8 * half + 2 * g + par, ((2 * g + par) * KT + half)) for g in range(4)]

        block = ctx.enter_context(nc.Block())

        @block.sync
        def _(sp):
            passed = sem("sp_passed")

            def step(n, parity):
                _, _, do_m, do_l = doing(n)
                m, l = n + 1, n + 2
                if cross and do_l:
                    if not known(l, 0):
                        sp.wait_ge(cx_ps, l)
                        alone(sp, passed)
                    sp.dma_start(cx[:, :], d["ctx"][bass.ds(l, 1), :, :].rearrange("b s c -> (b s) c")
                                 ).then_inc(cx_dma, 16)
                if not do_m:
                    return
                if sigmoid and not known(m, 0):
                    sp.wait_ge(sT_ps, n * NC + 1)
                    alone(sp, passed)
                elif not known(m, 0, 1):
                    sp.wait_ge(sT_ps, n * NC)
                    alone(sp, passed)
                for which, stack in (("q", qstack), ("k", kstack)):
                    sp.wait_ge(parts_ok[which], m + 1)
                    for r, pair in enumerate(PAIRS):
                        src = parts[which][1 - parity][pair[0 if which == "q" else 1]]
                        dst = stack[1 - parity][r * HD:(r + 1) * HD, 0:H * width[which]]
                        sp.dma_start(dst.rearrange("c (h x) -> c h x", h=HH), src[:, :]).then_inc(stack_dma[which], 16)
                if not sigmoid:
                    sp.wait_ge(nT_ok, m + 1)
                    dst = qstack[1 - parity][STACK:STACK_M, :].rearrange("c (h x) -> c h x", h=H)
                    sp.dma_start(dst, nT[:, :]).then_inc(n_dma, 16)

            over_batches_ahead(sp, step)

        @block.gpsimd
        def _(pool):
            norm_factors(pool, pool_own, t, {"self": EPS_LN, "cross": None, "sigmoid": EPS_RMS}[kind], factors_ok)

            def step(n, parity):
                _, do_n, _, do_l = doing(n)
                l = n + 2
                own = [0]

                def link(i):
                    own[0] += 1
                    i.then_inc(rope_own, 1)
                    pool.wait_ge(rope_own, l * 4 + own[0])

                if do_n and kind != "self":
                    pool.wait_ge(z_ok, n + 1)
                    bias = t["bc_x_o" if cross else "bc_l_o"]
                    for tt in range(TT):
                        x_t = t["x"][:, tile_at(n, tt)]
                        i = pool.tensor_tensor(x_t, x_t, bias[:, :], ALU.add)
                    i.then_inc(bo_ok, 1)
                if not do_l:
                    return
                if sigmoid:
                    for j, which in enumerate("qk"):
                        pool.wait_ge(tok_ok, 2 * l + j + 1)
                        if not known(l, 0):
                            pool.wait_ge(proj_ps[which], l)
                        pair = lambda a: a[:, :].rearrange("p (x two h) -> p x two h", two=2, h=HH)
                        link(pool.tensor_tensor(tok_cos[j][:, :], tok[j][:, :], t["cos"][:, :], ALU.mult))
                        pool.tensor_tensor(pair(tok_sin[j])[:, :, 0], pair(tok[j])[:, :, 1], pair(t["sin"])[:, :, 0], ALU.mult)
                        link(pool.tensor_tensor(pair(tok_sin[j])[:, :, 1], pair(tok[j])[:, :, 0], pair(t["sin"])[:, :, 1], ALU.mult))
                        i = pool.tensor_tensor(tok_rot[j][:, :], tok_cos[j][:, :], tok_sin[j][:, :], ALU.add)
                        i.then_inc(rot_ok, 1)
                for which in "qk":
                    pool.wait_ge(second_ok[which], l + 1)
                    p3 = parts[which][parity]
                    pool.tensor_tensor(p3[2][:, :], rest[which][:, :], p3[1][:, :], ALU.subtract).then_inc(parts_ok[which], 1)

            over_batches_ahead(pool, step)

        @block.scalar
        def _(act):
            def exp(n, c):
                g = n * NC + c
                act.wait_ge(sT_ps, g + 1)
                if not (known(n, 0) and c < 2):
                    act.wait_ge(pv_ps, g - 1)
                func = ACT.Sigmoid if sigmoid else ACT.Exp
                act.activation(probs[c % 2][0:KP, :], sT[c % 2][0:KP, :], func, scale=HD ** -0.5).then_inc(p_ok, 1)

            def transposed_rows(l):
                act.wait_ge(zT_ps, l + 1)
                if not known(l, 0):
                    act.wait_ge(v_ps, l)
                act.activation(zT[:, :, :].rearrange("p k s -> p (k s)"), bank("z")[:, :], ACT.Identity).then_inc(zT_ok, 1)

            def transposed_context(l):
                act.wait_ge(cx_ps, l + 1)
                if not known(l, 0):
                    act.wait_ge(v_ps, l)
                act.activation(cxT[:, 0, :], bank("cx")[:, 0:SC], ACT.Identity)
                act.activation(cxT[0:C - P, 1, :], bank("cx")[0:C - P, SC:2 * SC], ACT.Identity).then_inc(cx_ok, 1)

            def first_part(l, parity, which):
                act.wait_ge(proj_ps[which], l + 1)
                if not known(l, 0, 1):
                    act.wait_ge(stack_dma[which], (l - 1) * STACKED)
                w = width[which]
                dst = parts[which][parity][0]
                if sigmoid:
                    i = act.activation(dst[:, :], bank(which)[:, 0:KT * w], ACT.Identity)
                else:
                    col = t[("col_x_b" if cross else "col_in_") + which]
                    for j in range(KT):
                        i = act.activation(dst[:, j * w:(j + 1) * w], bank(which)[:, j * w:(j + 1) * w], ACT.Identity,
                                           bias=col[:, j:j + 1])
                i.then_inc(first_ok[which], 1)

            def second_part(l, parity, which):
                act.wait_ge(rest_ok[which], l + 1)
                act.activation(parts[which][parity][1][:, :], rest[which][:, :], ACT.Identity).then_inc(second_ok[which], 1)

            def maxima_rows(m):
                act.wait_ge(nT_ps, m + 1)
                if not known(m, 0):
                    act.wait_ge(n_dma, 16 * m)
                act.activation(nT[:, :], bank("nT")[0:BF_PARTS * H, 0:S // 2].bitcast(BF16), ACT.Identity).then_inc(nT_ok, 1)

            if sigmoid:
                plan = {0: ["z"], 5: ["q first"], 6: ["k first", "q second"], 7: ["k second"]}
            elif cross:
                plan = {0: ["z", "cx"], 1: ["q first", "k first"], 2: ["q second", "k second"], 3: ["nT"]}
            else:
                plan = {0: ["z"], 1: ["q first"], 2: ["k first", "q second"], 3: ["k second"], 7: ["nT"]}

            def step(n, parity):
                _, do_n, do_m, do_l = doing(n)
                m, l = n + 1, n + 2
                for c in range(NC):
                    if do_n:
                        exp(n, c)
                    for job in plan.get(c, []):
                        if job == "nT":
                            if do_m:
                                maxima_rows(m)
                        elif not do_l:
                            continue
                        elif job == "z":
                            transposed_rows(l)
                        elif job == "cx":
                            transposed_context(l)
                        elif job.endswith("first"):
                            first_part(l, parity, job[0])
                        else:
                            second_part(l, parity, job[0])

            over_batches_ahead(act, step)

        @block.vector
        def _(dve):
            passed = sem("dve_passed")

            def rows(l):
                if known(l, 0):
                    dve.wait_ge(factors_ok, 1)
                else:
                    dve.wait_ge(zT_ps, l)
                normalise_rows(dve, t, z, l, 2 if kind == "self" else 0).then_inc(z_ok, 1)

            def token_major(l, j):
                dve.wait_ge(tokq_ps if j == 0 else tokk_ps, l + 1)
                if not known(l, 0):
                    dve.wait_ge(proj_ps["qk"[j]], l)
                for tt in range(TT):
                    i = dve.scalar_tensor_tensor(tok[j][:, tt * D:(tt + 1) * D], bank("tokq" if j == 0 else "tokk")[:, tt * D:(tt + 1) * D],
                                                 t["factors"][:, 1, bass.ds(l * TT + tt, 1)],
                                                 t["bc_l_q" if j == 0 else "bc_l_k"][:, :], ALU.mult, ALU.add)
                i.then_inc(tok_ok, 1)

            def values(m, parity):
                dve.wait_ge(v_ps, m + 1)
                if not known(m, 0, 1):
                    dve.wait_ge(pv_ps, (m - 1) * NC)
                bias = t["bc_x_v" if cross else "bc_l_v" if sigmoid else "bc_in_v"]
                for k in range(KC):
                    src = bank("v")[0:KP, k * D:(k + 1) * D].rearrange("p (x two c) -> p x two c", two=2, c=HD)
                    b = bias[0:KP, :].rearrange("p (x two c) -> p x two c", two=2, c=HD)
                    for par in range(2):
                        dst = v[parity][0:KP, k, :, par * 48:par * 48 + HD]
                        i = dve.tensor_tensor(dst, src[:, :, par, :], b[:, :, par, :], ALU.add)
                i.then_inc(v_ok, 1)

            def left_over(l, parity, which):
                dve.wait_ge(first_ok[which], l + 1)
                if not known(l, 0):
                    dve.wait_ge(parts_ok[which], l)
                w = width[which]
                first = parts[which][parity][0]
                if sigmoid:
                    i = dve.tensor_tensor(rest[which][:, :], bank(which)[:, 0:KT * w], first[:, :], ALU.subtract)
                else:
                    col = t[("col_x_b" if cross else "col_in_") + which]
                    for j in range(KT):
                        i = dve.scalar_tensor_tensor(rest[which][:, j * w:(j + 1) * w], bank(which)[:, j * w:(j + 1) * w],
                                                     col[:, j:j + 1], first[:, j * w:(j + 1) * w], ALU.add, ALU.subtract)
                i.then_inc(rest_ok[which], 1)

            def maxima(m, i):
                dve.wait_ge(s_ps, m * NS + i + 1)
                tt, h0 = i // (NS // TT), i % (NS // TT) * HB
                dve.tensor_reduce(nmax[:, tt, h0:h0 + HB], bank(("s", i))[:, 0:HB * SK].rearrange("p (h k) -> p h k", h=HB),
                                  AX_X, ALU.max, negate=True).then_inc(max_ok, 1)

            def max_parts(m):
                own = [0]

                def link(i):
                    own[0] += 1
                    i.then_inc(parts_own, 1)
                    dve.wait_ge(parts_own, m * 3 + own[0])

                dve.wait_ge(max_ok, (m + 1) * NS)
                if not known(m, 0):
                    dve.wait_ge(nT_ps, m)
                link(dve.tensor_copy(nparts[:, :, 0, :], nmax[:, :, :]))
                link(dve.tensor_tensor(nrest[:, :, :], nmax[:, :, :], nparts[:, :, 0, :], ALU.subtract))
                link(dve.tensor_copy(nparts[:, :, 1, :], nrest[:, :, :]))
                dve.tensor_tensor(nparts[:, :, 2, :], nrest[:, :, :], nparts[:, :, 1, :], ALU.subtract).then_inc(n_ok, 1)

            def normalise(n, half):
                per = 2 if sigmoid else 1
                own = [0]

                def link(i):
                    own[0] += 1
                    i.then_inc(main_own, 1)
                    dve.wait_ge(main_own, n * 2 * per + half * per + own[0])

                dve.wait_ge(pv_ps, n * NC + (half + 1) * NC // 2)
                if not known(n, 0):
                    dve.wait_ge(out_ps, n)
                src = od[half][:, 1, :]
                if sigmoid:
                    link(dve.tensor_scalar(dsum[:, half], src, EPS_RENORM, None, ALU.add))
                    src = dsum[:, half]
                link(dve.reciprocal(rden[:, half], src))
                dve.tensor_tensor(attnT[:, half, :], od[half][:, 0, :], rden[:, half], ALU.mult).then_inc(attn_ok, 1)

            def residual(n):
                dve.wait_ge(out_ps, n + 1)
                if kind != "self":
                    dve.wait_ge(bo_ok, n + 1)
                x_n = t["x"][:, at(n)]
                dve.tensor_tensor(x_n, od[0][:, :, :].rearrange("p a s -> p (a s)"), x_n, ALU.add).then_inc(res_ok, 1)

            def stats(n):
                own = [0]

                def link(i):
                    own[0] += 1
                    i.then_inc(stats_own, 1)
                    dve.wait_ge(stats_own, n * 3 + own[0])

                dve.wait_ge(res_ok, n + 1)
                link(tile_stats(dve, passed, link, t["x"], n, st, t["mv"]))

            def step(n, parity):
                late, do_n, do_m, do_l = doing(n)
                m, l = n + 1, n + 2
                if do_l:
                    rows(l)
                if late:
                    residual(n - 1)
                if do_m:
                    values(m, 1 - parity)
                if do_l and sigmoid:
                    token_major(l, 0)
                    token_major(l, 1)
                if do_l and not sigmoid:
                    left_over(l, parity, "q")
                    left_over(l, parity, "k")
                if late:
                    stats(n - 1)
                if do_m and not sigmoid:
                    for i in range(NS // 2):
                        maxima(m, i)
                if do_n:
                    normalise(n, 0)
                if do_l and sigmoid:
                    left_over(l, parity, "q")
                    left_over(l, parity, "k")
                if do_m and not sigmoid:
                    for i in range(NS // 2, NS):
                        maxima(m, i)
                    max_parts(m)
                if do_n:
                    normalise(n, 1)

            over_batches_ahead(dve, step)

        @block.tensor
        def _(pe):
            passed = sem("pe_passed")
            ident = t["ident"]

            def prepare(job, n, parity):
                m, l = n + 1, n + 2
                if job == "z":
                    pe.wait_ge(z_ok, l + 1)
                    bank_free(pe, job, n)
                    for k in range(KT):
                        for tt in range(TT):
                            i = pe.transpose(bank("z")[:, k * S + tt * P:k * S + (tt + 1) * P],
                                             z[:, tt * D + k * P:tt * D + (k + 1) * P], ident[:, :])
                    i.then_inc(zT_ps, 1)
                elif job == "cx":
                    pe.wait_ge(cx_dma, 16 * (l + 1))
                    bank_free(pe, job, n)
                    pe.transpose(bank("cx")[:, 0:SC], cx[:, 0:P], ident[0:SC, 0:SC])
                    pe.transpose(bank("cx")[0:C - P, SC:2 * SC], cx[:, P:C], ident[0:SC, 0:SC]).then_inc(cx_ps, 1)
                elif job in ("q", "k") and sigmoid:
                    j = 0 if job == "q" else 1
                    pe.wait_ge(rot_ok, 2 * l + j + 1)
                    bank_free(pe, job, n)
                    for k in range(KT):
                        for tt in range(TT):
                            i = pe.transpose(bank(job)[:, k * S + tt * P:k * S + (tt + 1) * P],
                                             tok_rot[j][:, tt * D + k * P:tt * D + (k + 1) * P], ident[:, :])
                    i.then_inc(proj_ps[job], 1)
                elif job in ("q", "k"):
                    w, wd = WQ if job == "q" else WK, width[job]
                    pe.wait_ge(zT_ok, l + 1)
                    if cross and job == "k":
                        pe.wait_ge(cx_ok, l + 1)
                    bank_free(pe, job, n)
                    for mt in range(KT):
                        for k in range(KT):
                            src, kp = (cxT, (P, C - P)[k]) if cross and job == "k" else (zT, P)
                            i = pe.matmul(bank(job)[:, mt * wd:(mt + 1) * wd], t["wT"][0:kp, w, k, mt * P:(mt + 1) * P],
                                          src[0:kp, k, :], start=(k == 0), stop=(k == KT - 1))
                    i.then_inc(proj_ps[job], 1)
                elif job in ("tokq", "tokk", "v"):
                    w = {"tokq": WQ, "tokk": WK, "v": WV}[job]
                    pe.wait_ge(cx_ok if cross else zT_ok, (m if job == "v" else l) + 1)
                    bank_free(pe, job, n)
                    for tt in range(KC):
                        for k in range(KT):
                            src, kp = (cxT, (P, C - P)[k]) if cross else (zT, P)
                            i = pe.matmul(bank(job)[0:KP, tt * D:(tt + 1) * D], src[0:kp, k, tt * P:tt * P + KP],
                                          t["wT"][0:kp, w, k, :], start=(k == 0), stop=(k == KT - 1))
                    i.then_inc({"tokq": tokq_ps, "tokk": tokk_ps, "v": v_ps}[job], 1)
                elif job == "nT":
                    pe.wait_ge(n_ok, m + 1)
                    bank_free(pe, job, n)
                    alone(pe, passed)
                    for tt in range(TT):
                        i = pe.transpose(bank("nT")[0:BF_PARTS * H, tt * P // 2:(tt + 1) * P // 2].bitcast(BF16),
                                         nparts[:, tt, :, :].rearrange("p a h -> p (a h)"), t["ident_bf"][:, :])
                    i.then_inc(nT_ps, 1)
                else:
                    i0 = job[1]
                    if i0 == 0:
                        pe.wait_ge(stack_dma["q"], (m + 1) * STACKED)
                        pe.wait_ge(stack_dma["k"], (m + 1) * STACKED)
                    bank_free(pe, job, n)
                    tt, h0 = i0 // (NS // TT), i0 % (NS // TT) * HB
                    for j in range(HB):
                        i = pe.matmul(bank(job)[:, j * SK:(j + 1) * SK],
                                      qstack[1 - parity][0:STACK, (h0 + j) * S + tt * P:(h0 + j) * S + (tt + 1) * P],
                                      kstack[1 - parity][0:STACK, (h0 + j) * SK:(h0 + j + 1) * SK], start=True, stop=True)
                    i.then_inc(s_ps, 1)

            def scores(n, c, parity):
                if not (known(n, 0) and c < 2):
                    pe.wait_ge(p_ok, n * NC + c - 1)
                kt = c % KC
                for j, (_, _, col) in enumerate(heads(c)[2]):
                    i = pe.matmul(sT[c % 2][0:KP, j * S:(j + 1) * S],
                                  kstack[parity][0:RQ, col * SK + kt * KP:col * SK + (kt + 1) * KP],
                                  qstack[parity][0:RQ, col * S:(col + 1) * S], start=True, stop=True)
                i.then_inc(sT_ps, 1)

            def times_values(n, c, parity):
                half, par, hs = heads(c)
                if c == 0 and not known(n, 0):
                    pe.wait_ge(res_ok, n)
                pe.wait_ge(p_ok, n * NC + c + 1)
                kt = c % KC
                first = c % (NC // 2) == 0
                last = c % (NC // 2) == NC // 2 - 1
                for which in range(2):
                    for j, (g, h, _) in enumerate(hs):
                        lhs = v[parity][0:KP, kt, h // 2, par * 32:(par + 1) * 32] if which == 0 else t["head_ones"][0:KP, par, :]
                        i = pe.matmul(od[half][32 * g:32 * (g + 1), which, :], lhs, probs[c % 2][0:KP, j * S:(j + 1) * S],
                                      start=(first and which == 0), stop=last, skip_group_check=True)
                i.then_inc(pv_ps, 1)

            def project(n):
                pe.wait_ge(attn_ok, TT * (n + 1))
                for tt in range(TT):
                    for k in range(KT):
                        i = pe.matmul(od[0][:, tt, :], attnT[:, k, tt * P:(tt + 1) * P], t["wT"][:, WO, k, :],
                                      start=(k == 0), stop=(k == KT - 1))
                i.then_inc(out_ps, 1)

            def group(*numbers):
                return [("s", i) for i in numbers]

            if sigmoid:
                plan = {0: (["v", "z"], []), 1: (["tokq"], ["tokk"]), 5: (["q"], []), 6: (["k"], [])}
            elif cross:
                plan = {0: (["v", "z", "cx"], []), 1: (["q"], ["k"]), 2: (group(0, 1), group(2, 3)),
                        3: (group(4, 5), group(6, 7)), 4: ([], ["nT"])}
            else:
                plan = {0: (["v", "z"], []), 1: (["q"], ["k"]), 3: (group(0, 1), group(2, 3)),
                        4: (group(4, 5), group(6, 7)), 5: (group(8, 9), group(10, 11)),
                        6: (group(12, 13), group(14, 15)), 7: ([], ["nT"])}
            planned = [job for c in range(NC + 1) for jj in plan.get(c, ((), ())) for job in jj]
            assert planned == order, (planned, order)

            def step(n, parity):
                late, do_n, do_m, do_l = doing(n)

                def prepare_group(c, which):
                    for job in plan.get(c, ((), ()))[which]:
                        if (do_m, do_l)[jobs[job][0] - 1]:
                            prepare(job, n, parity)

                if do_n:
                    pe.wait_ge(stack_dma["q"], (n + 1) * STACKED)
                    pe.wait_ge(stack_dma["k"], (n + 1) * STACKED)
                    pe.wait_ge(v_ok, n + 1)
                    if not sigmoid:
                        pe.wait_ge(n_dma, 16 * (n + 1))
                for c in range(NC + 1):
                    if do_n and c < NC:
                        scores(n, c, parity)
                    if c == 0 and late:
                        project(n - 1)
                    prepare_group(c, 0)
                    if do_n and c >= 1:
                        times_values(n, c - 1, parity)
                    prepare_group(c, 1)

            over_batches_ahead(pe, step)


def linear_stage(nc, t, d):
    with ExitStack() as ctx:
        stage_sems = ctx.enter_context(StageSemaphores(nc))
        sem = lambda name: stage_sems.new("ffn_" + name)
        sb = lambda name, shape, dt: ctx.enter_context(nc.sbuf_tensor("ffn_" + name, shape, dt))
        st = sb("st", [P, TT, 8], F32)
        z = [sb(f"z{i}", [P, TT * D], F32) for i in range(2)]
        zT = [sb(f"zT{i}", [P, KT * S], F32) for i in range(2)]
        zT_bank = [ctx.enter_context(nc.psum_tensor(f"ffn_zT_bank{i}", [P, 512], F32)) for i in range(2)]
        out_bank = [ctx.enter_context(nc.psum_tensor(f"ffn_out_bank{i}", [P, 512], F32)) for i in range(2)]
        factors_ok, pool_own, z_ok, zT_ps, zT_ok, out_ps, res_ok, bo_ok, dve_own = map(
            sem, ("factors_ok", "pool_own", "z_ok", "zT_ps", "zT_ok", "out_ps", "res_ok", "bo_ok", "dve_own"))
        block = ctx.enter_context(nc.Block())

        @block.vector
        def _(dve):
            passed = sem("dve_passed")
            def step(n, parity, main, pre):
                m = n + 1
                own = [0]

                def link(i):
                    own[0] += 1
                    i.then_inc(dve_own, 1)
                    dve.wait_ge(dve_own, n * 3 + own[0])

                if pre:
                    if known(m, 0):
                        dve.wait_ge(factors_ok, 1)
                    if not known(m, 0, 1):
                        dve.wait_ge(zT_ps, m - 1)
                    normalise_rows(dve, t, z[1 - parity], m).then_inc(z_ok, 1)
                if main:
                    dve.wait_ge(out_ps, n + 1)
                    dve.wait_ge(bo_ok, n + 1)
                    x_n = t["x"][:, at(n)]
                    i = dve.tensor_tensor(x_n, out_bank[parity][:, :], x_n, ALU.add)
                    i.then_inc(res_ok, 1)
                    dve.wait_ge(res_ok, n + 1)
                    link(tile_stats(dve, passed, link, t["x"], n, st, t["mv"]))

            over_batches(dve, step)

        @block.gpsimd
        def _(pool):
            passed = sem("pool_passed")
            norm_factors(pool, pool_own, t, None, factors_ok)

            def step(n, parity, main, pre):
                if main:
                    pool.wait_ge(z_ok, n + 1)
                    for tt in range(TT):
                        x_t = t["x"][:, tile_at(n, tt)]
                        i = pool.tensor_tensor(x_t, x_t, t["bc_ffn"][:, :], ALU.add)
                    i.then_inc(bo_ok, 1)

            over_batches(pool, step)

        @block.scalar
        def _(act):
            def step(n, parity, main, pre):
                m = n + 1
                if pre:
                    act.wait_ge(zT_ps, m + 1)
                    if not known(m, 0, 1):
                        act.wait_ge(out_ps, m - 1)
                    act.activation(zT[1 - parity][:, :], zT_bank[1 - parity][:, :], ACT.Identity).then_inc(zT_ok, 1)

            over_batches(act, step)

        @block.tensor
        def _(pe):
            passed = sem("pe_passed")
            def step(n, parity, main, pre):
                m = n + 1
                if pre:
                    pe.wait_ge(z_ok, m + 1)
                    if not known(m, 0, 1):
                        pe.wait_ge(zT_ok, m - 1)
                    for k in range(KT):
                        for tt in range(TT):
                            i = pe.transpose(zT_bank[1 - parity][:, k * S + tt * P:k * S + (tt + 1) * P],
                                             z[1 - parity][:, tt * D + k * P:tt * D + (k + 1) * P], t["ident"][:, :])
                    i.then_inc(zT_ps, 1)
                if main:
                    pe.wait_ge(zT_ok, n + 1)
                    if not known(n, 0, 1):
                        pe.wait_ge(res_ok, n - 1)
                    for tt in range(TT):
                        for k in range(KT):
                            i = pe.matmul(out_bank[parity][:, tt * D:(tt + 1) * D],
                                          zT[parity][:, k * S + tt * P:k * S + (tt + 1) * P], t["ffn"][:, k, :],
                                          start=(k == 0), stop=(k == KT - 1))
                    i.then_inc(out_ps, 1)

            over_batches(pe, step)


def single_head_stage(nc, t, d):
    SCALE = D ** -0.5
    with ExitStack() as ctx:
        stage_sems = ctx.enter_context(StageSemaphores(nc))
        sem = lambda name: stage_sems.new("one_" + name)
        sb = lambda name, shape, dt: ctx.enter_context(nc.sbuf_tensor("one_" + name, shape, dt))
        st = sb("st", [P, TT, 8], F32)
        z = sb("z", [P, TT * D], F32)
        zT = sb("zT", [P, KT, S], F32)
        cx = sb("cx", [SC, C], F32)
        cxT = sb("cxT", [P, 2, SC], F32)
        qT = [sb(f"qT{i}", [P, KT, S], F32) for i in range(2)]
        kT = [sb(f"kT{i}", [P, KT, SC], F32) for i in range(2)]
        v = [sb(f"v{i}", [SC, D], F32) for i in range(2)]
        nmax = sb("nmax", [P, TT], F32)
        nbias = sb("nbias", [P, TT], F32)
        probs = sb("probs", [P, TT, SC], F32)
        sums = sb("sums", [P, TT], F32)
        rden = sb("rden", [P, TT], F32)
        pT = sb("pT", [SC, S], F32)
        pre_bank = [ctx.enter_context(nc.psum_tensor(f"one_pre{i}", [P, 512], F32)) for i in range(2)]
        s_bank = ctx.enter_context(nc.psum_tensor("one_s_bank", [P, 512], F32))
        pT_bank = ctx.enter_context(nc.psum_tensor("one_pT_bank", [P, 512], F32))
        out_bank = ctx.enter_context(nc.psum_tensor("one_out_bank", [P, 512], F32))
        factors_ok, pool_own = map(sem, ("factors_ok", "pool_own"))
        (z_ok, dve_own, main_own, zT_ps, zT_ok, cx_dma, cx_ps, cx_ok, q_ps, q_ok, k_ps, k_ok, v_ps, v_ok, s_ps,
         max_ok, exp_ok, pT_ps, pT_ok, out_ps, res_ok) = map(sem, (
             "z_ok", "dve_own", "main_own", "zT_ps", "zT_ok", "cx_dma", "cx_ps", "cx_ok", "q_ps", "q_ok", "k_ps",
             "k_ok", "v_ps", "v_ok", "s_ps", "max_ok", "exp_ok", "pT_ps", "pT_ok", "out_ps", "res_ok"))
        block = ctx.enter_context(nc.Block())

        @block.sync
        def _(sp):
            passed = sem("sp_passed")
            def step(n, parity, main, pre):
                m = n + 1
                if pre:
                    if main:
                        sp.wait_ge(cx_ps, m)
                        alone(sp, passed)
                    sp.dma_start(cx[:, :], d["ctx"][bass.ds(m, 1), :, :].rearrange("b s c -> (b s) c")
                                 ).then_inc(cx_dma, 16)

            over_batches(sp, step)

        @block.gpsimd
        def _(pool):
            norm_factors(pool, pool_own, t, None, factors_ok)

        @block.vector
        def _(dve):
            passed = sem("dve_passed")
            def step(n, parity, main, pre):
                m = n + 1
                own = [0]

                def link(i):
                    own[0] += 1
                    i.then_inc(dve_own, 1)
                    dve.wait_ge(dve_own, n * 3 + own[0])

                if main:
                    dve.wait_ge(s_ps, n + 1)
                    i = dve.tensor_reduce(nmax[:, :], s_bank[:, 0:TT * SC].rearrange("p (t k) -> p t k", t=TT),
                                          AX_X, ALU.max, negate=True)
                    i.then_inc(main_own, 1)
                    dve.wait_ge(main_own, 2 * n + 1)
                    dve.tensor_scalar(nbias[:, :], nmax[:, :], SCALE, None, ALU.mult).then_inc(max_ok, 1)
                if pre:
                    if main:
                        dve.wait_ge(zT_ps, m)
                    else:
                        dve.wait_ge(factors_ok, 1)
                    normalise_rows(dve, t, z, m).then_inc(z_ok, 1)
                    dve.wait_ge(v_ps, m + 1)
                    if not known(m, 0, 1):
                        dve.wait_ge(out_ps, m - 1)
                    dve.tensor_tensor(v[1 - parity][:, :], pre_bank[0][0:SC, 0:D], t["bc_c_v"][0:SC, :],
                                      ALU.add).then_inc(v_ok, 1)
                if main:
                    dve.wait_ge(exp_ok, n + 1)
                    dve.reciprocal(rden[:, :], sums[:, :]).then_inc(main_own, 1)
                    dve.wait_ge(main_own, 2 * n + 2)
                    dve.wait_ge(out_ps, n + 1)
                    for tt in range(TT):
                        x_t = t["x"][:, tile_at(n, tt)]
                        i = dve.scalar_tensor_tensor(x_t, out_bank[:, tt * D:(tt + 1) * D], rden[:, tt:tt + 1], x_t,
                                                     ALU.mult, ALU.add)
                    i.then_inc(res_ok, 1)
                    dve.wait_ge(res_ok, n + 1)
                    link(tile_stats(dve, passed, link, t["x"], n, st, t["mv"]))

            over_batches(dve, step)

        @block.scalar
        def _(act):
            def step(n, parity, main, pre):
                m = n + 1
                if main:
                    act.wait_ge(max_ok, n + 1)
                    if not known(n, 0):
                        act.wait_ge(pT_ps, n)
                        act.wait_ge(res_ok, n)
                    for tt in range(TT):
                        i = act.activation(probs[:, tt, :], s_bank[:, tt * SC:(tt + 1) * SC], ACT.Exp,
                                           bias=nbias[:, tt:tt + 1], scale=SCALE, accum_out=sums[:, tt:tt + 1])
                    i.then_inc(exp_ok, 1)
                if pre:
                    act.wait_ge(zT_ps, m + 1)
                    if main:
                        act.wait_ge(q_ps, m)
                    act.activation(zT[:, :, :].rearrange("p k s -> p (k s)"), pre_bank[0][:, :], ACT.Identity).then_inc(zT_ok, 1)
                    act.wait_ge(cx_ps, m + 1)
                    if main:
                        act.wait_ge(v_ps, m)
                    act.activation(cxT[:, 0, :], pre_bank[1][:, 0:SC], ACT.Identity)
                    act.activation(cxT[0:C - P, 1, :], pre_bank[1][0:C - P, SC:2 * SC], ACT.Identity).then_inc(cx_ok, 1)
                    act.wait_ge(q_ps, m + 1)
                    if not known(m, 0, 1):
                        act.wait_ge(s_ps, m - 1)
                    for j in range(KT):
                        i = act.activation(qT[1 - parity][:, j, :], pre_bank[0][:, j * S:(j + 1) * S], ACT.Identity,
                                           bias=t["col_c_bq"][:, j:j + 1])
                    i.then_inc(q_ok, 1)
                    act.wait_ge(k_ps, m + 1)
                    for j in range(KT):
                        i = act.activation(kT[1 - parity][:, j, :], pre_bank[1][:, j * SC:(j + 1) * SC], ACT.Identity,
                                           bias=t["col_c_bk"][:, j:j + 1])
                    i.then_inc(k_ok, 1)
                if main:
                    act.wait_ge(pT_ps, n + 1)
                    if not known(n, 0):
                        act.wait_ge(out_ps, n)
                    act.activation(pT[:, :], pT_bank[0:SC, 0:S], ACT.Identity).then_inc(pT_ok, 1)

            over_batches(act, step)

        @block.tensor
        def _(pe):
            passed = sem("pe_passed")
            ident = t["ident"]

            def step(n, parity, main, pre):
                m, par = n + 1, 1 - parity
                if main:
                    pe.wait_ge(q_ok, n + 1)
                    pe.wait_ge(k_ok, n + 1)
                    if not known(n, 0):
                        pe.wait_ge(exp_ok, n)
                    for tt in range(TT):
                        for k in range(KT):
                            i = pe.matmul(s_bank[:, tt * SC:(tt + 1) * SC], qT[parity][:, k, tt * P:(tt + 1) * P],
                                          kT[parity][:, k, :], start=(k == 0), stop=(k == KT - 1))
                    i.then_inc(s_ps, 1)
                if pre:
                    pe.wait_ge(z_ok, m + 1)
                    if main:
                        pe.wait_ge(v_ok, m)
                    for k in range(KT):
                        for tt in range(TT):
                            i = pe.transpose(pre_bank[0][:, k * S + tt * P:k * S + (tt + 1) * P],
                                             z[:, tt * D + k * P:tt * D + (k + 1) * P], ident[:, :])
                    i.then_inc(zT_ps, 1)
                    pe.wait_ge(cx_dma, 16 * (m + 1))
                    if main:
                        pe.wait_ge(k_ok, m)
                    pe.transpose(pre_bank[1][:, 0:SC], cx[:, 0:P], ident[0:SC, 0:SC])
                    pe.transpose(pre_bank[1][0:C - P, SC:2 * SC], cx[:, P:C], ident[0:SC, 0:SC]).then_inc(cx_ps, 1)
                    pe.wait_ge(zT_ok, m + 1)
                    for j in range(KT):
                        for k in range(KT):
                            i = pe.matmul(pre_bank[0][:, j * S:(j + 1) * S], t["c_wq"][:, k, j * P:(j + 1) * P],
                                          zT[:, k, :], start=(k == 0), stop=(k == KT - 1))
                    i.then_inc(q_ps, 1)
                    pe.wait_ge(cx_ok, m + 1)
                    for j in range(KT):
                        for k, kp in ((0, P), (1, C - P)):
                            i = pe.matmul(pre_bank[1][:, j * SC:(j + 1) * SC], t["c_wk"][0:kp, k, j * P:(j + 1) * P],
                                          cxT[0:kp, k, :], start=(k == 0), stop=(k == 1))
                    i.then_inc(k_ps, 1)
                    pe.wait_ge(q_ok, m + 1)
                    for k, kp in ((0, P), (1, C - P)):
                        i = pe.matmul(pre_bank[0][0:SC, 0:D], cxT[0:kp, k, :], t["c_wv"][0:kp, k, :],
                                      start=(k == 0), stop=(k == 1))
                    i.then_inc(v_ps, 1)
                if main:
                    pe.wait_ge(exp_ok, n + 1)
                    if not known(n, 0):
                        pe.wait_ge(pT_ok, n)
                    for tt in range(TT):
                        i = pe.transpose(pT_bank[0:SC, tt * P:(tt + 1) * P], probs[:, tt, :], ident[:, :])
                    i.then_inc(pT_ps, 1)
                    pe.wait_ge(pT_ok, n + 1)
                    pe.wait_ge(v_ok, n + 1)
                    if not known(n, 0):
                        pe.wait_ge(res_ok, n)
                    for tt in range(TT):
                        i = pe.matmul(out_bank[:, tt * D:(tt + 1) * D], pT[:, tt * P:(tt + 1) * P], v[parity][:, :],
                                      start=True, stop=True)
                    i.then_inc(out_ps, 1)

            over_batches(pe, step)


def expert_stage(nc, t, d):
    RING = 4
    with ExitStack() as ctx:
        stage_sems = ctx.enter_context(StageSemaphores(nc))
        sem = lambda name: stage_sems.new("moe_" + name)
        sb = lambda name, shape, dt: ctx.enter_context(nc.sbuf_tensor("moe_" + name, shape, dt))
        st = sb("st", [P, TT, 8], F32)
        z = [sb(f"z{i}", [P, TT * D], F32) for i in range(2)]
        zT_all = sb("zT_all", [P, B * KT * S], F32)
        zT = [sb(f"zT{i}", [P, KT, P], F32) for i in range(RING)]
        col_sums = sb("col_sums", [P, B * KT * TT], F32)
        emb = sb("emb", [P, KT, B, TT], F32)
        work = sb("work", [CHUNKS, 8, NB], F32)
        one = sb("one", [CHUNKS, 8], F32)
        picked = sb("picked", [CHUNKS, 2], I32)
        picked_row = sb("picked_row", [1, 2 * CHUNKS], I32)
        experts = [sb(f"experts{i}", [P, 2, KT, D], F32) for i in range(RING)]
        zT_bank = [ctx.enter_context(nc.psum_tensor(f"moe_zT_bank{i}", [P, 512], F32)) for i in range(2)]
        out_bank = [ctx.enter_context(nc.psum_tensor(f"moe_out_bank{i}", [P, 512], F32)) for i in range(RING)]
        hash_bank = ctx.enter_context(nc.psum_tensor("moe_hash", [P, 512], F32))
        factors_ok, pool_own = map(sem, ("factors_ok", "pool_own"))
        (z_ok, dve_own, zT_ps, zT_ok, sum_ok, emb_ok, hash_ps, hash_own, picked_ok, picked_dma, w_dma0, w_dma1, w_dma2,
         w_dma3, zcopy_ok, out_ps, res_ok, store) = map(sem, (
             "z_ok", "dve_own", "zT_ps", "zT_ok", "sum_ok", "emb_ok", "hash_ps", "hash_own", "picked_ok", "picked_dma",
             "w_dma0", "w_dma1", "w_dma2", "w_dma3", "zcopy_ok", "out_ps", "res_ok", "store"))
        w_dma = [w_dma0, w_dma1, w_dma2, w_dma3]
        block = ctx.enter_context(nc.Block())

        def over_chunks(eng, step):
            for slot in range(RING):
                step(0, slot, slot)
            with eng.Fori(1, CHUNKS // RING) as i:
                for slot in range(RING):
                    step(i, i * RING + slot, slot)

        @block.sync
        def _(sp):
            sp.wait_ge(picked_ok, 1)
            sp.dma_start(picked_row[:, :], picked[:, :]).then_inc(picked_dma, 16)
            sp.wait_ge(picked_dma, 16)

            def step(i, c, slot):
                for j in range(2):
                    e = sp.value_load(picked_row[0:1, bass.ds(c * 2 + j, 1)], min_val=0, max_val=E_COUNT - 1)
                    if not known(i, 0) and j == 0:
                        sp.wait_ge(out_ps, c - RING + 1)
                    sp.dma_start(experts[slot][:, j, :, :],
                                 d["experts"][bass.ds(e, 1), :, :].rearrange("e (t p) f -> p (e t) f", p=P)
                                 ).then_inc(w_dma[slot], 16)

            over_chunks(sp, step)

        @block.gpsimd
        def _(pool):
            passed = sem("pool_passed")
            norm_factors(pool, pool_own, t, None, factors_ok)
            pool.wait_ge(zT_ok, B)

            def step(i, c, slot):
                if not known(i, 0):
                    pool.wait_ge(out_ps, c - RING + 1)
                base = i * (RING // TT * KT * S) + (slot // TT) * (KT * S) + (slot % TT) * P
                alone(pool, passed)
                for k in range(KT):
                    j = pool.tensor_copy(zT[slot][:, k, :], zT_all[:, bass.ds(base + k * S, P)])
                j.then_inc(zcopy_ok, 1)

            over_chunks(pool, step)

        @block.vector
        def _(dve):
            passed = sem("dve_passed")
            def step(n, parity, main, pre):
                m = n + 1
                if pre:
                    if known(m, 0):
                        dve.wait_ge(factors_ok, 1)
                    if not known(m, 0, 1):
                        dve.wait_ge(zT_ps, m - 1)
                    normalise_rows(dve, t, z[1 - parity], m).then_inc(z_ok, 1)
                if main:
                    dve.wait_ge(zT_ok, n + 1)
                    dve.tensor_reduce(col_sums[:, bass.ds(n * (KT * TT), KT * TT)],
                                      zT_all[:, bass.ds(n * (KT * S), KT * S)].rearrange("p (x s) -> p x s", s=P),
                                      AX_X, ALU.add).then_inc(sum_ok, 1)

            over_batches(dve, step)
            own = [0]

            def link(i):
                own[0] += 1
                i.then_inc(hash_own, 1)
                dve.wait_ge(hash_own, own[0])

            dve.wait_ge(sum_ok, B)
            sums = col_sums[:, :].rearrange("p (b k t) -> p k b t", k=KT, t=TT)
            for k in range(KT):
                i = dve.tensor_scalar(emb[:, k], sums[:, k], 1.0 / P, None, ALU.mult)
            i.then_inc(emb_ok, 1)
            W = lambda j: work[:, j, :]
            powers, proj, bits, weights, small_abs, tie, cand, flipped = map(W, range(8))
            for b in range(NB):
                i = dve.memset(work[:, 0, b:b + 1], float(2 ** b))
            link(i)
            dve.wait_ge(hash_ps, 1)
            link(dve.tensor_copy(proj, hash_bank[0:CHUNKS, 0:NB]))
            link(dve.tensor_scalar(bits, proj, 0.0, None, ALU.is_gt))
            link(dve.tensor_tensor(weights, bits, powers, ALU.mult))
            link(dve.tensor_reduce(one[:, 0:1], weights, AX_X, ALU.add))
            link(dve.scalar_tensor_tensor(small_abs, proj, -1.0, proj, ALU.mult, ALU.max))
            link(dve.tensor_reduce(one[:, 1:2], small_abs, AX_X, ALU.min))
            link(dve.tensor_scalar(tie, small_abs, one[:, 1:2], None, ALU.is_equal))
            link(dve.tensor_scalar(tie, tie, -float(2 ** NB), float(2 ** NB), ALU.mult, ALU.add))
            link(dve.tensor_tensor(cand, tie, powers, ALU.add))
            link(dve.tensor_reduce(one[:, 2:3], cand, AX_X, ALU.min))
            link(dve.tensor_scalar(flipped, powers, one[:, 2:3], None, ALU.is_equal))
            link(dve.tensor_tensor(flipped, flipped, weights, ALU.mult))
            link(dve.tensor_reduce(one[:, 3:4], flipped, AX_X, ALU.add))
            link(dve.tensor_tensor(one[:, 4:5], one[:, 0:1], one[:, 2:3], ALU.add))
            link(dve.tensor_scalar(one[:, 5:6], one[:, 3:4], -2.0, None, ALU.mult))
            link(dve.tensor_tensor(one[:, 6:7], one[:, 4:5], one[:, 5:6], ALU.add))
            dve.tensor_copy(picked[:, 0:1], one[:, 0:1])
            dve.tensor_copy(picked[:, 1:2], one[:, 6:7]).then_inc(picked_ok, 1)

            def chunk(i, c, slot):
                dve.wait_ge(out_ps, c + 1)
                x_c = t["x"][:, bass.ds(c * D, D)]
                dve.scalar_tensor_tensor(x_c, out_bank[slot][:, 0:D], 0.5, x_c, ALU.mult, ALU.add).then_inc(res_ok, 1)

            over_chunks(dve, chunk)

        @block.scalar
        def _(act):
            def step(n, parity, main, pre):
                m = n + 1
                if pre:
                    act.wait_ge(zT_ps, m + 1)
                    act.activation(zT_all[:, bass.ds(m * (KT * S), KT * S)], zT_bank[1 - parity][:, :],
                                   ACT.Identity).then_inc(zT_ok, 1)

            over_batches(act, step)

            def chunk(i, c, slot):
                act.wait_ge(res_ok, c + 1)
                seq = i * (RING // TT) + slot // TT
                act.dma_start(d["out"][bass.ds(seq, 1), (slot % TT) * P:(slot % TT + 1) * P, :].rearrange("b p f -> (b p) f"),
                              t["x"][:, bass.ds(c * D, D)]).then_inc(store, 16)

            over_chunks(act, chunk)
            act.wait_ge(store, 16 * CHUNKS)

        @block.tensor
        def _(pe):
            passed = sem("pe_passed")
            def step(n, parity, main, pre):
                m = n + 1
                if pre:
                    pe.wait_ge(z_ok, m + 1)
                    if not known(m, 0, 1):
                        pe.wait_ge(zT_ok, m - 1)
                    for k in range(KT):
                        for tt in range(TT):
                            i = pe.transpose(zT_bank[1 - parity][:, k * S + tt * P:k * S + (tt + 1) * P],
                                             z[1 - parity][:, tt * D + k * P:tt * D + (k + 1) * P], t["ident"][:, :])
                    i.then_inc(zT_ps, 1)

            over_batches(pe, step)
            pe.wait_ge(emb_ok, 1)
            for k in range(KT):
                i = pe.matmul(hash_bank[0:CHUNKS, 0:NB], emb[:, k].rearrange("p b t -> p (b t)"), t["hyper"][:, k, :],
                              start=(k == 0), stop=(k == KT - 1))
            i.then_inc(hash_ps, 1)

            def chunk(i, c, slot):
                pe.wait_ge(zcopy_ok, c + 1)
                pe.wait_ge(w_dma[slot], i * 32 + 32)
                if not known(i, 0):
                    pe.wait_ge(res_ok, c - RING + 1)
                for j in range(2):
                    for k in range(KT):
                        m = pe.matmul(out_bank[slot][:, 0:D], zT[slot][:, k, :], experts[slot][:, j, k, :],
                                      start=(j == 0 and k == 0), stop=(j == 1 and k == KT - 1))
                m.then_inc(out_ps, 1)

            over_chunks(pe, chunk)


def decoder_kernel(nc, d):
    with ExitStack() as ctx:
        def sb(name, shape, dt):
            return ctx.enter_context(nc.sbuf_tensor(name, shape, dt))

        t = {"x": sb("x_res", [P, CHUNKS * D], F32),
             "wT": sb("wT", [P, len(W_NAMES), KT, D], F32),
             "ident": sb("ident", [P, P], F32), "ident_bf": sb("ident_bf", [P, P], BF16),
             "ones": sb("ones", [P, P], F32), "head_ones": sb("head_ones", [P, 2, 32], F32),
             "minus_half": sb("minus_half", [P, CHUNKS], F32),
             "mv": sb("mv", [P, CHUNKS * 2], F32), "factors": sb("factors", [P, 4, CHUNKS], F32),
             "hyper": sb("hyper_w", [P, KT, NB], F32), "cos": sb("cos_t", [P, TT * D], F32), "sin": sb("sin_t", [P, TT * D], F32),
             "ffn": sb("ffn_m", [P, KT, D], F32),
             "v": [sb(f"v_heads{i}", [P, TT, H // 2, 64], F32) for i in range(2)],
             "qstack": [sb(f"qstack{i}", [STACK_M, H * S], BF16) for i in range(2)],
             "kstack": [sb(f"kstack{i}", [STACK_M, H * S], BF16) for i in range(2)]}
        for name in ("c_wq", "c_wk", "c_wv"):
            t[name] = sb(name + "_m", [P, KT, D], F32)
        for name in ("bc_in_v", "bc_x_v", "bc_l_q", "bc_l_k", "bc_l_v", "bc_c_v", "bc_x_o", "bc_l_o", "bc_ffn"):
            t[name] = sb(name, [P, D], F32)
        for name in ("row_x_bo", "row_l_bo", "row_ffn_bias"):
            t[name] = sb(name, [1, D], F32)
        for name in ("col_in_q", "col_in_k", "col_x_bq", "col_x_bk", "col_c_bq", "col_c_bk"):
            t[name] = sb(name, [P, KT], F32)
        setup_stage(nc, t, d)
        attention_stage(nc, t, d, "self")
        attention_stage(nc, t, d, "cross")
        linear_stage(nc, t, d)
        attention_stage(nc, t, d, "sigmoid")
        single_head_stage(nc, t, d)
        expert_stage(nc, t, d)


_INS = {
    "x": "x", "ctx": "ctx_768", "in_proj": "L0_attn_in_proj_w", "out_proj": "L0_attn_out_proj_w",
    "ln_gamma": "L0_attn_ln_gamma", "ln_beta": "L0_attn_ln_beta",
    "x_wq": "L0_xattn_wq", "x_bq": "L0_xattn_bq", "x_wk": "L0_xattn_wk", "x_bk": "L0_xattn_bk",
    "x_wv": "L0_xattn_wv", "x_bv": "L0_xattn_bv", "x_wo": "L0_xattn_wo", "x_bo": "L0_xattn_bo",
    "ffn_w": "L0_ffn_kernel", "ffn_bias": "L0_ffn_bias", "ffn_a": "L0_ffn_a", "ffn_b": "L0_ffn_b",
    "l_qw": "L1_attn_q_w", "l_bq": "L1_attn_q_b", "l_kw": "L1_attn_k_w", "l_bk": "L1_attn_k_b",
    "l_vw": "L1_attn_v_w", "l_bv": "L1_attn_v_b", "l_ow": "L1_attn_o_w", "l_bo": "L1_attn_o_b",
    "qn": "L1_attn_qn_scale", "kn": "L1_attn_kn_scale",
    "c_wq": "L1_xattn_Wq", "c_bq": "L1_xattn_bq", "c_wk": "L1_xattn_Wk", "c_bk": "L1_xattn_bk",
    "c_wv": "L1_xattn_Wv", "c_bv": "L1_xattn_bv",
    "experts": "L1_ffn_expert_weights", "hyper": "L1_ffn_hyperplanes",
}


def kernel(**inputs):
    import numpy as _np
    import concourse.bacc as _bacc
    from concourse import mybir as _mybir
    from concourse.bass_utils import run_bass_kernel_spmd as _run

    nc = _bacc.Bacc("TRN2", target_bir_lowering=False, num_devices=1)
    arrays = {key: _np.ascontiguousarray(inputs[name]) for key, name in _INS.items()}
    arrays["cos"], arrays["sin"] = rope_tables()
    arrays = {f"in_{key}": a for key, a in arrays.items()}
    d = {key[3:]: nc.dram_tensor(key, a.shape, _mybir.dt.from_np(a.dtype), kind="ExternalInput").ap()
         for key, a in arrays.items()}
    d["out"] = nc.dram_tensor("out_y", (B, S, D), _mybir.dt.float32, kind="ExternalOutput").ap()
    decoder_kernel(nc, d)
    r = _run(nc, [arrays], core_ids=[0])
    return r.results[0]["out_y"]
```

```python
from contextlib import ExitStack

import numpy as np

import concourse.bass as bass
from concourse import mybir

ALU = mybir.AluOpType
ACT = mybir.ActivationFunctionType
F32 = mybir.dt.float32
BF16 = mybir.dt.bfloat16
I32 = mybir.dt.int32
AX_X = mybir.AxisListType.X

P = 128
B = 16
S = 256
D = 256
H = 16
HD = D // H
TT = S // P
KT = D // P
SC = 120
C = 192
HH = P // HD
BF_PARTS = 3
PAIRS = [(0, 0), (0, 1), (1, 0), (0, 2), (2, 0), (1, 1)]
STACK = len(PAIRS) * HD
STACK_M = STACK + BF_PARTS
EPS_LN = 1e-5
EPS_RMS = 1e-8
EPS_RENORM = 1e-8
NB = 6
E_COUNT = 64
CHUNKS = B * TT
W_NAMES = ["in_q", "in_k", "in_v", "in_o", "x_q", "x_k", "x_v", "x_o", "l_q", "l_k", "l_v", "l_o"]


def rope_tables():
    inv = (1.0 / np.float32(10000.0) ** (np.arange(0, HD, 2, dtype=np.float32) / np.float32(HD))).astype(np.float32)
    freqs = np.arange(S, dtype=np.float32)[:, None] * inv[None, :]
    emb = np.concatenate([freqs, freqs], axis=-1)
    cos, sin = np.cos(emb).astype(np.float32), np.sin(emb).astype(np.float32)
    sin = sin * np.where(np.arange(HD) % 2 == 0, -1.0, 1.0).astype(np.float32)
    out = []
    for t in (cos, sin):
        t = t.reshape(TT, P, 1, HD, 1).transpose(1, 0, 2, 3, 4)
        out.append(np.ascontiguousarray(np.broadcast_to(t, (P, TT, KT, HD, HH)).reshape(P, TT * D)).astype(np.float32))
    return out


def over_batches(eng, step):
    step(-1, 1, False, True)
    step(0, 0, True, True)
    with eng.Fori(0, B // 2 - 1) as i:
        step(2 * i + 1, 1, True, True)
        step(2 * i + 2, 0, True, True)
    step(B - 1, 1, True, False)


def over_batches_ahead(eng, step):
    for n in range(-3, 1):
        step(n, n % 2)
    with eng.Fori(0, B // 2 - 2) as i:
        step(2 * i + 1, 1)
        step(2 * i + 2, 0)
    for n in range(B - 3, B + 1):
        step(n, n % 2)


def doing(n, ahead):
    return not isinstance(n, int) or 0 <= n + ahead < B


def alone(eng, passed):
    eng.sem_inc(passed, 1)


class StageSemaphores:

    def __init__(self, nc):
        self.nc, self.held = nc, []

    def __enter__(self):
        return self

    def new(self, name):
        self.held.append(self.nc.alloc_semaphore(name))
        return self.held[-1]

    def __exit__(self, *_):
        self.nc.clear_and_free_semaphores(self.held)
        self.nc.all_engine_barrier()


def known(n, *values):
    return isinstance(n, int) and n in values


def at(n):
    return bass.ds(n * (TT * D), TT * D)


def tile_at(n, tt):
    return bass.ds(n * (TT * D) + tt * D, D)


def tile_stats(dve, passed, link, x, n, st, mv):
    alone(dve, passed)
    for t in range(TT):
        i = dve.bn_stats(st[:, t, 0:6], x[:, tile_at(n, t)])
    link(i)
    alone(dve, passed)
    for t in range(TT):
        i = dve.bn_aggr(st[:, t, 6:8], st[:, t, 0:6])
    link(i)
    alone(dve, passed)
    return dve.tensor_copy(mv[:, bass.ds(n * (TT * 2), TT * 2)].rearrange("p (t two) -> p t two", two=2), st[:, :, 6:8])


def norm_factors(pool, own_sem, t, second_eps, factors_ok):
    own = [0]

    def link(i):
        own[0] += 1
        i.then_inc(own_sem, 1)
        pool.wait_ge(own_sem, own[0])

    for lo, hi in ((0, 2 * TT), (2 * TT, CHUNKS)):
        f = t["factors"][:, :, lo:hi]
        var = t["mv"][:, 2 * lo:2 * hi].rearrange("p (c two) -> p c two", two=2)[:, :, 1]
        half = t["minus_half"][:, lo:hi]
        link(pool.tensor_scalar(f[:, 3], var, EPS_LN, None, ALU.add))
        i = pool.tensor_tensor(f[:, 0], f[:, 3], half, ALU.pow)
        if second_eps is not None:
            link(i)
            link(pool.tensor_tensor(f[:, 1], var, f[:, 0], ALU.mult))
            link(pool.tensor_tensor(f[:, 3], f[:, 1], f[:, 0], ALU.mult))
            link(pool.tensor_scalar(f[:, 3], f[:, 3], second_eps, None, ALU.add))
            link(pool.tensor_tensor(f[:, 1], f[:, 3], half, ALU.pow))
            i = pool.tensor_tensor(f[:, 2], f[:, 1], f[:, 0], ALU.mult)
        i.then_inc(factors_ok, 1)


def normalise_rows(dve, t, z, n, which=0):
    for tt in range(TT):
        i = dve.tensor_scalar(z[:, tt * D:(tt + 1) * D], t["x"][:, tile_at(n, tt)],
                              t["mv"][:, bass.ds(n * (TT * 2) + tt * 2, 1)], t["factors"][:, which, bass.ds(n * TT + tt, 1)],
                              ALU.subtract, ALU.mult)
    return i


def setup_stage(nc, t, d):
    with ExitStack() as ctx:
        stage_sems = ctx.enter_context(StageSemaphores(nc))
        sem = lambda name: stage_sems.new(name)
        sb = lambda name, shape, dt: ctx.enter_context(nc.sbuf_tensor(name, shape, dt))
        raw = sb("raw", [P, len(W_NAMES), 2, D], F32)
        st = sb("st", [P, CHUNKS, 6], F32)
        rows = sb("rows", [1, 5, D], F32)
        cols = sb("cols", [P, 4, KT], F32)
        beta_bc = sb("beta_bc", [P, KT, P], F32)
        zeros = sb("zeros", [P, P], F32)
        ffn_w = sb("ffn_w", [P, KT, D], F32)
        lora_a = sb("lora_a", [P, 2, HD], F32)
        lora_b = sb("lora_b", [HD, D], F32)
        lora_aT = sb("lora_aT", [HD, KT, P], F32)
        amax = sb("amax", [P, 1], F32)
        amax_all = sb("amax_all", [P, 1], F32)
        step7 = sb("step7", [P, 1], F32)
        inv_step = sb("inv_step", [P, 1], F32)
        quant = sb("quant", [P, KT, D], F32)
        ps = [ctx.enter_context(nc.psum_tensor(f"setup_ps{i}", [P, 2, D], F32)) for i in range(4)]

        w_in = sem("w_in")
        x_in = sem("x_in")
        small_in = sem("small_in")
        ident0 = sem("ident0")
        ident_ok = sem("ident_ok")
        ones_ok = sem("ones_ok")
        w_ps = sem("w_ps")
        w_out = sem("w_out")
        w_out_act = sem("w_out_act")
        bcast_ps = sem("bcast_ps")
        bcast_out = sem("bcast_out")
        bias_ps = sem("bias_ps")
        bias_out = sem("bias_out")
        beta_ok = sem("beta_ok")
        scaled = sem("scaled")
        amax_ok = sem("amax_ok")
        amax_red = sem("amax_red")
        dve_own = sem("dve_own")
        aT_ps = sem("aT_ps")
        aT_ok = sem("aT_ok")
        ab_ps = sem("ab_ps")

        w_src = {"in_q": d["in_proj"][0:D], "in_k": d["in_proj"][D:2 * D], "in_v": d["in_proj"][2 * D:3 * D],
                 "in_o": d["out_proj"], "x_q": d["x_wq"], "x_k": d["x_wk"], "x_v": d["x_wv"], "x_o": d["x_wo"],
                 "l_q": d["l_qw"], "l_k": d["l_kw"], "l_v": d["l_vw"], "l_o": d["l_ow"]}
        block = ctx.enter_context(nc.Block())

        @block.sync
        def _(sp):
            for j, name in enumerate(W_NAMES):
                src = w_src[name]
                sp.dma_start(raw[:, j, :, 0:src.shape[1]], src.rearrange("(t p) f -> p t f", p=P)).then_inc(w_in, 16)
            for j, name in enumerate(("x_bv", "l_bq", "l_bk", "l_bv", "c_bv")):
                sp.dma_start(rows[0:1, j, :], d[name].rearrange("(a n) -> a n", a=1)).then_inc(small_in, 16)
            for name in ("x_bo", "l_bo", "ffn_bias"):
                sp.dma_start(t["row_" + name][0:1, :], d[name].rearrange("(a n) -> a n", a=1)).then_inc(small_in, 16)
            with nc.allow_non_contiguous_dma(reason="a vector of 256 spread over partitions"):
                for j, name in enumerate(("ln_gamma", "ln_beta", "qn", "kn")):
                    sp.dma_start(cols[:, j, :], d[name].rearrange("(t p) -> p t", p=P)).then_inc(small_in, 16)
                for name in ("x_bq", "x_bk"):
                    for m in range(KT):
                        sp.dma_start(t["col_" + name][:, m:m + 1],
                                      d[name].rearrange("(m h c) -> m c h", h=HH, c=HD)[m]).then_inc(small_in, 16)
                for name in ("c_bq", "c_bk"):
                    sp.dma_start(t["col_" + name][:, :], d[name].rearrange("(t p) -> p t", p=P)).then_inc(small_in, 16)
            sp.dma_start(ffn_w[:, :, :], d["ffn_w"].rearrange("(t p) f -> p t f", p=P)).then_inc(small_in, 16)
            sp.dma_start(lora_a[:, :, :], d["ffn_a"].rearrange("(t p) f -> p t f", p=P)).then_inc(small_in, 16)
            sp.dma_start(lora_b[:, :], d["ffn_b"]).then_inc(small_in, 16)
            sp.dma_start(t["hyper"][:, :, :], d["hyper"].rearrange("(t p) f -> p t f", p=P)).then_inc(small_in, 16)
            sp.dma_start(t["c_wq"][:, :, :], d["c_wq"].rearrange("(t p) f -> p t f", p=P)).then_inc(small_in, 16)
            for name in ("c_wk", "c_wv"):
                sp.dma_start(t[name][:, 0, :], d[name][0:P, :]).then_inc(small_in, 16)
                sp.dma_start(t[name][0:C - P, 1, :], d[name][P:C, :]).then_inc(small_in, 16)
            sp.dma_start(t["cos"][:, :], d["cos"]).then_inc(small_in, 16)
            sp.dma_start(t["sin"][:, :], d["sin"]).then_inc(small_in, 16)
            sp.wait_ge(x_in, 64)
            sp.wait_ge(small_in, 16 * 29)

        @block.scalar
        def _(act):
            act.wait_ge(w_in, 16 * len(W_NAMES))
            x_v = d["x"].rearrange("b (t p) f -> p (b t) f", p=P)
            for q in range(4):
                n = CHUNKS // 4
                act.dma_start(t["x"][:, q * n * D:(q + 1) * n * D].rearrange("p (c f) -> p c f", f=D),
                             x_v[:, q * n:(q + 1) * n, :]).then_inc(x_in, 16)
            for j, name in enumerate(W_NAMES):
                if name[-1] in "vo":
                    act.wait_ge(w_ps, j + 1)
                    for k, rows_k in enumerate((P, C - P if name == "x_v" else P)):
                        i = act.activation(t["wT"][0:rows_k, j, k, :], ps[j % 4][0:rows_k, k, :], ACT.Identity)
                    i.then_inc(w_out_act, 1)

        @block.gpsimd
        def _(pool):
            ident, ident_bf = t["ident"], t["ident_bf"]
            pool.memset(ident[:, :], 0.0).then_inc(ident0, 1)
            pool.memset(ident_bf[:, :], 0.0).then_inc(ident0, 1)
            pool.wait_ge(ident0, 2)
            for m in (ident, ident_bf):
                pool.affine_select(out=m[:, :], in_=m[:, :], compare_op=ALU.not_equal, fill=1.0, base=0,
                                   pattern=[[-1, P]], channel_multiplier=1).then_inc(ident_ok, 1)
            for i, (buf, value) in enumerate(((t["v"][0][:, :, :, :], 0.0), (t["v"][1][:, :, :, :], 0.0),
                                              (t["kstack"][0][STACK:STACK_M, :], 1.0), (t["kstack"][1][STACK:STACK_M, :], 1.0))):
                pool.wait_ge(ident_ok, 2 + i)
                pool.memset(buf, value).then_inc(ident_ok, 1)
            pool.wait_ge(ident_ok, 6)
            pool.wait_ge(amax_ok, 1)
            pool.partition_all_reduce(amax_all[:, :], amax[:, :], P, bass.bass_isa.ReduceOp.max).then_inc(amax_red, 1)

        @block.vector
        def _(dve):
            own = [0]

            def link(i):
                own[0] += 1
                i.then_inc(dve_own, 1)
                dve.wait_ge(dve_own, own[0])

            dve.memset(t["ones"][:, :], 1.0).then_inc(ones_ok, 1)
            dve.memset(zeros[:, :], 0.0)
            dve.memset(t["minus_half"][:, :], -0.5)
            link(dve.memset(t["head_ones"][:, :, :], 0.0))
            for par in range(2):
                link(dve.memset(t["head_ones"][:, par, par * HD:(par + 1) * HD], 1.0))
            for j, name in enumerate(W_NAMES):
                if name[-1] in "qk":
                    dve.wait_ge(w_ps, j + 1)
                    for k, rows_k in enumerate((P, C - P if name == "x_k" else P)):
                        out = t["wT"][0:rows_k, j, k, :].rearrange("p (m c h) -> p m h c", m=KT, c=HD)
                        in_ = ps[j % 4][0:rows_k, k, :].rearrange("p (m h c) -> p m h c", m=KT, c=HD)
                        for m in range(KT):
                            i = dve.tensor_copy(out[:, m], in_[:, m])
                    i.then_inc(w_out, 1)

            def x_stats(lo, hi):
                for c in range(lo, hi):
                    i = dve.bn_stats(st[:, c, :], t["x"][:, c * D:(c + 1) * D])
                own[0] += 1
                i.then_inc(dve_own, 1)

            dve.wait_ge(x_in, 16 * 4)
            x_stats(0, CHUNKS // 2)
            dve.wait_ge(small_in, 16 * 29)
            for k in range(KT):
                i = dve.tensor_scalar(beta_bc[:, k, :], zeros[:, :], cols[:, 1, k:k + 1], None, ALU.add)
            i.then_inc(beta_ok, 1)
            dve.wait_ge(bias_ps, 1)
            dve.tensor_copy(t["col_in_q"][:, :], ps[2][:, 0, 0:KT])
            dve.tensor_copy(t["col_in_k"][:, :], ps[2][:, 0, KT:2 * KT])
            dve.tensor_copy(t["bc_in_v"][:, :], ps[3][:, 0, :]).then_inc(bias_out, 1)
            dve.wait_ge(w_out, len(W_NAMES) // 2)
            dve.wait_ge(w_out_act, len(W_NAMES) // 2)
            for j, col in ((0, 0), (1, 0), (2, 0), (8, 2), (9, 3)):
                for k in range(KT):
                    dve.tensor_scalar(t["wT"][:, j, k, :], t["wT"][:, j, k, :], cols[:, col, k:k + 1], None,
                                      ALU.mult).then_inc(scaled, 1)
            for j, name in enumerate(("bc_x_v", "bc_l_q", "bc_l_k", "bc_l_v", "bc_c_v", "bc_x_o", "bc_l_o", "bc_ffn")):
                dve.wait_ge(bcast_ps, j + 1)
                out, in_ = t[name][:, :], ps[j % 2][:, 0, :]
                if name in ("bc_l_q", "bc_l_k"):
                    out = out.rearrange("p (m c h) -> p m h c", m=KT, c=HD)
                    in_ = in_.rearrange("p (m h c) -> p m h c", m=KT, c=HD)
                    for m in range(KT):
                        i = dve.tensor_copy(out[:, m], in_[:, m])
                else:
                    i = dve.tensor_copy(out, in_)
                i.then_inc(bcast_out, 1)
                x_stats(CHUNKS // 2 + 2 * j, CHUNKS // 2 + 2 * j + 2)
            dve.wait_ge(dve_own, own[0])
            for c in range(CHUNKS):
                dve.bn_aggr(t["mv"][:, 2 * c:2 * c + 2], st[:, c, :])
            dve.tensor_reduce(amax[:, :], ffn_w[:, :, :].rearrange("p t f -> p (t f)"), AX_X, ALU.max,
                              apply_absolute_value=True).then_inc(amax_ok, 1)
            dve.wait_ge(amax_red, 1)
            link(dve.tensor_scalar(step7[:, :], amax_all[:, :], 1.0 / 7.0, None, ALU.mult))
            link(dve.reciprocal(inv_step[:, :], step7[:, :]))
            link(dve.tensor_scalar(quant[:, :, :], ffn_w[:, :, :], inv_step[:, 0:1], None, ALU.mult))
            link(dve.tensor_scalar(quant[:, :, :], quant[:, :, :], 12582912.0, None, ALU.add))
            link(dve.tensor_scalar(quant[:, :, :], quant[:, :, :], 12582912.0, None, ALU.subtract))
            link(dve.tensor_scalar(quant[:, :, :], quant[:, :, :], -8.0, 7.0, ALU.max, ALU.min))
            link(dve.tensor_scalar(quant[:, :, :], quant[:, :, :], step7[:, 0:1], None, ALU.mult))
            dve.wait_ge(aT_ps, 1)
            dve.tensor_copy(lora_aT[:, :, :], ps[2][0:HD, 0, :].rearrange("p (k c) -> p k c", k=KT)).then_inc(aT_ok, 1)
            dve.wait_ge(ab_ps, 1)
            dve.tensor_tensor(t["ffn"][:, :, :], quant[:, :, :], ps[3][:, :, :], ALU.add)

        @block.tensor
        def _(pe):
            ident = t["ident"]
            pe.wait_ge(ident_ok, 2)
            for j, name in enumerate(W_NAMES):
                pe.wait_ge(w_in, 16 * len(W_NAMES))
                if j >= 4:
                    pe.wait_ge(w_out if name[-1] in "qk" else w_out_act, (j - 4) // 4 * 2 + j % 2 + 1)
                kk = [(0, P), (1, C - P)] if name in ("x_k", "x_v") else [(0, P), (1, P)]
                for k, rows_k in kk:
                    for e in range(2):
                        i = pe.transpose(ps[j % 4][0:rows_k, k, e * P:(e + 1) * P],
                                         raw[:, j, e, k * P:k * P + rows_k], ident[:, :])
                i.then_inc(w_ps, 1)
            pe.wait_ge(w_out, len(W_NAMES) // 2)
            pe.wait_ge(w_out_act, len(W_NAMES) // 2)
            pe.wait_ge(beta_ok, 1)
            for j in range(2):
                for m in range(KT):
                    for k in range(KT):
                        pe.matmul(ps[2][:, 0, j * KT + m:j * KT + m + 1], t["wT"][:, j, k, m * P:(m + 1) * P],
                                  cols[:, 1, k:k + 1], start=(k == 0), stop=(k == KT - 1))
            for k in range(KT):
                i = pe.matmul(ps[3][:, 0, :], beta_bc[:, k, :], t["wT"][:, 2, k, :], start=(k == 0), stop=(k == KT - 1))
            i.then_inc(bias_ps, 1)
            pe.wait_ge(small_in, 16 * 29)
            pe.wait_ge(ones_ok, 1)
            srcs = [rows[0:1, j, :] for j in range(5)] + [t["row_" + n][0:1, :] for n in ("x_bo", "l_bo", "ffn_bias")]
            for j, src in enumerate(srcs):
                if j >= 2:
                    pe.wait_ge(bcast_out, j - 1)
                pe.matmul(ps[j % 2][:, 0, :], t["ones"][0:1, :], src, start=True, stop=True).then_inc(bcast_ps, 1)
            pe.wait_ge(bias_out, 1)
            for k in range(KT):
                i = pe.transpose(ps[2][0:HD, 0, k * P:(k + 1) * P], lora_a[:, k, :], ident[:, :])
            i.then_inc(aT_ps, 1)
            pe.wait_ge(aT_ok, 1)
            for k in range(KT):
                i = pe.matmul(ps[3][:, k, :], lora_aT[:, k, :], lora_b[:, :], start=True, stop=True)
            i.then_inc(ab_ps, 1)


def attention_stage(nc, t, d, kind):
    cross, sigmoid = kind == "cross", kind == "sigmoid"
    SK = SC if cross else S
    KC = 1 if cross else TT
    KP = SC if cross else P
    NC = 4 * KC
    HB = 512 // SK
    NS = TT * H // HB
    RQ = STACK if sigmoid else STACK_M
    STACKED = 16 * len(PAIRS)
    WQ, WK, WV, WO = [{"self": 0, "cross": 4, "sigmoid": 8}[kind] + i for i in range(4)]
    with ExitStack() as ctx:
        pre = kind + "_"
        stage_sems = ctx.enter_context(StageSemaphores(nc))
        sem = lambda name: stage_sems.new(pre + name)
        sb = lambda name, shape, dt: ctx.enter_context(nc.sbuf_tensor(pre + name, shape, dt))
        st = sb("st", [P, TT, 8], F32)
        z = sb("z", [P, TT * D], F32)
        zT = sb("zT", [P, KT, S], F32)
        rest = {"q": sb("qrest", [P, KT * S], F32), "k": sb("krest", [P, KT * SK], F32)}
        parts = {"q": [[sb(f"qpart{p}{i}", [P, KT * S], BF16) for i in range(BF_PARTS)] for p in range(2)],
                 "k": [[sb(f"kpart{p}{i}", [P, KT * SK], BF16) for i in range(BF_PARTS)] for p in range(2)]}
        width = {"q": S, "k": SK}
        probs = [sb(f"probs{i}", [P, 4 * S], F32) for i in range(2)]
        rden = sb("rden", [P, 2, S], F32)
        attnT = sb("attnT", [P, KT, S], F32)
        qstack, kstack, v = t["qstack"], t["kstack"], t["v"]
        if cross:
            cx = sb("cx", [SC, C], F32)
            cxT = sb("cxT", [P, 2, SC], F32)
        if sigmoid:
            tok = [sb(f"tok{i}", [P, TT * D], F32) for i in range(2)]
            tok_cos = [sb(f"tok_cos{i}", [P, TT * D], F32) for i in range(2)]
            tok_sin = [sb(f"tok_sin{i}", [P, TT * D], F32) for i in range(2)]
            tok_rot = [sb(f"tok_rot{i}", [P, TT * D], F32) for i in range(2)]
            dsum = sb("dsum", [P, 2, S], F32)
        else:
            nmax = sb("nmax", [P, TT, H], F32)
            nrest = sb("nrest", [P, TT, H], F32)
            nparts = sb("nparts", [P, TT, BF_PARTS, H], BF16)
            nT = sb("nT", [BF_PARTS * H, S], BF16)
        pre_bank = [ctx.enter_context(nc.psum_tensor(f"{pre}bank{i}", [P, 512], F32)) for i in range(2)]
        sT = [ctx.enter_context(nc.psum_tensor(f"{pre}sT{i}", [P, 4 * S], F32)) for i in range(2)]
        od = [ctx.enter_context(nc.psum_tensor(f"{pre}od{i}", [P, 2, S], F32)) for i in range(2)]

        factors_ok, pool_own = sem("factors_ok"), sem("pool_own")
        z_ok = sem("z_ok")
        parts_own = sem("parts_own")
        main_own = sem("main_own")
        stats_own = sem("stats_own")
        rope_own = sem("rope_own")
        zT_ps, zT_ok = sem("zT_ps"), sem("zT_ok")
        proj_ps = {"q": sem("q_ps"), "k": sem("k_ps")}
        first_ok = {"q": sem("q_first"), "k": sem("k_first")}
        rest_ok = {"q": sem("q_rest"), "k": sem("k_rest")}
        second_ok = {"q": sem("q_second"), "k": sem("k_second")}
        parts_ok = {"q": sem("q_parts"), "k": sem("k_parts")}
        stack_dma = {"q": sem("q_dma"), "k": sem("k_dma")}
        v_ps, v_ok = sem("v_ps"), sem("v_ok")
        sT_ps, p_ok = sem("sT_ps"), sem("p_ok")
        pv_ps, attn_ok = sem("pv_ps"), sem("attn_ok")
        out_ps, res_ok, bo_ok = sem("out_ps"), sem("res_ok"), sem("bo_ok")
        cx_dma, cx_ps, cx_ok = (sem("cx_dma"), sem("cx_ps"), sem("cx_ok")) if cross else (None,) * 3
        s_ps, max_ok, n_ok = (sem("s_ps"), sem("max_ok"), sem("n_ok")) if not sigmoid else (None,) * 3
        nT_ps, nT_ok, n_dma = (sem("nT_ps"), sem("nT_ok"), sem("n_dma")) if not sigmoid else (None,) * 3
        tok_ok, rot_ok, tokq_ps, tokk_ps = (
            (sem("tok_ok"), sem("rot_ok"), sem("tokq_ps"), sem("tokk_ps")) if sigmoid else (None,) * 4)

        jobs = {"v": (1, 1, v_ok, 1, 1)}
        if sigmoid:
            jobs.update(tokq=(0, 2, tok_ok, 2, 1), tokk=(1, 2, tok_ok, 2, 2))
        if cross:
            jobs.update(cx=(0, 2, cx_ok, 1, 1))
        jobs.update(q=(1 if cross else 0, 2, rest_ok["q"], 1, 1), k=(0 if cross else 1, 2, rest_ok["k"], 1, 1))
        if not sigmoid:
            jobs.update({("s", i): (i % 2, 1, max_ok, NS, i + 1) for i in range(NS)})
        jobs.update(z=(0, 3, zT_ok, 1, 1))
        if not sigmoid:
            jobs.update(nT=(1, 1, nT_ok, 1, 1))
        order = list(jobs)

        def bank(job):
            return pre_bank[jobs[job][0]]

        def bank_free(pe, job, n):
            for back, others in ((0, order[:order.index(job)]), (1, order), (2, order)):
                for other in reversed(others):
                    its_bank, ahead, s, per, val = jobs[other]
                    if its_bank == jobs[job][0] and doing(n - back, ahead):
                        pe.wait_ge(s, (n - back + ahead) * per + val)
                        return

        def heads(c):
            half, par = c // KC // 2, c // KC % 2
            return half, par, [(g, 8 * half + 2 * g + par, ((2 * g + par) * KT + half)) for g in range(4)]

        block = ctx.enter_context(nc.Block())

        @block.sync
        def _(sp):
            passed = sem("sp_passed")

            def step(n, parity):
                do_m, do_l = doing(n, 1), doing(n, 2)
                m, l = n + 1, n + 2
                if cross and do_l:
                    if not known(l, 0):
                        sp.wait_ge(cx_ps, l)
                        alone(sp, passed)
                    sp.dma_start(cx[:, :], d["ctx"][bass.ds(l, 1), :, :].rearrange("b s c -> (b s) c")
                                 ).then_inc(cx_dma, 16)
                if not do_m:
                    return
                if sigmoid and not known(m, 0):
                    sp.wait_ge(sT_ps, n * NC + 1)
                    alone(sp, passed)
                elif not known(m, 0, 1):
                    sp.wait_ge(sT_ps, n * NC)
                    alone(sp, passed)
                elif known(m, 1):
                    sp.wait_ge(s_ps, 1)
                for which, stack in (("q", qstack), ("k", kstack)):
                    sp.wait_ge(parts_ok[which], m + 1)
                    for r, pair in enumerate(PAIRS):
                        src = parts[which][1 - parity][pair[0 if which == "q" else 1]]
                        dst = stack[1 - parity][r * HD:(r + 1) * HD, 0:H * width[which]]
                        sp.dma_start(dst.rearrange("c (h x) -> c h x", h=HH), src[:, :]).then_inc(stack_dma[which], 16)

            over_batches_ahead(sp, step)

        @block.gpsimd
        def _(pool):
            norm_factors(pool, pool_own, t, {"self": EPS_LN, "cross": None, "sigmoid": EPS_RMS}[kind], factors_ok)

            def step(n, parity):
                do_n, do_l = doing(n, 0), doing(n, 2)
                l = n + 2
                own = [0]

                def link(i):
                    own[0] += 1
                    i.then_inc(rope_own, 1)
                    pool.wait_ge(rope_own, l * 4 + own[0])

                if do_n and kind != "self":
                    pool.wait_ge(z_ok, n + 1)
                    bias = t["bc_x_o" if cross else "bc_l_o"]
                    for tt in range(TT):
                        x_t = t["x"][:, tile_at(n, tt)]
                        i = pool.tensor_tensor(x_t, x_t, bias[:, :], ALU.add)
                    i.then_inc(bo_ok, 1)
                if not do_l:
                    return
                if sigmoid:
                    for j, which in enumerate("qk"):
                        pool.wait_ge(tok_ok, 2 * l + j + 1)
                        if not known(l, 0):
                            pool.wait_ge(proj_ps[which], l)
                        pair = lambda a: a[:, :].rearrange("p (x two h) -> p x two h", two=2, h=HH)
                        link(pool.tensor_tensor(tok_cos[j][:, :], tok[j][:, :], t["cos"][:, :], ALU.mult))
                        pool.tensor_tensor(pair(tok_sin[j])[:, :, 0], pair(tok[j])[:, :, 1], pair(t["sin"])[:, :, 0], ALU.mult)
                        link(pool.tensor_tensor(pair(tok_sin[j])[:, :, 1], pair(tok[j])[:, :, 0], pair(t["sin"])[:, :, 1], ALU.mult))
                        i = pool.tensor_tensor(tok_rot[j][:, :], tok_cos[j][:, :], tok_sin[j][:, :], ALU.add)
                        i.then_inc(rot_ok, 1)
                for which in "qk":
                    pool.wait_ge(second_ok[which], l + 1)
                    p3 = parts[which][parity]
                    pool.tensor_tensor(p3[2][:, :], rest[which][:, :], p3[1][:, :], ALU.subtract).then_inc(parts_ok[which], 1)

            over_batches_ahead(pool, step)

        @block.scalar
        def _(act):
            def exp(n, c):
                g = n * NC + c
                act.wait_ge(sT_ps, g + 1)
                if not (known(n, 0) and c < 2):
                    act.wait_ge(pv_ps, g - 1)
                func = ACT.Sigmoid if sigmoid else ACT.Exp
                act.activation(probs[c % 2][0:KP, :], sT[c % 2][0:KP, :], func, scale=HD ** -0.5).then_inc(p_ok, 1)

            def transposed_rows(l):
                act.wait_ge(zT_ps, l + 1)
                if not known(l, 0):
                    act.wait_ge(proj_ps["q"] if cross else v_ps, l)
                act.activation(zT[:, :, :].rearrange("p k s -> p (k s)"), bank("z")[:, :], ACT.Identity).then_inc(zT_ok, 1)

            def transposed_context(l):
                act.wait_ge(cx_ps, l + 1)
                if not known(l, 0):
                    act.wait_ge(v_ps, l)
                act.activation(cxT[:, 0, :], bank("cx")[:, 0:SC], ACT.Identity)
                act.activation(cxT[0:C - P, 1, :], bank("cx")[0:C - P, SC:2 * SC], ACT.Identity).then_inc(cx_ok, 1)

            def first_part(l, parity, which):
                act.wait_ge(proj_ps[which], l + 1)
                if not known(l, 0, 1):
                    act.wait_ge(stack_dma[which], (l - 1) * STACKED)
                w = width[which]
                dst = parts[which][parity][0]
                if sigmoid:
                    i = act.activation(dst[:, :], bank(which)[:, 0:KT * w], ACT.Identity)
                else:
                    col = t[("col_x_b" if cross else "col_in_") + which]
                    for j in range(KT):
                        i = act.activation(dst[:, j * w:(j + 1) * w], bank(which)[:, j * w:(j + 1) * w], ACT.Identity,
                                           bias=col[:, j:j + 1])
                i.then_inc(first_ok[which], 1)

            def second_part(l, parity, which):
                act.wait_ge(rest_ok[which], l + 1)
                act.activation(parts[which][parity][1][:, :], rest[which][:, :], ACT.Identity).then_inc(second_ok[which], 1)

            def maxima_rows(m, parity):
                act.wait_ge(nT_ps, m + 1)
                if not known(m, 0):
                    act.wait_ge(n_dma, 16 * m)
                act.activation(nT[:, :], bank("nT")[0:BF_PARTS * H, 0:S // 2].bitcast(BF16), ACT.Identity).then_inc(nT_ok, 1)
                act.wait_ge(nT_ok, m + 1)
                dst = qstack[parity][STACK:STACK_M, :].rearrange("c (h x) -> c h x", h=H)
                act.dma_start(dst, nT[:, :]).then_inc(n_dma, 16)

            if sigmoid:
                plan = {-1: ["z"], 5: ["q first"], 6: ["k first", "q second"], 7: ["k second"]}
            elif cross:
                plan = {-1: ["cx"], 1: ["q first", "k first"], 2: ["q second", "k second"], 3: ["z ahead", "nT"]}
            else:
                plan = {-1: ["z"], 1: ["q first", "k first"], 2: ["q second"], 3: ["k second"], 7: ["nT"]}

            def step(n, parity):
                do_n, do_m, do_l = doing(n, 0), doing(n, 1), doing(n, 2)
                m, l = n + 1, n + 2
                for c in range(-1, NC):
                    if do_n and c >= 0:
                        exp(n, c)
                    for job in plan.get(c, []):
                        if job == "z ahead":
                            if doing(n, 3):
                                transposed_rows(n + 3)
                        elif job == "nT":
                            if do_m:
                                maxima_rows(m, 1 - parity)
                        elif not do_l:
                            continue
                        elif job == "z":
                            transposed_rows(l)
                        elif job == "cx":
                            transposed_context(l)
                        elif job.endswith("first"):
                            first_part(l, parity, job[0])
                        else:
                            second_part(l, parity, job[0])

            over_batches_ahead(act, step)

        @block.vector
        def _(dve):
            passed = sem("dve_passed")

            def rows(l):
                if known(l, 0):
                    dve.wait_ge(factors_ok, 1)
                else:
                    if known(l, 2):
                        dve.wait_ge(factors_ok, 2)
                    dve.wait_ge(zT_ps, l)
                normalise_rows(dve, t, z, l, 2 if kind == "self" else 0).then_inc(z_ok, 1)

            def token_major(l, j):
                dve.wait_ge(tokq_ps if j == 0 else tokk_ps, l + 1)
                if not known(l, 0):
                    dve.wait_ge(proj_ps["qk"[j]], l)
                for tt in range(TT):
                    i = dve.scalar_tensor_tensor(tok[j][:, tt * D:(tt + 1) * D], bank("tokq" if j == 0 else "tokk")[:, tt * D:(tt + 1) * D],
                                                 t["factors"][:, 1, bass.ds(l * TT + tt, 1)],
                                                 t["bc_l_q" if j == 0 else "bc_l_k"][:, :], ALU.mult, ALU.add)
                i.then_inc(tok_ok, 1)

            def values(m, parity):
                dve.wait_ge(v_ps, m + 1)
                if not known(m, 0, 1):
                    dve.wait_ge(pv_ps, (m - 1) * NC)
                bias = t["bc_x_v" if cross else "bc_l_v" if sigmoid else "bc_in_v"]
                for k in range(KC):
                    src = bank("v")[0:KP, k * D:(k + 1) * D].rearrange("p (x two c) -> p x two c", two=2, c=HD)
                    b = bias[0:KP, :].rearrange("p (x two c) -> p x two c", two=2, c=HD)
                    for par in range(2):
                        dst = v[parity][0:KP, k, :, par * 48:par * 48 + HD]
                        i = dve.tensor_tensor(dst, src[:, :, par, :], b[:, :, par, :], ALU.add)
                i.then_inc(v_ok, 1)

            def left_over(l, parity, which):
                dve.wait_ge(first_ok[which], l + 1)
                if not known(l, 0):
                    dve.wait_ge(parts_ok[which], l)
                w = width[which]
                first = parts[which][parity][0]
                if sigmoid:
                    i = dve.tensor_tensor(rest[which][:, :], bank(which)[:, 0:KT * w], first[:, :], ALU.subtract)
                else:
                    col = t[("col_x_b" if cross else "col_in_") + which]
                    for j in range(KT):
                        i = dve.scalar_tensor_tensor(rest[which][:, j * w:(j + 1) * w], bank(which)[:, j * w:(j + 1) * w],
                                                     col[:, j:j + 1], first[:, j * w:(j + 1) * w], ALU.add, ALU.subtract)
                i.then_inc(rest_ok[which], 1)

            def maxima(m, i):
                dve.wait_ge(s_ps, m * NS + i + 1)
                tt, h0 = i // (NS // TT), i % (NS // TT) * HB
                dve.tensor_reduce(nmax[:, tt, h0:h0 + HB], bank(("s", i))[:, 0:HB * SK].rearrange("p (h k) -> p h k", h=HB),
                                  AX_X, ALU.max, negate=True).then_inc(max_ok, 1)

            def max_parts(m):
                own = [0]

                def link(i):
                    own[0] += 1
                    i.then_inc(parts_own, 1)
                    dve.wait_ge(parts_own, m * 3 + own[0])

                dve.wait_ge(max_ok, (m + 1) * NS)
                if not known(m, 0):
                    dve.wait_ge(nT_ps, m)
                link(dve.tensor_copy(nparts[:, :, 0, :], nmax[:, :, :]))
                link(dve.tensor_tensor(nrest[:, :, :], nmax[:, :, :], nparts[:, :, 0, :], ALU.subtract))
                link(dve.tensor_copy(nparts[:, :, 1, :], nrest[:, :, :]))
                dve.tensor_tensor(nparts[:, :, 2, :], nrest[:, :, :], nparts[:, :, 1, :], ALU.subtract).then_inc(n_ok, 1)

            def normalise(n, half):
                per = 2 if sigmoid else 1
                own = [0]

                def link(i):
                    own[0] += 1
                    i.then_inc(main_own, 1)
                    dve.wait_ge(main_own, n * 2 * per + half * per + own[0])

                dve.wait_ge(pv_ps, n * NC + (half + 1) * NC // 2)
                if not known(n, 0):
                    dve.wait_ge(out_ps, n)
                src = od[half][:, 1, :]
                if sigmoid:
                    link(dve.tensor_scalar(dsum[:, half], src, EPS_RENORM, None, ALU.add))
                    src = dsum[:, half]
                link(dve.reciprocal(rden[:, half], src))
                dve.tensor_tensor(attnT[:, half, :], od[half][:, 0, :], rden[:, half], ALU.mult).then_inc(attn_ok, 1)

            def residual(n):
                dve.wait_ge(out_ps, n + 1)
                if kind != "self":
                    dve.wait_ge(bo_ok, n + 1)
                x_n = t["x"][:, at(n)]
                dve.tensor_tensor(x_n, od[0][:, :, :].rearrange("p a s -> p (a s)"), x_n, ALU.add).then_inc(res_ok, 1)

            def stats(n):
                own = [0]

                def link(i):
                    own[0] += 1
                    i.then_inc(stats_own, 1)
                    dve.wait_ge(stats_own, n * 3 + own[0])

                dve.wait_ge(res_ok, n + 1)
                link(tile_stats(dve, passed, link, t["x"], n, st, t["mv"]))

            def step(n, parity):
                late, do_n, do_m, do_l = (doing(n, ahead) for ahead in (-1, 0, 1, 2))
                m, l = n + 1, n + 2
                if do_m:
                    values(m, 1 - parity)
                if late:
                    residual(n - 1)
                if do_l and sigmoid:
                    token_major(l, 0)
                    token_major(l, 1)
                if doing(n, 3):
                    rows(n + 3)
                if late:
                    stats(n - 1)
                if do_l and not sigmoid:
                    left_over(l, parity, "q")
                    left_over(l, parity, "k")
                if do_m and not sigmoid:
                    for i in range(NS):
                        maxima(m, i)
                    max_parts(m)
                if do_n:
                    normalise(n, 0)
                if do_l and sigmoid:
                    left_over(l, parity, "q")
                    left_over(l, parity, "k")
                if do_n:
                    normalise(n, 1)

            over_batches_ahead(dve, step)

        @block.tensor
        def _(pe):
            passed = sem("pe_passed")
            ident = t["ident"]

            def prepare(job, n, parity):
                m, l = n + 1, n + 2
                if job == "z":
                    pe.wait_ge(z_ok, n + 3 + 1)
                    bank_free(pe, job, n)
                    for k in range(KT):
                        for tt in range(TT):
                            i = pe.transpose(bank("z")[:, k * S + tt * P:k * S + (tt + 1) * P],
                                             z[:, tt * D + k * P:tt * D + (k + 1) * P], ident[:, :])
                    i.then_inc(zT_ps, 1)
                elif job == "cx":
                    pe.wait_ge(cx_dma, 16 * (l + 1))
                    bank_free(pe, job, n)
                    pe.transpose(bank("cx")[:, 0:SC], cx[:, 0:P], ident[0:SC, 0:SC])
                    pe.transpose(bank("cx")[0:C - P, SC:2 * SC], cx[:, P:C], ident[0:SC, 0:SC]).then_inc(cx_ps, 1)
                elif job in ("q", "k") and sigmoid:
                    j = 0 if job == "q" else 1
                    pe.wait_ge(rot_ok, 2 * l + j + 1)
                    bank_free(pe, job, n)
                    for k in range(KT):
                        for tt in range(TT):
                            i = pe.transpose(bank(job)[:, k * S + tt * P:k * S + (tt + 1) * P],
                                             tok_rot[j][:, tt * D + k * P:tt * D + (k + 1) * P], ident[:, :])
                    i.then_inc(proj_ps[job], 1)
                elif job in ("q", "k"):
                    w, wd = WQ if job == "q" else WK, width[job]
                    pe.wait_ge(zT_ok, l + 1)
                    if cross and job == "k":
                        pe.wait_ge(cx_ok, l + 1)
                    bank_free(pe, job, n)
                    for mt in range(KT):
                        for k in range(KT):
                            src, kp = (cxT, (P, C - P)[k]) if cross and job == "k" else (zT, P)
                            i = pe.matmul(bank(job)[:, mt * wd:(mt + 1) * wd], t["wT"][0:kp, w, k, mt * P:(mt + 1) * P],
                                          src[0:kp, k, :], start=(k == 0), stop=(k == KT - 1))
                    i.then_inc(proj_ps[job], 1)
                elif job in ("tokq", "tokk", "v"):
                    w = {"tokq": WQ, "tokk": WK, "v": WV}[job]
                    pe.wait_ge(cx_ok if cross else zT_ok, (m if job == "v" else l) + 1)
                    bank_free(pe, job, n)
                    for tt in range(KC):
                        for k in range(KT):
                            src, kp = (cxT, (P, C - P)[k]) if cross else (zT, P)
                            i = pe.matmul(bank(job)[0:KP, tt * D:(tt + 1) * D], src[0:kp, k, tt * P:tt * P + KP],
                                          t["wT"][0:kp, w, k, :], start=(k == 0), stop=(k == KT - 1))
                    i.then_inc({"tokq": tokq_ps, "tokk": tokk_ps, "v": v_ps}[job], 1)
                elif job == "nT":
                    pe.wait_ge(n_ok, m + 1)
                    bank_free(pe, job, n)
                    alone(pe, passed)
                    for tt in range(TT):
                        i = pe.transpose(bank("nT")[0:BF_PARTS * H, tt * P // 2:(tt + 1) * P // 2].bitcast(BF16),
                                         nparts[:, tt, :, :].rearrange("p a h -> p (a h)"), t["ident_bf"][:, :])
                    i.then_inc(nT_ps, 1)
                else:
                    i0 = job[1]
                    if i0 == 0:
                        pe.wait_ge(stack_dma["q"], (m + 1) * STACKED)
                        pe.wait_ge(stack_dma["k"], (m + 1) * STACKED)
                    bank_free(pe, job, n)
                    tt, h0 = i0 // (NS // TT), i0 % (NS // TT) * HB
                    for j in range(HB):
                        i = pe.matmul(bank(job)[:, j * SK:(j + 1) * SK],
                                      qstack[1 - parity][0:STACK, (h0 + j) * S + tt * P:(h0 + j) * S + (tt + 1) * P],
                                      kstack[1 - parity][0:STACK, (h0 + j) * SK:(h0 + j + 1) * SK], start=True, stop=True)
                    i.then_inc(s_ps, 1)

            def scores(n, c, parity):
                if not (known(n, 0) and c < 2):
                    pe.wait_ge(p_ok, n * NC + c - 1)
                kt = c % KC
                for j, (_, _, col) in enumerate(heads(c)[2]):
                    i = pe.matmul(sT[c % 2][0:KP, j * S:(j + 1) * S],
                                  kstack[parity][0:RQ, col * SK + kt * KP:col * SK + (kt + 1) * KP],
                                  qstack[parity][0:RQ, col * S:(col + 1) * S], start=True, stop=True)
                i.then_inc(sT_ps, 1)

            def times_values(n, c, parity):
                half, par, hs = heads(c)
                if c == 0 and not known(n, 0):
                    pe.wait_ge(res_ok, n)
                pe.wait_ge(p_ok, n * NC + c + 1)
                kt = c % KC
                first = c % (NC // 2) == 0
                last = c % (NC // 2) == NC // 2 - 1
                for which in range(2):
                    for j, (g, h, _) in enumerate(hs):
                        lhs = v[parity][0:KP, kt, h // 2, par * 32:(par + 1) * 32] if which == 0 else t["head_ones"][0:KP, par, :]
                        i = pe.matmul(od[half][32 * g:32 * (g + 1), which, :], lhs, probs[c % 2][0:KP, j * S:(j + 1) * S],
                                      start=(first and which == 0), stop=last, skip_group_check=True)
                i.then_inc(pv_ps, 1)

            def project(n):
                pe.wait_ge(attn_ok, TT * (n + 1))
                for tt in range(TT):
                    for k in range(KT):
                        i = pe.matmul(od[0][:, tt, :], attnT[:, k, tt * P:(tt + 1) * P], t["wT"][:, WO, k, :],
                                      start=(k == 0), stop=(k == KT - 1))
                i.then_inc(out_ps, 1)

            def group(*numbers):
                return [("s", i) for i in numbers]

            if sigmoid:
                plan = {0: (["v"], [], []), 1: ([], ["tokq"], ["tokk"]), 5: ([], ["q"], []), 6: ([], ["k"], []),
                        7: ([], [], ["z"])}
            elif cross:
                plan = {0: (["v", "cx"], [], []), 1: ([], ["q"], ["k"]), 2: ([], group(0, 1), group(2, 3)),
                        3: ([], group(4, 5), group(6, 7)), 4: ([], [], ["z", "nT"])}
            else:
                plan = {0: (["v"], [], []), 1: ([], ["q"], ["k"]), 2: ([], [], group(0, 1)),
                        3: ([], group(2, 3), group(4, 5)), 4: ([], group(6, 7), group(8)),
                        5: ([], group(9, 10), group(11, 12)), 6: ([], group(13, 14), group(15)), 7: ([], [], ["z", "nT"])}
            planned = [job for c in range(NC + 1) for jj in plan.get(c, ()) for job in jj]
            assert planned == order, (planned, order)

            def step(n, parity):
                late, do_n, do_m, do_l = (doing(n, ahead) for ahead in (-1, 0, 1, 2))

                def prepare_group(c, which):
                    for job in plan.get(c, ((), (), ()))[which]:
                        if doing(n, jobs[job][1]):
                            prepare(job, n, parity)

                prepare_group(0, 0)
                if do_n:
                    pe.wait_ge(stack_dma["q"], (n + 1) * STACKED)
                    pe.wait_ge(stack_dma["k"], (n + 1) * STACKED)
                    pe.wait_ge(v_ok, n + 1)
                    if not sigmoid:
                        pe.wait_ge(n_dma, 16 * (n + 1))
                for c in range(NC + 1):
                    if do_n and c < NC:
                        scores(n, c, parity)
                    if c == 0 and late:
                        project(n - 1)
                    prepare_group(c, 1)
                    if do_n and c >= 1:
                        times_values(n, c - 1, parity)
                    prepare_group(c, 2)

            over_batches_ahead(pe, step)


def linear_stage(nc, t, d):
    with ExitStack() as ctx:
        stage_sems = ctx.enter_context(StageSemaphores(nc))
        sem = lambda name: stage_sems.new("ffn_" + name)
        sb = lambda name, shape, dt: ctx.enter_context(nc.sbuf_tensor("ffn_" + name, shape, dt))
        st = sb("st", [P, TT, 8], F32)
        z = [sb(f"z{i}", [P, TT * D], F32) for i in range(2)]
        zT = [sb(f"zT{i}", [P, KT * S], F32) for i in range(2)]
        zT_bank = [ctx.enter_context(nc.psum_tensor(f"ffn_zT_bank{i}", [P, 512], F32)) for i in range(2)]
        out_bank = [ctx.enter_context(nc.psum_tensor(f"ffn_out_bank{i}", [P, 512], F32)) for i in range(2)]
        factors_ok, pool_own, z_ok, zT_ps, zT_ok, out_ps, res_ok, bo_ok, dve_own = map(
            sem, ("factors_ok", "pool_own", "z_ok", "zT_ps", "zT_ok", "out_ps", "res_ok", "bo_ok", "dve_own"))
        block = ctx.enter_context(nc.Block())

        @block.vector
        def _(dve):
            passed = sem("dve_passed")
            def step(n, parity):
                l = n + 2
                own = [0]

                def link(i):
                    own[0] += 1
                    i.then_inc(dve_own, 1)
                    dve.wait_ge(dve_own, n * 3 + own[0])

                if doing(n, 2):
                    if known(l, 0):
                        dve.wait_ge(factors_ok, 1)
                    if known(l, 2):
                        dve.wait_ge(factors_ok, 2)
                    if not known(l, 0, 1):
                        dve.wait_ge(zT_ps, l - 1)
                    normalise_rows(dve, t, z[parity], l).then_inc(z_ok, 1)
                if doing(n, 0):
                    dve.wait_ge(out_ps, n + 1)
                    dve.wait_ge(bo_ok, n + 1)
                    x_n = t["x"][:, at(n)]
                    i = dve.tensor_tensor(x_n, out_bank[parity][:, :], x_n, ALU.add)
                    i.then_inc(res_ok, 1)
                    dve.wait_ge(res_ok, n + 1)
                    link(tile_stats(dve, passed, link, t["x"], n, st, t["mv"]))

            over_batches_ahead(dve, step)

        @block.gpsimd
        def _(pool):
            passed = sem("pool_passed")
            norm_factors(pool, pool_own, t, None, factors_ok)

            def step(n, parity, main, pre):
                if main:
                    pool.wait_ge(z_ok, n + 1)
                    for tt in range(TT):
                        x_t = t["x"][:, tile_at(n, tt)]
                        i = pool.tensor_tensor(x_t, x_t, t["bc_ffn"][:, :], ALU.add)
                    i.then_inc(bo_ok, 1)

            over_batches(pool, step)

        @block.scalar
        def _(act):
            def step(n, parity, main, pre):
                m = n + 1
                if pre:
                    act.wait_ge(zT_ps, m + 1)
                    if not known(m, 0, 1):
                        act.wait_ge(out_ps, m - 1)
                    act.activation(zT[1 - parity][:, :], zT_bank[1 - parity][:, :], ACT.Identity).then_inc(zT_ok, 1)

            over_batches(act, step)

        @block.tensor
        def _(pe):
            passed = sem("pe_passed")
            def step(n, parity, main, pre):
                m = n + 1
                if pre:
                    pe.wait_ge(z_ok, m + 1)
                    if not known(m, 0, 1):
                        pe.wait_ge(zT_ok, m - 1)
                    for k in range(KT):
                        for tt in range(TT):
                            i = pe.transpose(zT_bank[1 - parity][:, k * S + tt * P:k * S + (tt + 1) * P],
                                             z[1 - parity][:, tt * D + k * P:tt * D + (k + 1) * P], t["ident"][:, :])
                    i.then_inc(zT_ps, 1)
                if main:
                    pe.wait_ge(zT_ok, n + 1)
                    if not known(n, 0, 1):
                        pe.wait_ge(res_ok, n - 1)
                    for tt in range(TT):
                        for k in range(KT):
                            i = pe.matmul(out_bank[parity][:, tt * D:(tt + 1) * D],
                                          zT[parity][:, k * S + tt * P:k * S + (tt + 1) * P], t["ffn"][:, k, :],
                                          start=(k == 0), stop=(k == KT - 1))
                    i.then_inc(out_ps, 1)

            over_batches(pe, step)


def single_head_stage(nc, t, d):
    SCALE = D ** -0.5
    with ExitStack() as ctx:
        stage_sems = ctx.enter_context(StageSemaphores(nc))
        sem = lambda name: stage_sems.new("one_" + name)
        sb = lambda name, shape, dt: ctx.enter_context(nc.sbuf_tensor("one_" + name, shape, dt))
        st = sb("st", [P, TT, 8], F32)
        z = sb("z", [P, TT * D], F32)
        zT = sb("zT", [P, KT, S], F32)
        cx = sb("cx", [SC, C], F32)
        cxT = sb("cxT", [P, 2, SC], F32)
        qT = [sb(f"qT{i}", [P, KT, S], F32) for i in range(2)]
        kT = [sb(f"kT{i}", [P, KT, SC], F32) for i in range(2)]
        v = [sb(f"v{i}", [SC, D], F32) for i in range(2)]
        nmax = sb("nmax", [P, TT], F32)
        nbias = sb("nbias", [P, TT], F32)
        probs = sb("probs", [P, TT, SC], F32)
        sums = sb("sums", [P, TT], F32)
        rden = sb("rden", [P, TT], F32)
        pT = sb("pT", [SC, S], F32)
        pre_bank = [ctx.enter_context(nc.psum_tensor(f"one_pre{i}", [P, 512], F32)) for i in range(3)]
        s_bank = ctx.enter_context(nc.psum_tensor("one_s_bank", [P, 512], F32))
        pT_bank = ctx.enter_context(nc.psum_tensor("one_pT_bank", [P, 512], F32))
        out_bank = ctx.enter_context(nc.psum_tensor("one_out_bank", [P, 512], F32))
        factors_ok, pool_own = map(sem, ("factors_ok", "pool_own"))
        (z_ok, dve_own, main_own, zT_ps, zT_ok, cx_dma, cx_ps, cx_ok, q_ps, q_ok, k_ps, k_ok, v_ps, v_ok, s_ps,
         max_ok, exp_ok, pT_ps, pT_ok, out_ps, res_ok) = map(sem, (
             "z_ok", "dve_own", "main_own", "zT_ps", "zT_ok", "cx_dma", "cx_ps", "cx_ok", "q_ps", "q_ok", "k_ps",
             "k_ok", "v_ps", "v_ok", "s_ps", "max_ok", "exp_ok", "pT_ps", "pT_ok", "out_ps", "res_ok"))
        block = ctx.enter_context(nc.Block())

        @block.sync
        def _(sp):
            passed = sem("sp_passed")
            def step(n, parity, main, pre):
                m = n + 1
                if pre:
                    if main:
                        sp.wait_ge(cx_ps, m)
                        alone(sp, passed)
                    sp.dma_start(cx[:, :], d["ctx"][bass.ds(m, 1), :, :].rearrange("b s c -> (b s) c")
                                 ).then_inc(cx_dma, 16)

            over_batches(sp, step)

        @block.gpsimd
        def _(pool):
            norm_factors(pool, pool_own, t, None, factors_ok)

        @block.vector
        def _(dve):
            passed = sem("dve_passed")
            def step(n, parity):
                m, l = n + 1, n + 2
                own = [0]

                def link(i):
                    own[0] += 1
                    i.then_inc(dve_own, 1)
                    dve.wait_ge(dve_own, n * 3 + own[0])

                if doing(n, 0):
                    dve.wait_ge(s_ps, n + 1)
                    i = dve.tensor_reduce(nmax[:, :], s_bank[:, 0:TT * SC].rearrange("p (t k) -> p t k", t=TT),
                                          AX_X, ALU.max, negate=True)
                    i.then_inc(main_own, 1)
                    dve.wait_ge(main_own, 2 * n + 1)
                    dve.tensor_scalar(nbias[:, :], nmax[:, :], SCALE, None, ALU.mult).then_inc(max_ok, 1)
                if doing(n, 2):
                    if known(l, 0):
                        dve.wait_ge(factors_ok, 1)
                    else:
                        if known(l, 2):
                            dve.wait_ge(factors_ok, 2)
                        dve.wait_ge(zT_ps, l)
                    normalise_rows(dve, t, z, l).then_inc(z_ok, 1)
                if doing(n, 1):
                    dve.wait_ge(v_ps, m + 1)
                    if not known(m, 0, 1):
                        dve.wait_ge(out_ps, m - 1)
                    dve.tensor_tensor(v[1 - parity][:, :], pre_bank[0][0:SC, 0:D], t["bc_c_v"][0:SC, :],
                                      ALU.add).then_inc(v_ok, 1)
                if doing(n, 0):
                    dve.wait_ge(exp_ok, n + 1)
                    dve.reciprocal(rden[:, :], sums[:, :]).then_inc(main_own, 1)
                    dve.wait_ge(main_own, 2 * n + 2)
                    dve.wait_ge(out_ps, n + 1)
                    for tt in range(TT):
                        x_t = t["x"][:, tile_at(n, tt)]
                        i = dve.scalar_tensor_tensor(x_t, out_bank[:, tt * D:(tt + 1) * D], rden[:, tt:tt + 1], x_t,
                                                     ALU.mult, ALU.add)
                    i.then_inc(res_ok, 1)
                    dve.wait_ge(res_ok, n + 1)
                    link(tile_stats(dve, passed, link, t["x"], n, st, t["mv"]))

            over_batches_ahead(dve, step)

        @block.scalar
        def _(act):
            def step(n, parity, main, pre):
                m = n + 1
                if pre:
                    act.wait_ge(zT_ps, m + 1)
                    if main:
                        act.wait_ge(q_ps, m)
                    act.activation(zT[:, :, :].rearrange("p k s -> p (k s)"), pre_bank[0][:, :], ACT.Identity).then_inc(zT_ok, 1)
                    act.wait_ge(cx_ps, m + 1)
                    if main:
                        act.wait_ge(v_ps, m)
                    act.activation(cxT[:, 0, :], pre_bank[1][:, 0:SC], ACT.Identity)
                    act.activation(cxT[0:C - P, 1, :], pre_bank[1][0:C - P, SC:2 * SC], ACT.Identity).then_inc(cx_ok, 1)
                if main:
                    act.wait_ge(max_ok, n + 1)
                    if not known(n, 0):
                        act.wait_ge(pT_ps, n)
                        act.wait_ge(res_ok, n)
                    for tt in range(TT):
                        i = act.activation(probs[:, tt, :], s_bank[:, tt * SC:(tt + 1) * SC], ACT.Exp,
                                           bias=nbias[:, tt:tt + 1], scale=SCALE, accum_out=sums[:, tt:tt + 1])
                    i.then_inc(exp_ok, 1)
                if pre:
                    act.wait_ge(q_ps, m + 1)
                    if not known(m, 0, 1):
                        act.wait_ge(s_ps, m - 1)
                    for j in range(KT):
                        i = act.activation(qT[1 - parity][:, j, :], pre_bank[2][:, j * S:(j + 1) * S], ACT.Identity,
                                           bias=t["col_c_bq"][:, j:j + 1])
                    i.then_inc(q_ok, 1)
                    act.wait_ge(k_ps, m + 1)
                    for j in range(KT):
                        i = act.activation(kT[1 - parity][:, j, :], pre_bank[1][:, j * SC:(j + 1) * SC], ACT.Identity,
                                           bias=t["col_c_bk"][:, j:j + 1])
                    i.then_inc(k_ok, 1)
                if main:
                    act.wait_ge(pT_ps, n + 1)
                    if not known(n, 0):
                        act.wait_ge(out_ps, n)
                    act.activation(pT[:, :], pT_bank[0:SC, 0:S], ACT.Identity).then_inc(pT_ok, 1)

            over_batches(act, step)

        @block.tensor
        def _(pe):
            passed = sem("pe_passed")
            ident = t["ident"]

            def step(n, parity, main, pre):
                m, par = n + 1, 1 - parity
                if pre:
                    pe.wait_ge(z_ok, m + 1)
                    if main:
                        pe.wait_ge(v_ok, m)
                    for k in range(KT):
                        for tt in range(TT):
                            i = pe.transpose(pre_bank[0][:, k * S + tt * P:k * S + (tt + 1) * P],
                                             z[:, tt * D + k * P:tt * D + (k + 1) * P], ident[:, :])
                    i.then_inc(zT_ps, 1)
                    pe.wait_ge(cx_dma, 16 * (m + 1))
                    if main:
                        pe.wait_ge(k_ok, m)
                    pe.transpose(pre_bank[1][:, 0:SC], cx[:, 0:P], ident[0:SC, 0:SC])
                    pe.transpose(pre_bank[1][0:C - P, SC:2 * SC], cx[:, P:C], ident[0:SC, 0:SC]).then_inc(cx_ps, 1)
                if main:
                    pe.wait_ge(q_ok, n + 1)
                    pe.wait_ge(k_ok, n + 1)
                    if not known(n, 0):
                        pe.wait_ge(exp_ok, n)
                    for tt in range(TT):
                        for k in range(KT):
                            i = pe.matmul(s_bank[:, tt * SC:(tt + 1) * SC], qT[parity][:, k, tt * P:(tt + 1) * P],
                                          kT[parity][:, k, :], start=(k == 0), stop=(k == KT - 1))
                    i.then_inc(s_ps, 1)
                if pre:
                    pe.wait_ge(zT_ok, m + 1)
                    if main:
                        pe.wait_ge(q_ok, m)
                    for j in range(KT):
                        for k in range(KT):
                            i = pe.matmul(pre_bank[2][:, j * S:(j + 1) * S], t["c_wq"][:, k, j * P:(j + 1) * P],
                                          zT[:, k, :], start=(k == 0), stop=(k == KT - 1))
                    i.then_inc(q_ps, 1)
                    pe.wait_ge(cx_ok, m + 1)
                    for j in range(KT):
                        for k, kp in ((0, P), (1, C - P)):
                            i = pe.matmul(pre_bank[1][:, j * SC:(j + 1) * SC], t["c_wk"][0:kp, k, j * P:(j + 1) * P],
                                          cxT[0:kp, k, :], start=(k == 0), stop=(k == 1))
                    i.then_inc(k_ps, 1)
                if main:
                    pe.wait_ge(exp_ok, n + 1)
                    if not known(n, 0):
                        pe.wait_ge(pT_ok, n)
                    for tt in range(TT):
                        i = pe.transpose(pT_bank[0:SC, tt * P:(tt + 1) * P], probs[:, tt, :], ident[:, :])
                    i.then_inc(pT_ps, 1)
                if pre:
                    for k, kp in ((0, P), (1, C - P)):
                        i = pe.matmul(pre_bank[0][0:SC, 0:D], cxT[0:kp, k, :], t["c_wv"][0:kp, k, :],
                                      start=(k == 0), stop=(k == 1))
                    i.then_inc(v_ps, 1)
                if main:
                    pe.wait_ge(pT_ok, n + 1)
                    pe.wait_ge(v_ok, n + 1)
                    if not known(n, 0):
                        pe.wait_ge(res_ok, n)
                    for tt in range(TT):
                        i = pe.matmul(out_bank[:, tt * D:(tt + 1) * D], pT[:, tt * P:(tt + 1) * P], v[parity][:, :],
                                      start=True, stop=True)
                    i.then_inc(out_ps, 1)

            over_batches(pe, step)


def expert_stage(nc, t, d):
    RING = 4
    with ExitStack() as ctx:
        stage_sems = ctx.enter_context(StageSemaphores(nc))
        sem = lambda name: stage_sems.new("moe_" + name)
        sb = lambda name, shape, dt: ctx.enter_context(nc.sbuf_tensor("moe_" + name, shape, dt))
        st = sb("st", [P, TT, 8], F32)
        z = [sb(f"z{i}", [P, TT * D], F32) for i in range(2)]
        zT_all = sb("zT_all", [P, B * KT * S], F32)
        zT = [sb(f"zT{i}", [P, KT, P], F32) for i in range(RING)]
        col_sums = sb("col_sums", [P, B * KT * TT], F32)
        emb = sb("emb", [P, KT, B, TT], F32)
        work = sb("work", [CHUNKS, 8, NB], F32)
        one = sb("one", [CHUNKS, 8], F32)
        picked = sb("picked", [CHUNKS, 2], I32)
        picked_row = sb("picked_row", [1, 2 * CHUNKS], I32)
        experts = [sb(f"experts{i}", [P, 2, KT, D], F32) for i in range(RING)]
        both = [sb(f"both{i}", [P, KT, D], F32) for i in range(RING)]
        zT_bank = [ctx.enter_context(nc.psum_tensor(f"moe_zT_bank{i}", [P, 512], F32)) for i in range(2)]
        out_bank = [ctx.enter_context(nc.psum_tensor(f"moe_out_bank{i}", [P, 512], F32)) for i in range(RING)]
        hash_bank = ctx.enter_context(nc.psum_tensor("moe_hash", [P, 512], F32))
        factors_ok, pool_own = map(sem, ("factors_ok", "pool_own"))
        (z_ok, dve_own, zT_ps, zT_ok, sum_ok, emb_ok, hash_ps, hash_own, picked_ok, picked_dma, w_dma0, w_dma1, w_dma2,
         w_dma3, zcopy_ok, out_ps, res_ok, store) = map(sem, (
             "z_ok", "dve_own", "zT_ps", "zT_ok", "sum_ok", "emb_ok", "hash_ps", "hash_own", "picked_ok", "picked_dma",
             "w_dma0", "w_dma1", "w_dma2", "w_dma3", "zcopy_ok", "out_ps", "res_ok", "store"))
        w_dma = [w_dma0, w_dma1, w_dma2, w_dma3]
        both_ok = sem("both_ok")
        block = ctx.enter_context(nc.Block())

        def over_chunks(eng, step):
            for slot in range(RING):
                step(0, slot, slot)
            with eng.Fori(1, CHUNKS // RING) as i:
                for slot in range(RING):
                    step(i, i * RING + slot, slot)

        def load_expert(eng, j, i, c, slot):
            e = eng.value_load(picked_row[0:1, bass.ds(c * 2 + j, 1)], min_val=0, max_val=E_COUNT - 1)
            if not known(i, 0):
                eng.wait_ge(both_ok, c - RING + 1)
            eng.dma_start(experts[slot][:, j, :, :],
                          d["experts"][bass.ds(e, 1), :, :].rearrange("e (t p) f -> p (e t) f", p=P)
                          ).then_inc(w_dma[slot], 16)

        @block.sync
        def _(sp):
            sp.wait_ge(picked_ok, 1)
            sp.dma_start(picked_row[:, :], picked[:, :]).then_inc(picked_dma, 16)
            sp.wait_ge(picked_dma, 16)

            over_chunks(sp, lambda i, c, slot: load_expert(sp, 0, i, c, slot))

        @block.gpsimd
        def _(pool):
            passed = sem("pool_passed")
            norm_factors(pool, pool_own, t, None, factors_ok)
            pool.wait_ge(zT_ok, B)

            def step(i, c, slot):
                if not known(i, 0):
                    pool.wait_ge(out_ps, c - RING + 1)
                base = i * (RING // TT * KT * S) + (slot // TT) * (KT * S) + (slot % TT) * P
                alone(pool, passed)
                for k in range(KT):
                    j = pool.tensor_copy(zT[slot][:, k, :], zT_all[:, bass.ds(base + k * S, P)])
                j.then_inc(zcopy_ok, 1)

            over_chunks(pool, step)

        @block.vector
        def _(dve):
            passed = sem("dve_passed")
            def step(n, parity, main, pre):
                m = n + 1
                if pre:
                    if known(m, 0):
                        dve.wait_ge(factors_ok, 1)
                    if known(m, 1):
                        dve.wait_ge(factors_ok, 2)
                    if not known(m, 0, 1):
                        dve.wait_ge(zT_ps, m - 1)
                    normalise_rows(dve, t, z[1 - parity], m).then_inc(z_ok, 1)

            over_batches(dve, step)
            own = [0]

            def link(i):
                own[0] += 1
                i.then_inc(hash_own, 1)
                dve.wait_ge(hash_own, own[0])

            dve.wait_ge(zT_ok, B)
            sums = col_sums[:, :].rearrange("p (b k t) -> p k b t", k=KT, t=TT)
            for k in range(KT):
                i = dve.tensor_scalar(emb[:, k], sums[:, k], 1.0 / P, None, ALU.mult)
            i.then_inc(emb_ok, 1)
            W = lambda j: work[:, j, :]
            powers, proj, bits, weights, small_abs, tie, cand, flipped = map(W, range(8))
            for b in range(NB):
                i = dve.memset(work[:, 0, b:b + 1], float(2 ** b))
            link(i)
            dve.wait_ge(hash_ps, 1)
            link(dve.tensor_copy(proj, hash_bank[0:CHUNKS, 0:NB]))
            link(dve.tensor_scalar(bits, proj, 0.0, None, ALU.is_gt))
            link(dve.tensor_tensor(weights, bits, powers, ALU.mult))
            link(dve.tensor_reduce(one[:, 0:1], weights, AX_X, ALU.add))
            link(dve.scalar_tensor_tensor(small_abs, proj, -1.0, proj, ALU.mult, ALU.max))
            link(dve.tensor_reduce(one[:, 1:2], small_abs, AX_X, ALU.min))
            link(dve.tensor_scalar(tie, small_abs, one[:, 1:2], None, ALU.is_equal))
            link(dve.tensor_scalar(tie, tie, -float(2 ** NB), float(2 ** NB), ALU.mult, ALU.add))
            link(dve.tensor_tensor(cand, tie, powers, ALU.add))
            link(dve.tensor_reduce(one[:, 2:3], cand, AX_X, ALU.min))
            link(dve.tensor_scalar(flipped, powers, one[:, 2:3], None, ALU.is_equal))
            link(dve.tensor_tensor(flipped, flipped, weights, ALU.mult))
            link(dve.tensor_reduce(one[:, 3:4], flipped, AX_X, ALU.add))
            link(dve.tensor_tensor(one[:, 4:5], one[:, 0:1], one[:, 2:3], ALU.add))
            link(dve.tensor_scalar(one[:, 5:6], one[:, 3:4], -2.0, None, ALU.mult))
            link(dve.tensor_tensor(one[:, 6:7], one[:, 4:5], one[:, 5:6], ALU.add))
            dve.tensor_copy(picked[:, 0:1], one[:, 0:1])
            dve.tensor_copy(picked[:, 1:2], one[:, 6:7]).then_inc(picked_ok, 1)

            def chunk(i, c, slot):
                dve.wait_ge(w_dma[slot], i * 32 + 32)
                if not known(i, 0):
                    dve.wait_ge(out_ps, c - RING + 1)
                pair = experts[slot]
                dve.tensor_tensor(both[slot][:, :, :], pair[:, 0], pair[:, 1], ALU.add).then_inc(both_ok, 1)
                if not (known(i, 0) and slot == 0):
                    output(c - 1, (slot - 1) % RING)

            def output(c, slot):
                dve.wait_ge(out_ps, c + 1)
                x_c = t["x"][:, bass.ds(c * D, D)]
                dve.scalar_tensor_tensor(x_c, out_bank[slot][:, 0:D], 0.5, x_c, ALU.mult, ALU.add).then_inc(res_ok, 1)

            over_chunks(dve, chunk)
            output(CHUNKS - 1, RING - 1)

        @block.scalar
        def _(act):
            def step(n, parity, main, pre):
                m = n + 1
                if pre:
                    act.wait_ge(zT_ps, m + 1)
                    for x in range(KT * TT):
                        i = act.activation(zT_all[:, bass.ds(m * (KT * S) + x * P, P)], zT_bank[1 - parity][:, x * P:(x + 1) * P],
                                           ACT.Identity, accum_out=col_sums[:, bass.ds(m * (KT * TT) + x, 1)])
                    i.then_inc(zT_ok, 1)

            over_batches(act, step)

            act.wait_ge(picked_dma, 16)

            def chunk(i, c, slot):
                load_expert(act, 1, i, c, slot)
                if not known(i, 0):
                    output(i - 1, c - RING, slot)

            def output(i, c, slot):
                act.wait_ge(res_ok, c + 1)
                seq = i * (RING // TT) + slot // TT
                act.dma_start(d["out"][bass.ds(seq, 1), (slot % TT) * P:(slot % TT + 1) * P, :].rearrange("b p f -> (b p) f"),
                              t["x"][:, bass.ds(c * D, D)]).then_inc(store, 16)

            over_chunks(act, chunk)
            for slot in range(RING):
                output(CHUNKS // RING - 1, CHUNKS - RING + slot, slot)
            act.wait_ge(store, 16 * CHUNKS)

        @block.tensor
        def _(pe):
            passed = sem("pe_passed")
            def step(n, parity, main, pre):
                m = n + 1
                if pre:
                    pe.wait_ge(z_ok, m + 1)
                    if not known(m, 0, 1):
                        pe.wait_ge(zT_ok, m - 1)
                    for k in range(KT):
                        for tt in range(TT):
                            i = pe.transpose(zT_bank[1 - parity][:, k * S + tt * P:k * S + (tt + 1) * P],
                                             z[1 - parity][:, tt * D + k * P:tt * D + (k + 1) * P], t["ident"][:, :])
                    i.then_inc(zT_ps, 1)

            over_batches(pe, step)
            pe.wait_ge(emb_ok, 1)
            for k in range(KT):
                i = pe.matmul(hash_bank[0:CHUNKS, 0:NB], emb[:, k].rearrange("p b t -> p (b t)"), t["hyper"][:, k, :],
                              start=(k == 0), stop=(k == KT - 1))
            i.then_inc(hash_ps, 1)

            def chunk(i, c, slot):
                pe.wait_ge(zcopy_ok, c + 1)
                pe.wait_ge(both_ok, c + 1)
                if not known(i, 0):
                    pe.wait_ge(res_ok, c - RING + 1)
                for k in range(KT):
                    m = pe.matmul(out_bank[slot][:, 0:D], zT[slot][:, k, :], both[slot][:, k, :],
                                  start=(k == 0), stop=(k == KT - 1))
                m.then_inc(out_ps, 1)

            over_chunks(pe, chunk)


def decoder_kernel(nc, d):
    with ExitStack() as ctx:
        def sb(name, shape, dt):
            return ctx.enter_context(nc.sbuf_tensor(name, shape, dt))

        t = {"x": sb("x_res", [P, CHUNKS * D], F32),
             "wT": sb("wT", [P, len(W_NAMES), KT, D], F32),
             "ident": sb("ident", [P, P], F32), "ident_bf": sb("ident_bf", [P, P], BF16),
             "ones": sb("ones", [P, P], F32), "head_ones": sb("head_ones", [P, 2, 32], F32),
             "minus_half": sb("minus_half", [P, CHUNKS], F32),
             "mv": sb("mv", [P, CHUNKS * 2], F32), "factors": sb("factors", [P, 4, CHUNKS], F32),
             "hyper": sb("hyper_w", [P, KT, NB], F32), "cos": sb("cos_t", [P, TT * D], F32), "sin": sb("sin_t", [P, TT * D], F32),
             "ffn": sb("ffn_m", [P, KT, D], F32),
             "v": [sb(f"v_heads{i}", [P, TT, H // 2, 64], F32) for i in range(2)],
             "qstack": [sb(f"qstack{i}", [STACK_M, H * S], BF16) for i in range(2)],
             "kstack": [sb(f"kstack{i}", [STACK_M, H * S], BF16) for i in range(2)]}
        for name in ("c_wq", "c_wk", "c_wv"):
            t[name] = sb(name + "_m", [P, KT, D], F32)
        for name in ("bc_in_v", "bc_x_v", "bc_l_q", "bc_l_k", "bc_l_v", "bc_c_v", "bc_x_o", "bc_l_o", "bc_ffn"):
            t[name] = sb(name, [P, D], F32)
        for name in ("row_x_bo", "row_l_bo", "row_ffn_bias"):
            t[name] = sb(name, [1, D], F32)
        for name in ("col_in_q", "col_in_k", "col_x_bq", "col_x_bk", "col_c_bq", "col_c_bk"):
            t[name] = sb(name, [P, KT], F32)
        setup_stage(nc, t, d)
        attention_stage(nc, t, d, "self")
        attention_stage(nc, t, d, "cross")
        linear_stage(nc, t, d)
        attention_stage(nc, t, d, "sigmoid")
        single_head_stage(nc, t, d)
        expert_stage(nc, t, d)


_INS = {
    "x": "x", "ctx": "ctx_768", "in_proj": "L0_attn_in_proj_w", "out_proj": "L0_attn_out_proj_w",
    "ln_gamma": "L0_attn_ln_gamma", "ln_beta": "L0_attn_ln_beta",
    "x_wq": "L0_xattn_wq", "x_bq": "L0_xattn_bq", "x_wk": "L0_xattn_wk", "x_bk": "L0_xattn_bk",
    "x_wv": "L0_xattn_wv", "x_bv": "L0_xattn_bv", "x_wo": "L0_xattn_wo", "x_bo": "L0_xattn_bo",
    "ffn_w": "L0_ffn_kernel", "ffn_bias": "L0_ffn_bias", "ffn_a": "L0_ffn_a", "ffn_b": "L0_ffn_b",
    "l_qw": "L1_attn_q_w", "l_bq": "L1_attn_q_b", "l_kw": "L1_attn_k_w", "l_bk": "L1_attn_k_b",
    "l_vw": "L1_attn_v_w", "l_bv": "L1_attn_v_b", "l_ow": "L1_attn_o_w", "l_bo": "L1_attn_o_b",
    "qn": "L1_attn_qn_scale", "kn": "L1_attn_kn_scale",
    "c_wq": "L1_xattn_Wq", "c_bq": "L1_xattn_bq", "c_wk": "L1_xattn_Wk", "c_bk": "L1_xattn_bk",
    "c_wv": "L1_xattn_Wv", "c_bv": "L1_xattn_bv",
    "experts": "L1_ffn_expert_weights", "hyper": "L1_ffn_hyperplanes",
}


def kernel(**inputs):
    import numpy as _np
    import concourse.bacc as _bacc
    from concourse import mybir as _mybir
    from concourse.bass_utils import run_bass_kernel_spmd as _run

    nc = _bacc.Bacc("TRN2", target_bir_lowering=False, num_devices=1)
    arrays = {key: _np.ascontiguousarray(inputs[name]) for key, name in _INS.items()}
    arrays["cos"], arrays["sin"] = rope_tables()
    arrays = {f"in_{key}": a for key, a in arrays.items()}
    d = {key[3:]: nc.dram_tensor(key, a.shape, _mybir.dt.from_np(a.dtype), kind="ExternalInput").ap()
         for key, a in arrays.items()}
    d["out"] = nc.dram_tensor("out_y", (B, S, D), _mybir.dt.float32, kind="ExternalOutput").ap()
    decoder_kernel(nc, d)
    r = _run(nc, [arrays], core_ids=[0])
    return r.results[0]["out_y"]
```
